# Optimizing a Trainium2 kernel written in Bass

```python
import numpy as np
import jax
import jax.numpy as jnp

def _softmax(x, axis=-1):
    return jax.nn.softmax(x, axis=axis)

def _gelu(x):
    return jax.nn.gelu(x, approximate=True)

def _silu(x):
    return jax.nn.silu(x)

def _sigmoid(x):
    return jax.nn.sigmoid(x)

def _layernorm(x, axis=-1, eps=1e-05):
    m = jnp.mean(x, axis=axis, keepdims=True)
    v = jnp.var(x, axis=axis, keepdims=True)
    return (x - m) / jnp.sqrt(v + eps)

def _scatter_add(tgt, idx, src, axis=0):
    return tgt.at[idx].add(src)

def _segment_sum(src, seg, n):
    return jax.ops.segment_sum(src, seg, n)
kernel_name = 'mk_seq_postln_d2_jaxref_r8_9afc93'

def setup_inputs(seed: int=0):
    np.random.seed(seed)
    _w = jnp.asarray

    def _L0_attn_setup():
        import jax, jax.numpy as jnp
        import numpy as np
        NUM_HEADS = 16
        HIDDEN = 256
        HEAD_DIM = HIDDEN // NUM_HEADS
        ROTARY_DIM = HEAD_DIM // 4
        ROPE_BASE = 10000.0

        def _rope_angles(seq_len, dtype=jnp.float32):
            inv_freq = 1.0 / ROPE_BASE ** (jnp.arange(0, ROTARY_DIM, 2, dtype=dtype) / ROTARY_DIM)
            t = jnp.arange(seq_len, dtype=dtype)
            freqs = jnp.einsum('s,d->sd', t, inv_freq)
            emb = jnp.concatenate([freqs, freqs], axis=-1)
            return (jnp.cos(emb), jnp.sin(emb))

        def _rotate_half(x):
            x1, x2 = jnp.split(x, 2, axis=-1)
            return jnp.concatenate([-x2, x1], axis=-1)
        key = jax.random.key(seed)
        k1, k2, k3 = jax.random.split(key, 3)
        B, S = (2, 256)
        scale_qkv = 1.0 / np.sqrt(HIDDEN)
        return {'hidden_states': jax.random.normal(k1, (B, S, HIDDEN), dtype=jnp.float32), 'w_qkv': jax.random.normal(k2, (HIDDEN, 3 * HIDDEN), dtype=jnp.float32) * scale_qkv, 'b_qkv': jnp.zeros((3 * HIDDEN,), dtype=jnp.float32), 'w_out': jax.random.normal(k3, (HIDDEN, HIDDEN), dtype=jnp.float32) * scale_qkv, 'b_out': jnp.zeros((HIDDEN,), dtype=jnp.float32)}
    _L0_attn_in = _L0_attn_setup()

    def _L0_ffn_setup():
        import jax, jax.numpy as jnp
        import numpy as np
        import math
        B, S, D = (2, 256, 256)
        P = 4
        PW = 2
        L = 2
        STD = 0.02
        EPS = 1e-05

        def _layer_norm(x, g, b):
            m = jnp.mean(x, axis=-1, keepdims=True)
            v = jnp.mean(jnp.square(x - m), axis=-1, keepdims=True)
            return (x - m) * jax.lax.rsqrt(v + EPS) * g + b
        key = jax.random.key(seed)
        ks = jax.random.split(key, 16)
        n = lambda k, shape: jax.random.normal(k, shape, dtype=jnp.float32) * STD
        inp = {'x': jax.random.normal(ks[0], (B, S, D), dtype=jnp.float32), 'amp_w': n(ks[1], (D, D)), 'amp_b': jnp.zeros((D,), jnp.float32), 'ph_w': n(ks[2], (D, D)), 'ph_b': jnp.zeros((D,), jnp.float32), 'ent_w': n(ks[3], (L, D, P * D)), 'ent_b': jnp.zeros((L, P * D), jnp.float32), 'ent_pw': n(ks[4], (L, P * D, D)), 'ent_pb': jnp.zeros((L, D), jnp.float32), 'path_w': n(ks[5], (L, PW, D, D)), 'path_b': jnp.zeros((L, PW, D), jnp.float32), 'phase': jax.random.normal(ks[6], (L, PW, D), dtype=jnp.float32), 'ln3_g': jnp.ones((L, D), jnp.float32), 'ln3_b': jnp.zeros((L, D), jnp.float32), 'ln4_g': jnp.ones((L, D), jnp.float32), 'ln4_b': jnp.zeros((L, D), jnp.float32)}
        return inp
    _L0_ffn_in = _L0_ffn_setup()

    def _L1_attn_setup():
        import jax, jax.numpy as jnp
        import numpy as np
        B, T, C, H = (4, 512, 256, 16)
        Dh = C // H

        def _feature_map(x):
            return jax.nn.elu(x) + 1.0
        key = jax.random.key(seed)
        ks = jax.random.split(key, 7)
        s = 0.02
        return {'x': jax.random.normal(ks[0], (B, T, C), dtype=jnp.float32), 'cos': jax.random.uniform(ks[1], (T, Dh), dtype=jnp.float32), 'sin': jax.random.uniform(ks[2], (T, Dh), dtype=jnp.float32), 'Wq': jax.random.normal(ks[3], (C, C), dtype=jnp.float32) * s, 'Wk': jax.random.normal(ks[4], (C, C), dtype=jnp.float32) * s, 'Wv': jax.random.normal(ks[5], (C, C), dtype=jnp.float32) * s, 'Wo': jax.random.normal(ks[6], (C, C), dtype=jnp.float32) * s}
    _L1_attn_in = _L1_attn_setup()

    def _L1_ffn_setup():
        import jax, jax.numpy as jnp
        import numpy as np
        N_BLOCKS = 6
        DIM = 256
        HIDDEN = 4 * DIM
        LN_EPS = 1e-05
        W_SCALE = 0.02

        def _block(x, w1, b1, w2, b2):
            h = jax.nn.gelu(jnp.einsum('bsd,hd->bsh', x, w1) + b1, approximate=False)
            return jnp.einsum('bsh,dh->bsd', h, w2) + b2 + x

        def _layernorm(x, g, b):
            mu = jnp.mean(x, axis=-1, keepdims=True)
            var = jnp.mean(jnp.square(x - mu), axis=-1, keepdims=True)
            return (x - mu) * jax.lax.rsqrt(var + LN_EPS) * g + b
        key = jax.random.key(seed)
        ks = jax.random.split(key, 4)
        x = jax.random.normal(ks[0], (4, 256, DIM), dtype=jnp.float32)
        W1 = jax.random.normal(ks[1], (N_BLOCKS, HIDDEN, DIM), dtype=jnp.float32) * W_SCALE
        B1 = jnp.zeros((N_BLOCKS, HIDDEN), dtype=jnp.float32)
        W2 = jax.random.normal(ks[2], (N_BLOCKS, DIM, HIDDEN), dtype=jnp.float32) * W_SCALE
        B2 = jnp.zeros((N_BLOCKS, DIM), dtype=jnp.float32)
        LN_G = jnp.ones((N_BLOCKS - 1, DIM), dtype=jnp.float32)
        LN_B = jnp.zeros((N_BLOCKS - 1, DIM), dtype=jnp.float32)
        return {'x': x, 'W1': W1, 'B1': B1, 'W2': W2, 'B2': B2, 'LN_G': LN_G, 'LN_B': LN_B}
    _L1_ffn_in = _L1_ffn_setup()
    _d = {'L0_attn_hidden_states': _L0_attn_in['hidden_states'], 'L0_attn_w_qkv': _L0_attn_in['w_qkv'], 'L0_attn_b_qkv': _L0_attn_in['b_qkv'], 'L0_attn_w_out': _L0_attn_in['w_out'], 'L0_attn_b_out': _L0_attn_in['b_out'], 'L0_ffn_amp_w': _L0_ffn_in['amp_w'], 'L0_ffn_amp_b': _L0_ffn_in['amp_b'], 'L0_ffn_ph_w': _L0_ffn_in['ph_w'], 'L0_ffn_ph_b': _L0_ffn_in['ph_b'], 'L0_ffn_ent_w': _L0_ffn_in['ent_w'], 'L0_ffn_ent_b': _L0_ffn_in['ent_b'], 'L0_ffn_ent_pw': _L0_ffn_in['ent_pw'], 'L0_ffn_ent_pb': _L0_ffn_in['ent_pb'], 'L0_ffn_path_w': _L0_ffn_in['path_w'], 'L0_ffn_path_b': _L0_ffn_in['path_b'], 'L0_ffn_phase': _L0_ffn_in['phase'], 'L0_ffn_ln3_g': _L0_ffn_in['ln3_g'], 'L0_ffn_ln3_b': _L0_ffn_in['ln3_b'], 'L0_ffn_ln4_g': _L0_ffn_in['ln4_g'], 'L0_ffn_ln4_b': _L0_ffn_in['ln4_b'], 'L1_attn_cos': _L1_attn_in['cos'], 'L1_attn_sin': _L1_attn_in['sin'], 'L1_attn_Wq': _L1_attn_in['Wq'], 'L1_attn_Wk': _L1_attn_in['Wk'], 'L1_attn_Wv': _L1_attn_in['Wv'], 'L1_attn_Wo': _L1_attn_in['Wo'], 'L1_ffn_W1': _L1_ffn_in['W1'], 'L1_ffn_B1': _L1_ffn_in['B1'], 'L1_ffn_W2': _L1_ffn_in['W2'], 'L1_ffn_B2': _L1_ffn_in['B2'], 'L1_ffn_LN_G': _L1_ffn_in['LN_G'], 'L1_ffn_LN_B': _L1_ffn_in['LN_B']}
    _x0 = _d['L0_attn_hidden_states']
    _d['L0_attn_hidden_states'] = jax.random.normal(jax.random.fold_in(jax.random.key(seed), 1), (4, 512, 256), dtype=_x0.dtype)
    del _x0
    return _d

def reference(L0_attn_hidden_states, L0_attn_w_qkv, L0_attn_b_qkv, L0_attn_w_out, L0_attn_b_out, L0_ffn_amp_w, L0_ffn_amp_b, L0_ffn_ph_w, L0_ffn_ph_b, L0_ffn_ent_w, L0_ffn_ent_b, L0_ffn_ent_pw, L0_ffn_ent_pb, L0_ffn_path_w, L0_ffn_path_b, L0_ffn_phase, L0_ffn_ln3_g, L0_ffn_ln3_b, L0_ffn_ln4_g, L0_ffn_ln4_b, L1_attn_cos, L1_attn_sin, L1_attn_Wq, L1_attn_Wk, L1_attn_Wv, L1_attn_Wo, L1_ffn_W1, L1_ffn_B1, L1_ffn_W2, L1_ffn_B2, L1_ffn_LN_G, L1_ffn_LN_B):

    def _L0_attn_ref(hidden_states, w_qkv, b_qkv, w_out, b_out):
        import jax, jax.numpy as jnp
        import numpy as np
        NUM_HEADS = 16
        HIDDEN = 256
        HEAD_DIM = HIDDEN // NUM_HEADS
        ROTARY_DIM = HEAD_DIM // 4
        ROPE_BASE = 10000.0

        def _rope_angles(seq_len, dtype=jnp.float32):
            inv_freq = 1.0 / ROPE_BASE ** (jnp.arange(0, ROTARY_DIM, 2, dtype=dtype) / ROTARY_DIM)
            t = jnp.arange(seq_len, dtype=dtype)
            freqs = jnp.einsum('s,d->sd', t, inv_freq)
            emb = jnp.concatenate([freqs, freqs], axis=-1)
            return (jnp.cos(emb), jnp.sin(emb))

        def _rotate_half(x):
            x1, x2 = jnp.split(x, 2, axis=-1)
            return jnp.concatenate([-x2, x1], axis=-1)
        B, S, H = hidden_states.shape
        qkv = jnp.einsum('bsh,hf->bsf', hidden_states, w_qkv) + b_qkv
        qkv = qkv.reshape(B, S, NUM_HEADS, 3 * HEAD_DIM)
        q = jnp.transpose(qkv[..., :HEAD_DIM], (0, 2, 1, 3))
        k = jnp.transpose(qkv[..., HEAD_DIM:2 * HEAD_DIM], (0, 2, 1, 3))
        v = jnp.transpose(qkv[..., 2 * HEAD_DIM:], (0, 2, 1, 3))
        cos, sin = _rope_angles(S, q.dtype)
        q_rot, q_pass = (q[..., :ROTARY_DIM], q[..., ROTARY_DIM:])
        k_rot, k_pass = (k[..., :ROTARY_DIM], k[..., ROTARY_DIM:])
        q_rot = q_rot * cos + _rotate_half(q_rot) * sin
        k_rot = k_rot * cos + _rotate_half(k_rot) * sin
        q = jnp.concatenate([q_rot, q_pass], axis=-1)
        k = jnp.concatenate([k_rot, k_pass], axis=-1)
        scores = jnp.einsum('bhqd,bhkd->bhqk', q, k)
        causal = jnp.tril(jnp.ones((S, S), dtype=bool))
        scores = jnp.where(causal, scores, jnp.float32(-jnp.inf).astype(scores.dtype))
        probs = jax.nn.softmax(scores, axis=-1)
        attn = jnp.einsum('bhqk,bhkd->bhqd', probs, v)
        attn = jnp.transpose(attn, (0, 2, 1, 3)).reshape(B, S, H)
        return jnp.einsum('bsh,hf->bsf', attn, w_out) + b_out

    def _L0_ffn_ref(x, amp_w, amp_b, ph_w, ph_b, ent_w, ent_b, ent_pw, ent_pb, path_w, path_b, phase, ln3_g, ln3_b, ln4_g, ln4_b):
        import jax, jax.numpy as jnp
        import numpy as np
        import math
        B, S, D = (2, 256, 256)
        P = 4
        PW = 2
        L = 2
        STD = 0.02
        EPS = 1e-05

        def _layer_norm(x, g, b):
            m = jnp.mean(x, axis=-1, keepdims=True)
            v = jnp.mean(jnp.square(x - m), axis=-1, keepdims=True)
            return (x - m) * jax.lax.rsqrt(v + EPS) * g + b
        amp = jax.nn.sigmoid(x @ amp_w + amp_b)
        ph = jnp.tanh(x @ ph_w + ph_b) * math.pi
        h = (jnp.cos(ph) + jnp.sin(ph)) * amp
        for l in range(L):
            e = h @ ent_w[l] + ent_b[l]
            ent = e @ ent_pw[l] + ent_pb[l]
            h = _layer_norm(h + ent, ln3_g[l], ln3_b[l])
            t = jnp.einsum('bsd,pdf->pbsf', h, path_w[l]) + path_b[l][:, None, None, :]
            mod = jnp.cos(phase[l]) + jnp.sin(phase[l])
            interf = jnp.sum(t * mod[:, None, None, :], axis=0)
            h = _layer_norm(h + interf, ln4_g[l], ln4_b[l])
        return h

    def _L1_attn_ref(x, cos, sin, Wq, Wk, Wv, Wo):
        import jax, jax.numpy as jnp
        import numpy as np
        B, T, C, H = (4, 512, 256, 16)
        Dh = C // H

        def _feature_map(x):
            return jax.nn.elu(x) + 1.0
        b, t, c = x.shape
        h, dh = (H, c // H)

        def proj(W):
            y = jnp.einsum('btc,oc->bto', x, W)
            return y.reshape(b, t, h, dh).transpose(0, 2, 1, 3)
        q = _feature_map(proj(Wq))
        k = _feature_map(proj(Wk))
        v = proj(Wv)
        kv = jnp.einsum('bhtd,bhte->bhde', k, v)
        z = 1.0 / (jnp.einsum('bhtd,bhd->bht', q, k.sum(axis=2)) + 1e-06)
        out = jnp.einsum('bhtd,bhde,bht->bhte', q, kv, z)
        out = out.transpose(0, 2, 1, 3).reshape(b, t, c)
        return jnp.einsum('btc,oc->bto', out, Wo)

    def _L1_ffn_ref(x, W1, B1, W2, B2, LN_G, LN_B):
        import jax, jax.numpy as jnp
        import numpy as np
        N_BLOCKS = 6
        DIM = 256
        HIDDEN = 4 * DIM
        LN_EPS = 1e-05
        W_SCALE = 0.02

        def _block(x, w1, b1, w2, b2):
            h = jax.nn.gelu(jnp.einsum('bsd,hd->bsh', x, w1) + b1, approximate=False)
            return jnp.einsum('bsh,dh->bsd', h, w2) + b2 + x

        def _layernorm(x, g, b):
            mu = jnp.mean(x, axis=-1, keepdims=True)
            var = jnp.mean(jnp.square(x - mu), axis=-1, keepdims=True)
            return (x - mu) * jax.lax.rsqrt(var + LN_EPS) * g + b
        for i in range(N_BLOCKS):
            x = _block(x, W1[i], B1[i], W2[i], B2[i])
            if i < N_BLOCKS - 1:
                x = _layernorm(x, LN_G[i], LN_B[i])
        return x
    x = L0_attn_hidden_states
    x = _layernorm(x + _L0_attn_ref(x, L0_attn_w_qkv, L0_attn_b_qkv, L0_attn_w_out, L0_attn_b_out), axis=-1)
    x = _layernorm(x + _L0_ffn_ref(x, L0_ffn_amp_w, L0_ffn_amp_b, L0_ffn_ph_w, L0_ffn_ph_b, L0_ffn_ent_w, L0_ffn_ent_b, L0_ffn_ent_pw, L0_ffn_ent_pb, L0_ffn_path_w, L0_ffn_path_b, L0_ffn_phase, L0_ffn_ln3_g, L0_ffn_ln3_b, L0_ffn_ln4_g, L0_ffn_ln4_b), axis=-1)
    x = _layernorm(x + _L1_attn_ref(x, L1_attn_cos, L1_attn_sin, L1_attn_Wq, L1_attn_Wk, L1_attn_Wv, L1_attn_Wo), axis=-1)
    x = _layernorm(x + _L1_ffn_ref(x, L1_ffn_W1, L1_ffn_B1, L1_ffn_W2, L1_ffn_B2, L1_ffn_LN_G, L1_ffn_LN_B), axis=-1)
    return x

_drawn_inputs = setup_inputs


def setup_inputs(seed=0):
    import zlib

    import numpy as np

    out = dict(_drawn_inputs(seed))
    spreads = {'L0_attn_b_qkv': (0.0, 0.1),
     'L0_attn_b_out': (0.0, 0.1),
     'L0_ffn_amp_b': (0.0, 0.1),
     'L0_ffn_ph_b': (0.0, 0.1),
     'L0_ffn_ent_b': (0.0, 0.1),
     'L0_ffn_ent_pb': (0.0, 0.1),
     'L0_ffn_path_b': (0.0, 0.1),
     'L0_ffn_ln3_g': (1.0, 0.2),
     'L0_ffn_ln3_b': (0.0, 0.1),
     'L0_ffn_ln4_g': (1.0, 0.2),
     'L0_ffn_ln4_b': (0.0, 0.1),
     'L1_ffn_B1': (0.0, 0.1),
     'L1_ffn_B2': (0.0, 0.1),
     'L1_ffn_LN_G': (1.0, 0.2),
     'L1_ffn_LN_B': (0.0, 0.1)}
    factors = {}
    for name, (base, spread) in spreads.items():
        noise = np.random.default_rng([zlib.crc32(name.encode()), seed]).standard_normal(out[name].shape)
        drawn = base * np.exp(spread * noise) if base else spread * noise
        out[name] = jnp.asarray(drawn.astype(out[name].dtype))
    for name, factor in factors.items():
        out[name] = (out[name] * factor).astype(out[name].dtype)
    return out
```

```python
from contextlib import ExitStack

import numpy as np

import concourse.bass as bass
from concourse import mybir

ALU = mybir.AluOpType
ACT = mybir.ActivationFunctionType
AX = mybir.AxisListType
F32 = mybir.dt.float32
F32R = mybir.dt.float32r
I32 = mybir.dt.int32
BF16 = mybir.dt.bfloat16

P = 128
B, S, D = 4, 512, 256
RT = S // P
KC = D // P
NT = B * RT
H, DH = 16, 16
PAIRS = H // 2
SLOT = 64
STAGES = 4
M0 = 1024
MC0 = M0 // P
BLOCKS = 6
HID = 1024
FC = HID // P
EPS = 1e-5
MASKED = -1e30
RSQRT_MAGIC = 0x5F3759DF
ROUND_MAGIC = 1.5 * 2.0 ** 23
TWO_PI = (6.28125, float(np.float32(2 * np.pi - 6.28125)),
          float(2 * np.pi - 6.28125 - np.float64(np.float32(2 * np.pi - 6.28125))))
PI_F32 = float(np.float32(np.pi))


BIAS_COLS = 4 + 2 * MC0 + BLOCKS * FC
STAGE_ORDER = (1, 3, 0, 2)


class Chain:

    def __init__(self, eng, sem):
        self.eng, self.sem, self.base, self.n = eng, sem, 0, 0

    def step(self, instruction):
        instruction.then_inc(self.sem, 1)
        self.n += 1

    def settle(self):
        self.eng.wait_ge(self.sem, self.base + self.n)

    def enter(self, i, per):
        self.outer, self.per = self.base + self.n, per
        self.base, self.n = self.outer + i * per, 0

    def leave(self, times):
        assert self.n == self.per, (self.n, self.per)
        self.base, self.n = self.outer + times * self.per, 0


def bcast(ap, axis, shape):
    return ap.unsqueeze(axis).broadcast_to(shape)


def layernorm(v, chain, w, r, xn, done):
    stats, mv, var, y, t = w["stats"], w["mv"], w["var"], w["y"], w["t"]
    for k in range(RT):
        ins = v.bn_stats(stats[:, k, :], r[:, k, :])
    chain.step(ins)
    chain.settle()
    v.sem_inc(w["carrier"], 1)
    for k in range(RT):
        ins = v.bn_aggr(mv[:, k, :], stats[:, k, :])
    chain.step(ins)
    chain.settle()
    chain.step(v.tensor_scalar(var[:, :], mv[:, :, 1], EPS, None, ALU.add))
    chain.settle()
    chain.step(v.tensor_scalar(t[:, :].bitcast(I32), var[:, :].bitcast(I32), 1, None,
                               ALU.arith_shift_right))
    chain.settle()
    chain.step(v.tensor_scalar(y[:, :].bitcast(I32), t[:, :].bitcast(I32), -1.0,
                               float(RSQRT_MAGIC), ALU.mult, ALU.add))
    chain.settle()
    for _ in range(3):
        chain.step(v.tensor_tensor(t[:, :], y[:, :], y[:, :], ALU.mult))
        chain.settle()
        chain.step(v.scalar_tensor_tensor(t[:, :], t[:, :], -0.5, var[:, :], ALU.mult, ALU.mult))
        chain.settle()
        chain.step(v.scalar_tensor_tensor(y[:, :], t[:, :], 1.5, y[:, :], ALU.add, ALU.mult))
        chain.settle()
    for k in range(RT):
        ins = v.tensor_scalar(xn[:, k, :], r[:, k, :], mv[:, k, 0:1], y[:, k:k + 1],
                              ALU.subtract, ALU.mult)
    ins.then_inc(done, 1)


class Shared:
    pass


def sb(stack, nc, name, shape, dt=F32):
    return stack.enter_context(nc.sbuf_tensor(name, shape, dt))


def sems(stack, nc, names):
    return {n: stack.enter_context(nc.semaphore(n)) for n in names.split()}


def build(nc, A, out):
    g = Shared()
    top = ExitStack()
    with top:
        g.ps = top.enter_context(nc.psum_tensor("ps", [P, 8, 512], F32))
        g.ident = sb(top, nc, "ident", [P, P])
        g.ident_r = sb(top, nc, "ident_r", [P, P], F32R)
        g.xT_h = sb(top, nc, "xT_h", [P, B, KC, S], F32R)
        g.xT_l = sb(top, nc, "xT_l", [P, B, KC, S], F32R)
        g.lnw = {"stats": sb(top, nc, "ln_stats", [P, RT, 6]), "mv": sb(top, nc, "ln_mv", [P, RT, 2]),
                 "var": sb(top, nc, "ln_var", [P, RT]), "y": sb(top, nc, "ln_y", [P, RT]),
                 "t": sb(top, nc, "ln_t", [P, RT])}
        g.carrier = sems(top, nc, "v_carrier a_carrier g_carrier")
        g.lnw["carrier"] = g.carrier["v_carrier"]
        g.xn = sb(top, nc, "xn", [P, 2, RT, D])
        g.hs = sb(top, nc, "hs", [P, 2, RT, D])
        g.rsum = sb(top, nc, "rsum", [P, RT, D])
        g.x_a = sb(top, nc, "x_a", [P, NT, D])
        g.bias_col = sb(top, nc, "bias_col", [P, BIAS_COLS])
        attention0(nc, A, g)
        g.w1_raw = sb(top, nc, "w1_raw", [P, FC, D])
        g.w2_raw = sb(top, nc, "w2_raw", [P, KC, HID])
        g.pre = sems(top, nc, "w1_in w2_in rows_in")
        g.mlp_g = sb(top, nc, "mlp_g", [P, BLOCKS - 1, D])
        g.mlp_b = sb(top, nc, "mlp_b", [P, BLOCKS - 1, D])
        g.mlp_b2 = sb(top, nc, "mlp_b2", [P, BLOCKS, D])
        g.x3_dram = nc.dram_tensor("x3_kept", (B, S, D), F32, kind="Internal").ap()
        with ExitStack() as wl1:
            g.x_b = sb(wl1, nc, "x_b", [P, NT, D])
            g.wq_h = sb(wl1, nc, "wq_h", [P, KC, D], F32R)
            g.wq_l = sb(wl1, nc, "wq_l", [P, KC, D], F32R)
            g.wkv_h = sb(wl1, nc, "wkv_h", [P, KC, 2 * D], F32R)
            g.wkv_l = sb(wl1, nc, "wkv_l", [P, KC, 2 * D], F32R)
            g.wo_h = sb(wl1, nc, "wo_h", [P, KC, D], F32R)
            g.wo_l = sb(wl1, nc, "wo_l", [P, KC, D], F32R)
            with ExitStack() as stage:
                g.stage_w_h = sb(stage, nc, "stage_w_h", [P, STAGES, KC, D], F32R)
                g.stage_w_l = sb(stage, nc, "stage_w_l", [P, STAGES, KC, D], F32R)
                g.stage_c = sb(stage, nc, "stage_c", [P, STAGES, D])
                g.stage_g = sb(stage, nc, "stage_g", [P, STAGES, D])
                g.stage_b = sb(stage, nc, "stage_b", [P, STAGES, D])
                g.gate_h = sb(stage, nc, "gate_h", [P, KC, 2 * D], F32R)
                g.gate_l = sb(stage, nc, "gate_l", [P, KC, 2 * D], F32R)
                prep(nc, A, g)
                gates(nc, A, g)
                stages(nc, A, g)
            attention1(nc, A, g)
        ffn1(nc, A, g, out)


def prep(nc, A, g):
    ps, ident, pre = g.ps, g.ident, g.pre
    stack = ExitStack()
    with stack:
        s = sems(stack, nc, "small_in gate_in l1_in0 l1_in1 l1_in2 l1_in3 ent_in pw_in path_in "
                        "p_bias p_wt p_ent p_prod v_bias v_chain v_m a_split a_ent a_trig "
                        "v_wt v_trig v_prod  a_h v_l")
        raw_gate = sb(stack, nc, "raw_gate", [P, KC, 2 * D])
        raw_l1 = g.hs[:, :, :, :].rearrange("p a (n c) d -> p (a n) c d", c=KC)
        raw_ent = g.xn[:, :, :, :].rearrange("p a b c -> p (a b c)").rearrange("p (c n) -> p c n", c=KC)
        raw_pw = g.w1_raw
        raw_path = sb(stack, nc, "raw_path", [P, 4, KC, D])
        ent_t = g.w2_raw[:, :, :].rearrange("p c n -> p (c n)").rearrange("p (m d) -> p m d", d=D)
        bias_rows = sb(stack, nc, "bias_rows", [4 + 16 + BLOCKS * FC, P])
        phase, turn, sin_half, sin_full = (
            g.x_b[:, 4 * n:4 * n + 4, :].rearrange("p a d -> p (a d)") for n in range(4))
        path_b = sb(stack, nc, "path_b", [P, 4, D])
        ent_pb = sb(stack, nc, "ent_pb", [P, 2, D])
        prod = sb(stack, nc, "prod", [P, KC, D])
        prod2 = sb(stack, nc, "prod2", [P, KC, D])
        rows = bias_rows.shape[0]
        block = stack.enter_context(nc.Block())

        @block.sync
        def _(sp):
            for name, at, n in (("L0_ffn_amp_b", 0, 2), ("L0_ffn_ph_b", 2, 2)):
                sp.dma_start(bias_rows[at:at + n, :],
                             A[name].rearrange("(c p) -> c p", p=P)).then_inc(s["small_in"], 16)
            sp.dma_start(bias_rows[4:20, :],
                         A["L0_ffn_ent_b"].rearrange("l (c p) -> (l c) p", p=P)).then_inc(s["small_in"], 16)
            sp.dma_start(bias_rows[20:rows, :],
                         A["L1_ffn_B1"].rearrange("l (c p) -> (l c) p", p=P)).then_inc(s["small_in"], 16)
            for n, name in enumerate(("L1_attn_Wq", "L1_attn_Wk", "L1_attn_Wv", "L1_attn_Wo")):
                sp.dma_start(raw_l1[:, n, :, :],
                             A[name].rearrange("(c p) n -> p c n", p=P)).then_inc(s[f"l1_in{n}"], 16)
            sp.dma_start(raw_ent[:, :, :],
                         A["L0_ffn_ent_w"][0].rearrange("(c p) n -> p c n", p=P)).then_inc(s["ent_in"], 16)
            sp.dma_start(raw_pw[:, :, :],
                         A["L0_ffn_ent_pw"][0].rearrange("(c p) n -> p c n", p=P)).then_inc(s["pw_in"], 16)
            sp.wait_ge(s["p_ent"], 4)
            sp.dma_start(raw_ent[:, :, :],
                         A["L0_ffn_ent_w"][1].rearrange("(c p) n -> p c n", p=P)).then_inc(s["ent_in"], 16)
            sp.wait_ge(s["p_prod"], 1)
            sp.dma_start(raw_pw[:, :, :],
                         A["L0_ffn_ent_pw"][1].rearrange("(c p) n -> p c n", p=P)).then_inc(s["pw_in"], 16)
            for tile, name in ((g.mlp_g, "L1_ffn_LN_G"), (g.mlp_b, "L1_ffn_LN_B"), (g.mlp_b2, "L1_ffn_B2")):
                sp.dma_start(tile[:, :, :], A[name].unsqueeze(0).broadcast_to([P, *A[name].shape])
                             ).then_inc(pre["rows_in"], 16)
            for n, name in enumerate(("ln3", "ln4")):
                for l in range(2):
                    for which in ("g", "b"):
                        sp.dma_start((g.stage_g if which == "g" else g.stage_b)[:, 2 * l + n, :],
                                     A[f"L0_ffn_{name}_{which}"][l:l + 1, :].broadcast_to([P, D])
                                     ).then_inc(pre["rows_in"], 16)

        @block.scalar
        def _(act):
            act.dma_start(phase, A["L0_ffn_phase"].rearrange("l w d -> (l w d)").unsqueeze(0)
                          .broadcast_to([P, 4 * D])).then_inc(s["path_in"], 16)
            act.dma_start(raw_gate[:, :, 0:D],
                          A["L0_ffn_amp_w"].rearrange("(c p) n -> p c n", p=P)).then_inc(s["gate_in"], 16)
            act.dma_start(raw_gate[:, :, D:2 * D],
                          A["L0_ffn_ph_w"].rearrange("(c p) n -> p c n", p=P)).then_inc(s["gate_in"], 16)
            for n in range(4):
                act.dma_start(raw_path[:, n, :, :], A["L0_ffn_path_w"][n // 2, n % 2]
                              .rearrange("(c p) n -> p c n", p=P)).then_inc(s["path_in"], 16)
            act.dma_start(path_b[:, :, :], A["L0_ffn_path_b"].rearrange("l w d -> (l w) d").unsqueeze(0)
                          .broadcast_to([P, 4, D])).then_inc(s["path_in"], 16)
            act.dma_start(ent_pb[:, :, :], A["L0_ffn_ent_pb"].unsqueeze(0)
                          .broadcast_to([P, 2, D])).then_inc(s["path_in"], 16)
            act.wait_ge(s["gate_in"], 32)
            act.activation(g.gate_h[:, :, :], raw_gate[:, :, :], ACT.Copy).then_inc(s["a_h"], 1)
            for n, (t, lo) in enumerate(((g.wq_h, 0), (g.wkv_h, 0), (g.wkv_h, D), (g.wo_h, 0))):
                act.wait_ge(s["p_wt"], n + 1)
                act.activation(t[:, :, lo:lo + D], ps[:, n, :].rearrange("p (c n) -> p c n", c=KC),
                               ACT.Copy).then_inc(s["a_h"], 1)
            for l in range(2):
                if l:
                    act.wait_ge(s["p_prod"], l)
                for n in range(4):
                    act.wait_ge(s["p_ent"], 4 * l + n + 1)
                    act.activation(ent_t[:, 2 * n:2 * n + 2, :],
                                   ps[:, 4 * (1 - l) + n, :].rearrange("p (c n) -> p c n", c=2),
                                   ACT.Copy).then_inc(s["a_ent"], 1)
            act.wait_ge(s["v_trig"], 1)
            act.activation(sin_half, turn, ACT.Sin, scale=0.5).then_inc(s["a_trig"], 1)
            act.activation(sin_full, turn, ACT.Sin).then_inc(s["a_trig"], 1)
            for n in range(STAGES):
                act.wait_ge(s["v_prod"], n + 1)
                act.activation(g.stage_w_h[:, STAGE_ORDER[n], :, :], (prod, prod2)[n % 2][:, :, :],
                               ACT.Copy).then_inc(s["a_split"], 1)

        @block.tensor
        def _(pe):
            pe.wait_ge(s["small_in"], 64)
            pe.transpose(ps[:, 4, 0:rows], bias_rows[:, :], ident[0:rows, 0:rows]).then_inc(s["p_bias"], 1)
            for n in range(4):
                pe.wait_ge(s[f"l1_in{n}"], 16)
                for c in range(KC):
                    for o in range(KC):
                        mm = pe.transpose(ps[:, n, c * D + o * P:c * D + (o + 1) * P],
                                          raw_l1[:, n, o, c * P:(c + 1) * P], ident[:, :])
                mm.then_inc(s["p_wt"], 1)
            for l in range(2):
                pe.wait_ge(s["ent_in"], 16 * (l + 1))
                if l:
                    pe.wait_ge(s["v_wt"], 4)
                else:
                    pe.wait_ge(s["v_bias"], 1)
                for n in range(4):
                    for j in range(2):
                        for c in range(KC):
                            m = 2 * n + j
                            mm = pe.transpose(ps[:, 4 * (1 - l) + n, j * D + c * P:j * D + (c + 1) * P],
                                              raw_ent[:, c, m * P:(m + 1) * P], ident[:, :])
                    mm.then_inc(s["p_ent"], 1)
                pe.wait_ge(s["pw_in"], 16 * (l + 1))
                pe.wait_ge(s["a_ent"], 4 * (l + 1))
                for c in range(KC):
                    for m in range(MC0):
                        mm = pe.matmul(ps[:, 4 + 2 * l, c * D:(c + 1) * D], ent_t[:, m, c * P:(c + 1) * P],
                                       raw_pw[:, m, :], start=(m == 0), stop=(m == MC0 - 1))
                pe.wait_ge(s["v_bias"], 1)
                for m in range(MC0):
                    col = 4 + l * MC0 + m
                    mm2 = pe.matmul(ps[:, 5 + 2 * l, 0:D], g.bias_col[:, col:col + 1].broadcast_to([P, P]),
                                    raw_pw[:, m, :], start=(m == 0), stop=(m == MC0 - 1))
                mm2.then_inc(s["p_prod"], 1)

        @block.vector
        def _(v):
            chain = Chain(v, s["v_chain"])
            v.wait_ge(s["a_h"], 1)
            v.wait_ge(s["gate_in"], 32)
            v.tensor_tensor(g.gate_l[:, :, :], raw_gate[:, :, :], g.gate_h[:, :, :].bitcast(F32),
                            ALU.subtract).then_inc(s["v_l"], 1)
            v.wait_ge(s["p_bias"], 1)
            v.tensor_copy(g.bias_col[:, :], ps[:, 4, 0:rows]).then_inc(s["v_bias"], 1)
            for n, (low, high, lo) in enumerate(((g.wq_l, g.wq_h, 0), (g.wkv_l, g.wkv_h, 0),
                                                 (g.wkv_l, g.wkv_h, D), (g.wo_l, g.wo_h, 0))):
                v.wait_ge(s["a_h"], 1 + n + 1)
                v.tensor_tensor(low[:, :, lo:lo + D], ps[:, n, :].rearrange("p (c n) -> p c n", c=KC),
                                high[:, :, lo:lo + D].bitcast(F32), ALU.subtract).then_inc(s["v_wt"], 1)
            v.wait_ge(s["path_in"], 16 * 7)
            chain.step(v.tensor_scalar(sin_half, phase, float(1 / (2 * np.pi)), ROUND_MAGIC,
                                       ALU.mult, ALU.add))
            chain.settle()
            chain.step(v.tensor_scalar(sin_full, sin_half, ROUND_MAGIC, None, ALU.subtract))
            chain.settle()
            before = phase
            for c in TWO_PI:
                chain.step(v.scalar_tensor_tensor(turn, sin_full, -c, before,
                                                  ALU.mult, ALU.add))
                chain.settle()
                before = turn
            v.tensor_scalar(turn, turn, PI_F32, -PI_F32, ALU.min, ALU.max).then_inc(s["v_trig"], 1)
            v.wait_ge(s["a_trig"], 2)
            chain.step(v.tensor_tensor(turn, sin_half, sin_half, ALU.mult))
            chain.settle()
            chain.step(v.scalar_tensor_tensor(turn, turn, -2.0, sin_full, ALU.mult, ALU.add))
            chain.settle()
            chain.step(v.tensor_scalar(turn, turn, 1.0, None, ALU.add))
            chain.settle()
            mod = turn.rearrange("p (n d) -> p n d", n=4)
            chain.step(v.tensor_tensor(path_b[:, :, :], path_b[:, :, :], mod, ALU.mult))
            chain.settle()
            for n in range(STAGES):
                dst = (prod, prod2)[n % 2]
                st = STAGE_ORDER[n]
                if n >= 2:
                    v.wait_ge(s["a_split"], n - 1)
                if n < 2:
                    l = n
                    m = [bcast(mod[:, 2 * l + w, :], 1, [P, KC, D]) for w in range(2)]
                    chain.step(v.tensor_tensor(raw_path[:, 2 * l, :, :], raw_path[:, 2 * l, :, :], m[0], ALU.mult))
                    chain.step(v.tensor_tensor(raw_path[:, 2 * l + 1, :, :], raw_path[:, 2 * l + 1, :, :], m[1],
                                               ALU.mult))
                    chain.settle()
                    chain.step(v.tensor_tensor(dst[:, :, :], raw_path[:, 2 * l, :, :],
                                               raw_path[:, 2 * l + 1, :, :], ALU.add))
                    v.tensor_tensor(g.stage_c[:, st, :], path_b[:, 2 * l, :], path_b[:, 2 * l + 1, :], ALU.add)
                else:
                    l = n - 2
                    v.wait_ge(s["p_prod"], l + 1)
                    chain.step(v.tensor_copy(dst[:, :, :],
                                             ps[:, 4 + 2 * l, :].rearrange("p (c n) -> p c n", c=KC)))
                    v.tensor_tensor(g.stage_c[:, st, :], ps[:, 5 + 2 * l, 0:D], ent_pb[:, l, :], ALU.add)
                chain.settle()
                for c in range(KC):
                    ins = v.tensor_tensor(dst[:, c, c * P:(c + 1) * P], dst[:, c, c * P:(c + 1) * P],
                                          ident[:, :], ALU.add)
                    chain.step(ins)
                chain.settle()
                v.sem_inc(s["v_prod"], 1)
                v.wait_ge(s["a_split"], n + 1)
                chain.step(v.tensor_tensor(g.stage_w_l[:, st, :, :], dst[:, :, :],
                                           g.stage_w_h[:, st, :, :].bitcast(F32), ALU.subtract))
            chain.settle()


def attention0(nc, A, g):
    ps, ident, ident_r, xn = g.ps, g.ident, g.ident_r, g.xn
    x_in, x_res = g.hs[:, 0, :, :], g.hs[:, 1, :, :]
    GROUPS = H // 4
    LEAD = 3
    COLS = [S - P * i for i in range(RT)]
    OFF = [sum(COLS[:i]) for i in range(RT)]
    stack = ExitStack()
    with stack:
        s = sems(stack, nc, "const_in qkv_in out_in wsplit_h wsplit_l const_v mask_v "
                 "x_in xres_in x_free p_xT a_xh v_xl p_qkv v_qkv g_rope g_chain a_stack v_stack g_val "
                 "p_stackT a_qT v_kT p_max v_max v_neg p_negT v_negT m_row0 m_row1 p_score a_exp p_out a_out p_oT v_out "
                 "v_chain p_attT a_atth v_attl p_proj v_res v_norm g_x1 p_nT a_nh v_nl")
        wqkv_h = sb(stack, nc, "wqkv_h", [P, KC, 3 * D], F32R)
        wqkv_l = sb(stack, nc, "wqkv_l", [P, KC, 3 * D], F32R)
        wout_h = sb(stack, nc, "wout_h", [P, KC, D], F32R)
        wout_l = sb(stack, nc, "wout_l", [P, KC, D], F32R)
        ident_b = sb(stack, nc, "ident_b", [P, P], BF16)
        mask_b = sb(stack, nc, "mask_b", [P, P], BF16)
        q_mask = sb(stack, nc, "q_mask", [P, S])
        k_mask = sb(stack, nc, "k_mask", [P, P])
        rope = sb(stack, nc, "rope", [P, 2, RT, 4])
        b_qkv = sb(stack, nc, "b_qkv", [P, 3 * D])
        b_out = sb(stack, nc, "b_out", [P, D])
        att_h = sb(stack, nc, "att_h", [P, KC, S], F32R)
        att_l = sb(stack, nc, "att_l", [P, KC, S], F32R)
        qkv = sb(stack, nc, "qkv", [P, 2, 3 * D])
        turned = sb(stack, nc, "turned", [P, 2, 2 * H * 4])
        q_stack = sb(stack, nc, "q_stack", [P, H, SLOT], F32R)
        k_stack = sb(stack, nc, "k_stack", [P, H, SLOT], F32R)
        qT = sb(stack, nc, "qT", [P, PAIRS, S], F32R)
        kT = sb(stack, nc, "kT", [P, PAIRS, S], F32R)
        val = sb(stack, nc, "val", [P, RT, H, 2 * DH])
        out_T = sb(stack, nc, "out_T", [P, S])
        neg_max = sb(stack, nc, "neg_max", [P, P], F32R)
        top_score = sb(stack, nc, "top_score", [P, 2, 2 * RT])
        neg_rows = sb(stack, nc, "neg_rows", [2 * RT, 2, P], F32R)
        probs = sb(stack, nc, "probs", [P, 2, 2, sum(COLS)])
        inv = sb(stack, nc, "inv", [P, RT, 4])
        att = sb(stack, nc, "att", [P, RT, D])
        flat = probs[:, :, :, :].rearrange("p a b c -> p (a b c)")
        raw_qkv = flat[:, 0:KC * 3 * D].rearrange("p (c n) -> p c n", c=KC)
        raw_out = flat[:, KC * 3 * D:KC * 4 * D].rearrange("p (c n) -> p c n", c=KC)
        x_dram = A["L0_attn_hidden_states"].rearrange("b (t p) d -> p b t d", p=P)
        block = stack.enter_context(nc.Block())

        @block.sync
        def _(sp):
            sp.dma_start(ident[:, :], A["c_ident"]).then_inc(s["const_in"], 16)
            sp.dma_start(q_mask[:, :], A["c_qmask"]).then_inc(s["const_in"], 16)
            sp.dma_start(k_mask[:, :], A["c_kmask"]).then_inc(s["const_in"], 16)
            sp.dma_start(rope[:, :, :, :], A["c_rope"]).then_inc(s["const_in"], 16)
            sp.dma_start(b_qkv[:, :], A["L0_attn_b_qkv"].unsqueeze(0).broadcast_to([P, 3 * D])
                         ).then_inc(s["const_in"], 16)
            sp.dma_start(b_out[:, :], A["L0_attn_b_out"].unsqueeze(0).broadcast_to([P, D])
                         ).then_inc(s["const_in"], 16)
            with sp.Fori(0, B) as i:
                sp.wait_ge(s["x_free"], i + 1)
                sp.dma_start(x_in, x_dram[:, i, :, :]).then_inc(s["x_in"], 16)
                sp.dma_start(x_res, x_dram[:, i, :, :]).then_inc(s["xres_in"], 16)
                for p in range(PAIRS):
                    sp.wait_ge(s["v_negT"], i * PAIRS + p + 2)
                    for o in range(2):
                        row = o * SLOT + 3 * DH
                        sp.dma_start(qT[row:row + 1, p, :].bitcast(F32).rearrange("o (t c) -> o t c", t=RT),
                                     neg_rows[o * RT:(o + 1) * RT, p % 2, :].bitcast(F32)
                                     ).then_inc(s[f"m_row{p % 2}"], 16)

        @block.gpsimd
        def _(pool):
            pool.memset(val[:, :, :, DH:2 * DH], 1.0).then_inc(s["g_val"], 1)
            pool.wait_ge(s["const_in"], 96)
            chain = Chain(pool, s["g_chain"])
            with pool.Fori(0, B) as i:
                chain.enter(i, 4 * RT)
                for t in range(RT):
                    pool.wait_ge(s["v_qkv"], i * RT + t + 1)
                    heads = qkv[:, t % 2, :].rearrange("p (h c d) -> p h c d", h=H, c=3)
                    r = heads[:, :, 0:2, 0:4]
                    halves = [heads[:, :, 0:2, 0:2], heads[:, :, 0:2, 2:4]]
                    by_cos = turned[:, 0, :].rearrange("p (h c d) -> p h c d", h=H, c=2)
                    by_sin = turned[:, 1, :].rearrange("p (h c d) -> p h c d", h=H, c=2)

                    def table(w, lo, hi):
                        return rope[:, w, t, lo:hi].unsqueeze(1).unsqueeze(1).broadcast_to([P, H, 2, hi - lo])

                    chain.step(pool.tensor_tensor(by_cos, r, table(0, 0, 4), ALU.mult))
                    chain.step(pool.tensor_tensor(by_sin[:, :, :, 0:2], halves[1], table(1, 0, 2), ALU.mult))
                    chain.step(pool.tensor_tensor(by_sin[:, :, :, 2:4], halves[0], table(1, 2, 4), ALU.mult))
                    chain.settle()
                    chain.step(pool.tensor_tensor(r, by_cos, by_sin, ALU.add))
                    chain.settle()
                    if t == 0:
                        pool.wait_ge(s["v_out"], i * GROUPS + 1)
                    pool.sem_inc(g.carrier["g_carrier"], 1)
                    pool.tensor_copy(val[:, t, :, 0:DH], heads[:, :, 2, :]).then_inc(s["g_val"], 1)
                pool.wait_ge(s["v_norm"], i + 1)
                pool.sem_inc(g.carrier["g_carrier"], 1)
                pool.tensor_copy(g.x_a[:, bass.ts(i, RT), :], xn[:, 0, :, :]).then_inc(s["g_x1"], 1)

        @block.scalar
        def _(act):
            act.dma_start(raw_qkv, A["L0_attn_w_qkv"].rearrange("(c p) n -> p c n", p=P)
                          ).then_inc(s["qkv_in"], 16)
            act.dma_start(raw_out, A["L0_attn_w_out"].rearrange("(c p) n -> p c n", p=P)
                          ).then_inc(s["out_in"], 16)
            act.wait_ge(s["qkv_in"], 16)
            act.activation(wqkv_h[:, :, :], raw_qkv, ACT.Copy).then_inc(s["wsplit_h"], 1)
            act.wait_ge(s["out_in"], 16)
            act.activation(wout_h[:, :, :], raw_out, ACT.Copy).then_inc(s["wsplit_h"], 1)

            def copy_outputs(i, q):
                act.wait_ge(s["p_out"], i * PAIRS + 2 * q + 2)
                act.wait_ge(s["p_oT"], i * GROUPS + q + 1)
                act.activation(out_T[:, :], ps[:, 6, :], ACT.Copy).then_inc(s["a_out"], 1)

            with act.Fori(0, B) as i:
                for c in range(KC):
                    act.wait_ge(s["p_xT"], i * KC + c + 1)
                    act.activation(att_h[:, c, :], ps[:, c, :], ACT.Copy).then_inc(s["a_xh"], 1)
                for t in range(RT + 2):
                    if t < RT:
                        act.wait_ge(s["g_val"], i * RT + t + 2)
                        act.wait_ge(s["mask_v"], 1)
                        act.wait_ge(s["p_stackT"], 2 * (i * RT + t) + 1)
                        heads = qkv[:, t % 2, :].rearrange("p (h c d) -> p h c d", h=H, c=3)
                        act.activation(
                            q_stack[:, :, :].rearrange("p h (n d) -> p h n d", d=DH)[:, :, 0:3:2, :],
                            bcast(heads[:, :, 0, :], 2, [P, H, 2, DH]), ACT.Copy)
                        act.activation(
                            k_stack[:, :, :].rearrange("p h (n d) -> p h n d", d=DH)[:, :, 0:2, :],
                            bcast(heads[:, :, 1, :], 2, [P, H, 2, DH]), ACT.Copy).then_inc(s["a_stack"], 1)
                    if 0 < t <= RT:
                        u = t - 1
                        act.wait_ge(s["p_stackT"], 2 * (i * RT + u) + 3)
                        act.activation(qT[:, :, u * P:(u + 1) * P],
                                       ps[:, 6:8, :].rearrange("p a (b c) -> p (a b) c", c=P),
                                       ACT.Copy).then_inc(s["a_qT"], 1)
                for p in range(PAIRS):
                    for j in range(RT):
                        n = p * RT + j
                        act.wait_ge(s["p_score"], i * PAIRS * RT + n + 1)
                        if j == 0 and p >= 2:
                            act.wait_ge(s["p_out"], i * PAIRS + p - 1)
                        act.activation(probs[:, p % 2, :, OFF[j]:OFF[j] + COLS[j]],
                                       ps[:, 2 + 2 * (n % 2):4 + 2 * (n % 2), 0:COLS[j]],
                                       ACT.Exp).then_inc(s["a_exp"], 1)
                    if p >= 2 and p % 2 == 0:
                        copy_outputs(i, p // 2 - 1)
                copy_outputs(i, GROUPS - 1)
                for c in range(KC):
                    act.wait_ge(s["p_attT"], i * KC + c + 1)
                    act.activation(att_h[:, c, :], ps[:, c, :], ACT.Copy).then_inc(s["a_atth"], 1)
                for c in range(KC):
                    act.wait_ge(s["p_nT"], i * KC + c + 1)
                    act.sem_inc(g.carrier["a_carrier"], 1)
                    act.activation(g.xT_h[:, i, c, :], ps[:, 4 + c, :], ACT.Copy).then_inc(s["a_nh"], 1)

        @block.tensor
        def _(pe):
            pe.wait_ge(s["const_in"], 96)
            pe.wait_ge(s["wsplit_l"], 2)
            pe.wait_ge(s["const_v"], 1)

            def max_pass(i, p):
                for t in range(RT):
                    for o in range(2):
                        n = i * 2 * PAIRS * RT + (p * RT + t) * 2 + o
                        rows = slice(o * SLOT, (o + 1) * SLOT)
                        pe.wait_ge(s["v_max"], n + 1)
                        pe.matmul(ps[:, o, 0:(t + 1) * P], qT[rows, p, t * P:(t + 1) * P],
                                  kT[rows, p, 0:(t + 1) * P], start=True, stop=True).then_inc(s["p_max"], 1)
                    yield t

            def score_pass(i, p, j):
                n = p * RT + j
                bank = 2 + 2 * (n % 2)
                if j == 0:
                    pe.wait_ge(s[f"m_row{p % 2}"], 32 * (i * (PAIRS // 2) + p // 2 + 1))
                if n >= 2:
                    pe.wait_ge(s["a_exp"], i * PAIRS * RT + n - 1)
                for o in range(2):
                    rows = slice(o * SLOT, (o + 1) * SLOT)
                    pe.matmul(ps[:, bank + o, 0:COLS[j]], kT[rows, p, j * P:(j + 1) * P],
                              qT[rows, p, j * P:S], start=True, stop=False)
                for o in range(2):
                    mm = pe.matmul(ps[:, bank + o, 0:P], ident_b[:, :], mask_b[:, :], start=False, stop=True)
                mm.then_inc(s["p_score"], 1)

            def value_pass(i, p, j):
                if j == 0 and p % 2 == 0:
                    pe.wait_ge(s["a_out"], i * GROUPS + p // 2 + 1)
                pe.wait_ge(s["a_exp"], i * PAIRS * RT + p * RT + j + 1)
                for o in range(2):
                    rows = 2 * DH * (2 * (p % 2) + o)
                    mm = pe.matmul(ps[rows:rows + 2 * DH, 6, j * P:S], val[:, j, 2 * p + o, :],
                                   probs[:, p % 2, o, OFF[j]:OFF[j] + COLS[j]], start=(j == 0), stop=(j == RT - 1))
                if j == RT - 1:
                    mm.then_inc(s["p_out"], 1)

            def max_rows(i, p, groups):
                pe.wait_ge(s["v_neg"], i * PAIRS + p + 3)
                pe.wait_ge(s["v_negT"], i * PAIRS + p + 1)
                pe.wait_ge(s["v_out"], i * GROUPS + groups + 1)
                pe.transpose(ps[:, 7, 0:P].bitcast(F32R), neg_max[:, :],
                             ident_r[:, :]).then_inc(s["p_negT"], 1)

            def transpose_outputs(i, q, maxima):
                pe.wait_ge(s["a_out"], i * GROUPS + q + 2)
                pe.wait_ge(s["v_negT"], i * PAIRS + maxima + 1)
                pe.wait_ge(s["v_out"], i * GROUPS + q + 1)
                for t in range(RT):
                    mm = pe.transpose(ps[:, 7, t * P:(t + 1) * P], out_T[:, t * P:(t + 1) * P], ident[:, :])
                mm.then_inc(s["p_oT"], 1)

            with pe.Fori(0, B) as i:
                pe.wait_ge(s["x_in"], 16 * i + 16)
                pe.wait_ge(s["v_attl"], i * KC + 1)
                for c in range(KC):
                    for t in range(RT):
                        mm = pe.transpose(ps[:, c, t * P:(t + 1) * P], x_in[:, t, c * P:(c + 1) * P], ident[:, :])
                    mm.then_inc(s["p_xT"], 1)
                for t in range(RT + 1):
                    if t < RT:
                        if t == 0:
                            pe.wait_ge(s["v_xl"], i * KC + KC)
                            pe.wait_ge(s["v_res"], i + 1)
                        if t == 1:
                            pe.wait_ge(s["v_nl"], i * KC + 1)
                        if t >= 2:
                            pe.wait_ge(s["v_qkv"], i * RT + t - 1)
                        bank = 2 + 2 * (t % 2)
                        for half in range(2):
                            cols = slice(half * 384, (half + 1) * 384)
                            n = 0
                            for c in range(KC):
                                for x, w in ((att_h, wqkv_h), (att_h, wqkv_l), (att_l, wqkv_h)):
                                    mm = pe.matmul(ps[:, bank + half, 0:384], x[:, c, t * P:(t + 1) * P],
                                                   w[:, c, cols], start=(n == 0), stop=(n == 5))
                                    n += 1
                        mm.then_inc(s["p_qkv"], 1)
                    if t >= 1:
                        u = t - 1
                        pe.wait_ge(s["v_stack"], i * RT + u + 1)
                        if u >= 1:
                            pe.wait_ge(s["a_qT"], i * RT + u)
                            pe.wait_ge(s["v_kT"], i * RT + u)
                        for stackd, bank in ((k_stack, 0), (q_stack, 6)):
                            for p in range(PAIRS):
                                mm = pe.transpose(
                                    ps[:, bank + p // 4, (p % 4) * P:(p % 4 + 1) * P].bitcast(F32R),
                                    stackd[:, 2 * p:2 * p + 2, :].rearrange("p a b -> p (a b)"), ident_r[:, :])
                            mm.then_inc(s["p_stackT"], 1)
                pe.wait_ge(s["a_qT"], (i + 1) * RT)
                pe.wait_ge(s["v_kT"], (i + 1) * RT)
                for p in range(-LEAD, PAIRS + 2):
                    ahead = max_pass(i, p + LEAD) if p + LEAD < PAIRS else iter(())
                    for j in range(RT):
                        next(ahead, None)
                        if 0 <= p < PAIRS:
                            score_pass(i, p, j)
                        if 1 <= p <= PAIRS:
                            value_pass(i, p - 1, j)
                        if j == 1 and 0 <= p + LEAD - 1 < PAIRS:
                            max_rows(i, p + LEAD - 1, max(0, p - 2) // 2)
                        if j == 2 and p >= 3 and p % 2:
                            transpose_outputs(i, (p - 3) // 2, min(p + LEAD, PAIRS))
                pe.wait_ge(s["v_out"], (i + 1) * GROUPS + 1)
                for c in range(KC):
                    for t in range(RT):
                        mm = pe.transpose(ps[:, c, t * P:(t + 1) * P], att[:, t, c * P:(c + 1) * P], ident[:, :])
                    mm.then_inc(s["p_attT"], 1)
                pe.wait_ge(s["v_attl"], (i + 1) * KC + 1)
                for t in range(RT):
                    n = 0
                    for c in range(KC):
                        for x, w in ((att_h, wout_h), (att_h, wout_l), (att_l, wout_h)):
                            mm = pe.matmul(ps[:, 2 + t // 2, (t % 2) * D:(t % 2 + 1) * D],
                                           x[:, c, t * P:(t + 1) * P], w[:, c, :], start=(n == 0), stop=(n == 5))
                            n += 1
                mm.then_inc(s["p_proj"], 1)
                pe.wait_ge(s["v_norm"], i + 1)
                for c in range(KC):
                    for t in range(RT):
                        mm = pe.transpose(ps[:, 4 + c, t * P:(t + 1) * P], xn[:, 0, t, c * P:(c + 1) * P],
                                          ident[:, :])
                    mm.then_inc(s["p_nT"], 1)

        @block.vector
        def _(v):
            chain = Chain(v, s["v_chain"])
            for name in ("x_free", "v_attl", "v_res", "v_nl", "p_stackT", "v_out", "a_out", "p_oT", "v_negT"):
                v.sem_inc(s[name], 1)
            v.sem_inc(s["v_max"], 2)
            v.sem_inc(s["v_neg"], 2)
            v.sem_inc(s["g_x1"], 1)
            v.wait_ge(s["const_in"], 96)
            v.tensor_copy(ident_r[:, :], ident[:, :])
            v.tensor_copy(ident_b[:, :], ident[:, :])
            v.tensor_copy(mask_b[:, :], k_mask[:, :]).then_inc(s["const_v"], 1)
            v.memset(neg_max[:, :].bitcast(F32), 0.0)
            v.memset(q_stack[:, :, 3 * DH:SLOT].bitcast(F32), 0.0)
            chain.step(v.memset(k_stack[:, :, 3 * DH:SLOT].bitcast(F32), 0.0))
            chain.settle()
            v.memset(k_stack[:, :, 3 * DH:3 * DH + 1].bitcast(F32), 1.0).then_inc(s["mask_v"], 1)
            v.wait_ge(s["wsplit_h"], 1)
            v.tensor_tensor(wqkv_l[:, :, :], raw_qkv, wqkv_h[:, :, :].bitcast(F32),
                            ALU.subtract).then_inc(s["wsplit_l"], 1)
            v.wait_ge(s["wsplit_h"], 2)
            v.tensor_tensor(wout_l[:, :, :], raw_out, wout_h[:, :, :].bitcast(F32),
                            ALU.subtract).then_inc(s["wsplit_l"], 1)

            def take_outputs(i, q):
                v.wait_ge(s["p_oT"], i * GROUPS + q + 2)
                o = ps[:, 7, :].rearrange("p (t h d) -> p t h d", t=RT, h=4)
                chain.step(v.reciprocal(inv[:, :, :], o[:, :, :, DH]))
                chain.settle()
                v.tensor_tensor(
                    att[:, :, 4 * q * DH:4 * (q + 1) * DH].rearrange("p t (h d) -> p t h d", h=4),
                    o[:, :, :, 0:DH], bcast(inv[:, :, :], 3, [P, RT, 4, DH]), ALU.mult).then_inc(s["v_out"], 1)

            with v.Fori(0, B) as i:
                chain.enter(i, GROUPS + 16)
                for c in range(KC):
                    v.wait_ge(s["a_xh"], i * KC + c + 1)
                    v.tensor_tensor(att_l[:, c, :], ps[:, c, :], att_h[:, c, :].bitcast(F32),
                                    ALU.subtract).then_inc(s["v_xl"], 1)
                for t in range(RT + 2):
                    if t < RT:
                        v.wait_ge(s["p_qkv"], i * RT + t + 1)
                        if t >= 2:
                            v.wait_ge(s["a_stack"], i * RT + t - 1)
                            v.wait_ge(s["g_val"], i * RT + t)
                        bank = 2 + 2 * (t % 2)
                        v.tensor_tensor(qkv[:, t % 2, :].rearrange("p (a b) -> p a b", a=2),
                                        ps[:, bank:bank + 2, 0:384],
                                        b_qkv[:, :].rearrange("p (a b) -> p a b", a=2),
                                        ALU.add).then_inc(s["v_qkv"], 1)
                    if 1 <= t <= RT:
                        u = t - 1
                        v.wait_ge(s["a_stack"], i * RT + u + 1)
                        heads = qkv[:, u % 2, :].rearrange("p (h c d) -> p h c d", h=H, c=3)
                        v.tensor_tensor(q_stack[:, :, DH:2 * DH], heads[:, :, 0, :],
                                        q_stack[:, :, 0:DH].bitcast(F32), ALU.subtract)
                        v.tensor_tensor(k_stack[:, :, 2 * DH:3 * DH], heads[:, :, 1, :],
                                        k_stack[:, :, 0:DH].bitcast(F32), ALU.subtract).then_inc(s["v_stack"], 1)
                        v.wait_ge(s["p_stackT"], 2 * (i * RT + u) + 2)
                        v.tensor_copy(kT[:, :, u * P:(u + 1) * P],
                                      ps[:, 0:2, :].rearrange("p a (b c) -> p (a b) c", c=P)
                                      ).then_inc(s["v_kT"], 1)
                for p in range(-LEAD, PAIRS + 2):
                    if p + LEAD < PAIRS:
                        v.wait_ge(s["v_neg"], i * PAIRS + p + LEAD + 1)
                    for t in range(RT):
                        if p + LEAD < PAIRS:
                            for o in range(2):
                                n = i * 2 * PAIRS * RT + ((p + LEAD) * RT + t) * 2 + o
                                v.wait_ge(s["p_max"], n + 1)
                                v.sem_inc(g.carrier["v_carrier"], 1)
                                v.tensor_tensor_reduce(
                                    ps[:, o, 0:(t + 1) * P], ps[:, o, 0:(t + 1) * P],
                                    q_mask[:, S - (t + 1) * P:S], 1.0, MASKED, ALU.add, ALU.max,
                                    top_score[:, (p + LEAD) % 2, o * RT + t:o * RT + t + 1]).then_inc(s["v_max"], 1)
                        if t == 1 and 0 <= p + LEAD - 1 < PAIRS:
                            q = p + LEAD - 1
                            if q >= 2:
                                v.wait_ge(s[f"m_row{q % 2}"], 32 * (i * (PAIRS // 2) + q // 2))
                            v.wait_ge(s["p_negT"], i * PAIRS + q + 1)
                            v.tensor_copy(neg_rows[:, q % 2, :],
                                          ps[0:2 * RT, 7, 0:P]).then_inc(s["v_negT"], 1)
                        if t == 3 and p >= 3 and p % 2:
                            take_outputs(i, (p - 3) // 2)
                    if p + LEAD < PAIRS:
                        q = p + LEAD
                        v.wait_ge(s["v_max"], i * 2 * PAIRS * RT + (q + 1) * 2 * RT + 2)
                        v.tensor_scalar(neg_max[:, 0:2 * RT], top_score[:, q % 2, :], -1.0, None,
                                        ALU.mult).then_inc(s["v_neg"], 1)
                for c in range(KC):
                    v.wait_ge(s["a_atth"], i * KC + c + 1)
                    v.tensor_tensor(att_l[:, c, :], ps[:, c, :], att_h[:, c, :].bitcast(F32),
                                    ALU.subtract).then_inc(s["v_attl"], 1)
                v.wait_ge(s["xres_in"], 16 * i + 16)
                chain.step(v.tensor_tensor(x_res, x_res, bcast(b_out[:, :], 1, [P, RT, D]), ALU.add))
                chain.settle()
                v.wait_ge(s["p_proj"], i + 1)
                ins = v.tensor_tensor(g.rsum[:, :, :], ps[:, 2:4, :].rearrange("p a (b c) -> p (a b) c", c=D),
                                      x_res, ALU.add)
                chain.step(ins)
                chain.settle()
                v.sem_inc(s["v_res"], 1)
                v.sem_inc(s["x_free"], 1)
                v.wait_ge(s["g_x1"], i + 1)
                layernorm(v, chain, g.lnw, g.rsum, xn[:, 0, :, :], s["v_norm"])
                for c in range(KC):
                    v.wait_ge(s["a_nh"], i * KC + c + 1)
                    v.tensor_tensor(g.xT_l[:, i, c, :], ps[:, 4 + c, :], g.xT_h[:, i, c, :].bitcast(F32),
                                    ALU.subtract).then_inc(s["v_nl"], 1)
            chain.leave(B)


def gates(nc, A, g):
    ps = g.ps
    stack = ExitStack()
    with stack:
        s = sems(stack, nc, "p_gate a_gate a_trig v_h v_chain a_hh v_hl")
        amp = sb(stack, nc, "amp", [P, B, KC, S])
        tanh = sb(stack, nc, "tanh", [P, B, KC, S])
        half = g.x_b[:, :, :].rearrange("p (b n) d -> p b (n d)", b=B).rearrange("p b (c s) -> p b c s", c=KC)
        block = stack.enter_context(nc.Block())

        @block.sync
        def _(sp):
            sp.dma_start(g.w1_raw[:, :, :],
                         A["L1_ffn_W1"][0].rearrange("(c p) n -> p c n", p=P)).then_inc(g.pre["w1_in"], 16)
            sp.dma_start(g.w2_raw[:, :, :],
                         A["L1_ffn_W2"][0].rearrange("(c p) n -> p c n", p=P)).then_inc(g.pre["w2_in"], 16)

        @block.tensor
        def _(pe):
            for b in range(B):
                for w in range(2):
                    for m in range(KC):
                        n = (b * 2 + w) * KC + m
                        if n >= 8:
                            pe.wait_ge(s["a_gate"], n - 7)
                        k = 0
                        for c in range(KC):
                            cols = slice(w * D + m * P, w * D + (m + 1) * P)
                            for wt, x in ((g.gate_h, g.xT_h), (g.gate_h, g.xT_l), (g.gate_l, g.xT_h)):
                                mm = pe.matmul(ps[:, n % 8, :], wt[:, c, cols], x[:, b, c, :],
                                               start=(k == 0), stop=(k == 5))
                                k += 1
                        mm.then_inc(s["p_gate"], 1)

        @block.scalar
        def _(act):
            for b in range(B):
                for w, (func, dst) in enumerate(((ACT.Sigmoid, amp), (ACT.Tanh, tanh))):
                    for m in range(KC):
                        n = (b * 2 + w) * KC + m
                        act.wait_ge(s["p_gate"], n + 1)
                        act.activation(dst[:, b, m, :], ps[:, n % 8, :], func,
                                       bias=g.bias_col[:, 2 * w + m:2 * w + m + 1]).then_inc(s["a_gate"], 1)
            for b in range(B):
                act.wait_ge(s["a_gate"], (b + 1) * 4)
                act.activation(half[:, b, :, :], tanh[:, b, :, :], ACT.Sin, scale=PI_F32 / 2
                               ).then_inc(s["a_trig"], 1)
                act.wait_ge(s["a_trig"], 2 * b + 1)
                act.activation(tanh[:, b, :, :], tanh[:, b, :, :], ACT.Sin, scale=PI_F32
                               ).then_inc(s["a_trig"], 1)
            for b in range(B):
                act.wait_ge(s["v_h"], b + 1)
                act.activation(g.xT_h[:, b, :, :], amp[:, b, :, :], ACT.Copy).then_inc(s["a_hh"], 1)

        @block.vector
        def _(v):
            chain = Chain(v, s["v_chain"])
            for b in range(B):
                v.wait_ge(s["a_trig"], 2 * b + 2)
                chain.step(v.tensor_tensor(half[:, b, :, :], half[:, b, :, :], half[:, b, :, :], ALU.mult))
                chain.settle()
                chain.step(v.scalar_tensor_tensor(half[:, b, :, :], half[:, b, :, :], -2.0, tanh[:, b, :, :],
                                                  ALU.mult, ALU.add))
                chain.settle()
                v.scalar_tensor_tensor(amp[:, b, :, :], half[:, b, :, :], 1.0, amp[:, b, :, :],
                                       ALU.add, ALU.mult).then_inc(s["v_h"], 1)
                if b:
                    v.wait_ge(s["a_hh"], b)
                    v.tensor_tensor(g.xT_l[:, b - 1, :, :], amp[:, b - 1, :, :],
                                    g.xT_h[:, b - 1, :, :].bitcast(F32), ALU.subtract).then_inc(s["v_hl"], 1)
            v.wait_ge(s["a_hh"], B)
            v.tensor_tensor(g.xT_l[:, B - 1, :, :], amp[:, B - 1, :, :],
                            g.xT_h[:, B - 1, :, :].bitcast(F32), ALU.subtract).then_inc(s["v_hl"], 1)


def stages(nc, A, g):
    ps, ident, xn, hs = g.ps, g.ident, g.xn, g.hs
    stack = ExitStack()
    with stack:
        s = sems(stack, nc, "p_lin v_sum v_norm g_hs p_T a_th v_tl v_chain g_chain v_norm2 g_x2")
        block = stack.enter_context(nc.Block())


        @block.tensor
        def _(pe):
            def linear(st, b):
                pe.wait_ge(s["v_tl"], st * 2 * B + 2 * (b + 1))
                pe.wait_ge(s["v_sum"], st * B + (4, 2, 3, 5)[b])
                for t in range(RT):
                    n = 0
                    for c in range(KC):
                        for x, w in ((g.xT_h, g.stage_w_h), (g.xT_h, g.stage_w_l), (g.xT_l, g.stage_w_h)):
                            mm = pe.matmul(ps[:, 2 * (b % 3) + t // 2, (t % 2) * D:(t % 2 + 1) * D],
                                           x[:, b, c, t * P:(t + 1) * P], w[:, st, c, :],
                                           start=(n == 0), stop=(n == 5))
                            n += 1
                mm.then_inc(s["p_lin"], 1)

            def transposes(st, b, src, ready, count):
                pe.wait_ge(ready, count)
                pe.wait_ge(s["v_tl"], st * 2 * B + 2 * b + 2 * B)
                for c in range(KC):
                    for t in range(RT):
                        mm = pe.transpose(ps[:, 6 + c, t * P:(t + 1) * P], src[:, b % 2, t, c * P:(c + 1) * P],
                                          ident[:, :])
                    mm.then_inc(s["p_T"], 1)

            with pe.Fori(0, STAGES - 1) as st:
                for b in range(B):
                    linear(st, b)
                for b in range(B):
                    transposes(st, b, hs, s["g_hs"], st * B + b + 3)
            for b in range(B):
                linear(STAGES - 1, b)
            for b in range(B):
                transposes(STAGES - 1, b, xn, s["v_norm2"], b + 1)

        @block.scalar
        def _(act):
            def high(st, b):
                for c in range(KC):
                    act.wait_ge(s["p_T"], st * 2 * B + 2 * b + c + 1 + 4)
                    act.activation(g.xT_h[:, b, c, :], ps[:, 6 + c, :], ACT.Copy).then_inc(s["a_th"], 1)

            with act.Fori(0, STAGES - 1) as st:
                for b in range(B):
                    high(st, b)
            for b in range(B):
                high(STAGES - 1, b)

        @block.gpsimd
        def _(pool):
            chain = Chain(pool, s["g_chain"])
            pool.wait_ge(g.pre["rows_in"], 16 * 11)

            def affine(st, b):
                pool.wait_ge(s["v_norm"], st * B + b + 2)
                pool.sem_inc(g.carrier["g_carrier"], 1)
                chain.step(pool.tensor_tensor(xn[:, b % 2, :, :], xn[:, b % 2, :, :],
                                              bcast(g.stage_g[:, st, :], 1, [P, RT, D]), ALU.mult))
                chain.settle()

            def shift(st, b):
                pool.sem_inc(g.carrier["g_carrier"], 1)
                pool.tensor_tensor(hs[:, b % 2, :, :], xn[:, b % 2, :, :],
                                   bcast(g.stage_b[:, st, :], 1, [P, RT, D]), ALU.add).then_inc(s["g_hs"], 1)

            with pool.Fori(0, STAGES - 1) as st:
                chain.enter(st, B)
                for b in range(B):
                    affine(st, b)
                    pool.wait_ge(s["p_T"], st * 2 * B + 2 * b + 2)
                    shift(st, b)
            chain.leave(STAGES - 1)
            for b in range(B):
                affine(STAGES - 1, b)
                if b < 2:
                    pool.wait_ge(s["p_T"], (STAGES - 1) * 2 * B + 2 * b + 2)
                else:
                    pool.wait_ge(s["v_norm2"], b - 1)
                shift(STAGES - 1, b)
                pool.wait_ge(s["v_norm2"], b + 1)
                pool.tensor_copy(g.x_b[:, b * RT:(b + 1) * RT, :], xn[:, b % 2, :, :]).then_inc(s["g_x2"], 1)

        @block.vector
        def _(v):
            chain = Chain(v, s["v_chain"])
            v.sem_inc(s["v_tl"], 2 * B)
            v.sem_inc(s["v_sum"], B)
            v.sem_inc(s["v_norm"], 1)
            v.sem_inc(s["g_hs"], 2)
            v.sem_inc(s["p_T"], 4)

            def norm(st, b, extra=()):
                v.wait_ge(s["p_lin"], st * B + b + 1)
                bank = 2 * (b % 3)
                v.wait_ge(s["v_norm"], st * B + b + 1)
                chain.step(v.tensor_tensor(g.rsum[:, :, :],
                                           ps[:, bank:bank + 2, :].rearrange("p a (b c) -> p (a b) c", c=D),
                                           bcast(g.stage_c[:, st, :], 1, [P, RT, D]), ALU.add))
                chain.settle()
                v.sem_inc(s["v_sum"], 1)
                v.wait_ge(s["g_hs"], st * B + b + 1)
                for sem, count in extra:
                    v.wait_ge(sem, count)
                layernorm(v, chain, g.lnw, g.rsum, xn[:, b % 2, :, :], s["v_norm"])

            def low(st, b):
                for c in range(KC):
                    v.wait_ge(s["a_th"], st * 2 * B + 2 * b + c + 1)
                    v.tensor_tensor(g.xT_l[:, b, c, :], ps[:, 6 + c, :], g.xT_h[:, b, c, :].bitcast(F32),
                                    ALU.subtract).then_inc(s["v_tl"], 1)

            with v.Fori(0, STAGES - 1) as st:
                chain.enter(st, 15 * B)
                for b in range(B):
                    norm(st, b)
                    if b:
                        low(st, b - 1)
                low(st, B - 1)
            chain.leave(STAGES - 1)
            st = STAGES - 1
            for b in range(B):
                if b:
                    v.wait_ge(s["v_norm2"], b)
                norm(st, b, [(s["g_x2"], b - 1), (s["p_T"], st * 2 * B + 2 * b + 2)] if b >= 2 else [])
                v.wait_ge(s["v_norm"], st * B + b + 2)
                v.wait_ge(s["g_hs"], st * B + b + 3)
                chain.step(v.tensor_tensor(g.rsum[:, :, :], hs[:, b % 2, :, :],
                                           g.x_a[:, b * RT:(b + 1) * RT, :], ALU.add))
                chain.settle()
                layernorm(v, chain, g.lnw, g.rsum, xn[:, b % 2, :, :], s["v_norm2"])
                if b:
                    low(st, b - 1)
            low(st, B - 1)


def attention1(nc, A, g):
    ps, ident, hs = g.ps, g.ident, g.hs
    UNITS = KC + RT
    NUM = P + P // DH
    stack = ExitStack()
    with stack:
        s = sems(stack, nc, "blocks_in g_ones p_unit a_exp a_v v_unit p_kv v_bd p_num v_att v_z "
                 "p_attT a_th v_tl p_proj v_sum v_chain v_norm g_xa x3_out0 x3_out1 p_T a_xh v_xl")
        blocks = sb(stack, nc, "blocks", [P, NUM])
        q = sb(stack, nc, "q", [P, 2, KC, S])
        k = sb(stack, nc, "k", [P, 2, RT, D])
        v1 = sb(stack, nc, "v1", [P, 2, RT, KC, P + 1])
        ex = sb(stack, nc, "ex", [P, 2, S])
        pos = sb(stack, nc, "pos", [P, 2, S])
        bd = sb(stack, nc, "bd", [P, KC, NUM])
        z = sb(stack, nc, "z", [P, 2, KC, P // DH])
        att = sb(stack, nc, "att1", [P, RT, D])
        att_h = sb(stack, nc, "att1_h", [P, KC, S], F32R)
        att_l = sb(stack, nc, "att1_l", [P, KC, S], F32R)
        block = stack.enter_context(nc.Block())

        @block.sync
        def _(sp):
            sp.dma_start(blocks[:, :], A["c_blocks"]).then_inc(s["blocks_in"], 16)
            for b in range(B):
                sp.wait_ge(s["v_norm"], b + 1)
                sp.dma_start(g.x3_dram[b].rearrange("(t p) d -> p t d", p=P), hs[:, b % 2, :, :]
                             ).then_inc(s[f"x3_out{b % 2}"], 16)
            sp.wait_ge(s["x3_out0"], 16 * B // 2)
            sp.wait_ge(s["x3_out1"], 16 * B // 2)

        @block.gpsimd
        def _(pool):
            pool.memset(v1[:, :, :, :, P:P + 1], 1.0).then_inc(s["g_ones"], 1)
            for b in range(B):
                pool.wait_ge(s["v_norm"], b + 1)
                pool.tensor_tensor(g.x_a[:, b * RT:(b + 1) * RT, :], hs[:, b % 2, :, :],
                                   bcast(g.mlp_b2[:, 0, :], 1, [P, RT, D]), ALU.add).then_inc(s["g_xa"], 1)

        @block.tensor
        def _(pe):
            pe.wait_ge(s["g_ones"], 1)

            def unit(b, j):
                n = b * UNITS + j
                if n >= 3:
                    pe.wait_ge(s["a_exp"], n - 2)
                    if (n - 3) % UNITS >= KC:
                        pe.wait_ge(s["a_v"], (n - 3) // UNITS * RT + (n - 3) % UNITS - KC + 1)
                i = 0
                for c in range(KC):
                    if j < KC:
                        cols = slice(j * P, (j + 1) * P)
                        parts = ((g.wq_h[:, c, cols], g.xT_h[:, b, c, :]), (g.wq_h[:, c, cols], g.xT_l[:, b, c, :]),
                                 (g.wq_l[:, c, cols], g.xT_h[:, b, c, :]))
                    else:
                        cols = slice((j - KC) * P, (j - KC + 1) * P)
                        parts = ((g.xT_h[:, b, c, cols], g.wkv_h[:, c, :]), (g.xT_h[:, b, c, cols], g.wkv_l[:, c, :]),
                                 (g.xT_l[:, b, c, cols], g.wkv_h[:, c, :]))
                    for lhsT, rhs in parts:
                        mm = pe.matmul(ps[:, n % 3, :], lhsT, rhs, start=(i == 0), stop=(i == 5))
                        i += 1
                mm.then_inc(s["p_unit"], 1)

            def key_values(b):
                pe.wait_ge(s["v_unit"], (b + 1) * UNITS)
                pe.wait_ge(s["a_v"], (b + 1) * RT)
                if b:
                    pe.wait_ge(s["v_att"], 2 * b)
                for m in range(KC):
                    for t in range(RT):
                        mm = pe.matmul(ps[:, 3, m * D:m * D + P + 1], k[:, b % 2, t, m * P:(m + 1) * P],
                                       v1[:, b % 2, t, m, :], start=(t == 0), stop=(t == RT - 1))
                mm.then_inc(s["p_kv"], 1)

            def numerators(b, half):
                if half == 0:
                    pe.wait_ge(s["v_bd"], b + 1)
                else:
                    pe.wait_ge(s["v_att"], 2 * b + 1)
                for t in (2 * half, 2 * half + 1):
                    for m in range(KC):
                        mm = pe.matmul(ps[:, 3 + t % 2, m * NUM:(m + 1) * NUM], q[:, b % 2, m, t * P:(t + 1) * P],
                                       bd[:, m, :], start=True, stop=True)
                mm.then_inc(s["p_num"], 1)

            def transpose_attention(b):
                pe.wait_ge(s["v_att"], 2 * b + 2)
                if b:
                    pe.wait_ge(s["v_sum"], b)
                for c in range(KC):
                    for t in range(RT):
                        mm = pe.transpose(ps[:, 5 + c, t * P:(t + 1) * P], att[:, t, c * P:(c + 1) * P], ident[:, :])
                    mm.then_inc(s["p_attT"], 1)

            def project(b):
                pe.wait_ge(s["v_tl"], KC * (b + 1))
                for t in range(RT):
                    n = 0
                    for c in range(KC):
                        for x, w in ((att_h, g.wo_h), (att_h, g.wo_l), (att_l, g.wo_h)):
                            mm = pe.matmul(ps[:, 5 + t // 2, (t % 2) * D:(t % 2 + 1) * D],
                                           x[:, c, t * P:(t + 1) * P], w[:, c, :], start=(n == 0), stop=(n == 5))
                            n += 1
                mm.then_inc(s["p_proj"], 1)

            def transpose_next(b, c):
                pe.wait_ge(s["v_norm"], b + 1)
                if b + c:
                    pe.wait_ge(s["v_xl"], KC * b + c)
                for t in range(RT):
                    mm = pe.transpose(ps[:, 7, t * P:(t + 1) * P], hs[:, b % 2, t, c * P:(c + 1) * P], ident[:, :])
                mm.then_inc(s["p_T"], 1)

            for step in range(B + 2):
                if 0 <= step - 2:
                    transpose_attention(step - 2)
                if step < B:
                    for j in range(UNITS):
                        unit(step, j)
                if 0 <= step - 1 < B:
                    key_values(step - 1)
                if 0 <= step - 2:
                    project(step - 2)
                for half in range(2):
                    if 0 <= step - 1 < B:
                        numerators(step - 1, half)
                    if 0 <= step - 3:
                        transpose_next(step - 3, half)

        @block.scalar
        def _(act):
            for step in range(B + 2):
                if 0 <= step - 2:
                    b = step - 2
                    for c in range(KC):
                        act.wait_ge(s["p_attT"], KC * b + c + 1)
                        if b:
                            act.wait_ge(s["p_proj"], b)
                        act.activation(att_h[:, c, :], ps[:, 5 + c, :], ACT.Copy).then_inc(s["a_th"], 1)
                if step < B:
                    b = step
                    for j in range(UNITS):
                        n = b * UNITS + j
                        width = S if j < KC else D
                        act.wait_ge(s["p_unit"], n + 1)
                        if n >= 2:
                            act.wait_ge(s["v_unit"], n - 1)
                        act.activation(ex[:, n % 2, 0:width], ps[:, n % 3, 0:width], ACT.Exp)
                        act.activation(pos[:, n % 2, 0:width], ps[:, n % 3, 0:width], ACT.Relu
                                       ).then_inc(s["a_exp"], 1)
                        if j >= KC:
                            if b >= 2:
                                act.wait_ge(s["p_kv"], b - 1)
                            act.activation(v1[:, b % 2, j - KC, :, 0:P],
                                           ps[:, n % 3, D:2 * D].rearrange("p (m n) -> p m n", m=KC),
                                           ACT.Copy).then_inc(s["a_v"], 1)
                if 0 <= step - 3:
                    b = step - 3
                    for c in range(KC):
                        act.wait_ge(s["p_T"], KC * b + c + 1)
                        act.activation(g.xT_h[:, b, c, :], ps[:, 7, :], ACT.Copy).then_inc(s["a_xh"], 1)

        @block.vector
        def _(v):
            chain = Chain(v, s["v_chain"])
            v.wait_ge(s["blocks_in"], 16)

            def unit(b, j):
                n = b * UNITS + j
                width = S if j < KC else D
                v.wait_ge(s["a_exp"], n + 1)
                if b >= 2:
                    if j < KC:
                        v.wait_ge(s["p_num"], 2 * (b - 1))
                    else:
                        v.wait_ge(s["p_kv"], b - 1)
                dst = q[:, b % 2, j, :] if j < KC else k[:, b % 2, j - KC, :]
                v.scalar_tensor_tensor(dst, ex[:, n % 2, 0:width], 1.0, pos[:, n % 2, 0:width],
                                       ALU.min, ALU.add).then_inc(s["v_unit"], 1)

            def block_diagonal(b):
                v.wait_ge(s["p_kv"], b + 1)
                if b:
                    v.wait_ge(s["p_num"], 2 * b)
                kv = ps[:, 3, :].rearrange("p (m n) -> p m n", m=KC)
                v.tensor_tensor(bd[:, :, 0:P], kv[:, :, 0:P], bcast(blocks[:, 0:P], 1, [P, KC, P]), ALU.mult)
                v.tensor_tensor(bd[:, :, P:NUM], kv[:, :, P:P + 1].broadcast_to([P, KC, NUM - P]),
                                bcast(blocks[:, P:NUM], 1, [P, KC, NUM - P]), ALU.mult).then_inc(s["v_bd"], 1)

            def normalise(b, half):
                v.wait_ge(s["p_num"], 2 * b + half + 1)
                if b + half:
                    v.wait_ge(s["v_att"], 2 * b + half)
                o = ps[:, 3:5, 0:KC * NUM].rearrange("p t (m n) -> p t m n", m=KC)
                v.tensor_scalar(z[:, :, :, :], o[:, :, :, P:NUM], 1e-6, None, ALU.add).then_inc(s["v_z"], 1)
                v.wait_ge(s["v_z"], 2 * (2 * b + half) + 1)
                v.reciprocal(z[:, :, :, :], z[:, :, :, :]).then_inc(s["v_z"], 1)
                v.wait_ge(s["v_z"], 2 * (2 * b + half) + 2)
                if b:
                    v.wait_ge(s["p_attT"], KC * b)
                for i in range(2):
                    ins = v.tensor_tensor(
                        att[:, 2 * half + i, :].rearrange("p (m h d) -> p m h d", m=KC, d=DH),
                        o[:, i, :, 0:P].rearrange("p m (h d) -> p m h d", d=DH),
                        bcast(z[:, i, :, :], 3, [P, KC, P // DH, DH]), ALU.mult)
                ins.then_inc(s["v_att"], 1)

            for step in range(B + 2):
                if 0 <= step - 2:
                    b = step - 2
                    for c in range(KC):
                        v.wait_ge(s["a_th"], KC * b + c + 1)
                        v.tensor_tensor(att_l[:, c, :], ps[:, 5 + c, :], att_h[:, c, :].bitcast(F32),
                                        ALU.subtract).then_inc(s["v_tl"], 1)
                if step < B:
                    for j in range(UNITS):
                        unit(step, j)
                if 0 <= step - 1 < B:
                    block_diagonal(step - 1)
                if 0 <= step - 2:
                    b = step - 2
                    v.wait_ge(s["p_proj"], b + 1)
                    if b:
                        v.wait_ge(s["v_norm"], b)
                    v.tensor_tensor(g.rsum[:, :, :], ps[:, 5:7, :].rearrange("p a (b c) -> p (a b) c", c=D),
                                    g.x_b[:, b * RT:(b + 1) * RT, :], ALU.add).then_inc(s["v_sum"], 1)
                for half in range(2):
                    if 0 <= step - 1 < B:
                        normalise(step - 1, half)
                    if 0 <= step - 3:
                        v.wait_ge(s["a_xh"], KC * (step - 3) + half + 1)
                        v.tensor_tensor(g.xT_l[:, step - 3, half, :], ps[:, 7, :],
                                        g.xT_h[:, step - 3, half, :].bitcast(F32),
                                        ALU.subtract).then_inc(s["v_xl"], 1)
                if 0 <= step - 2:
                    b = step - 2
                    v.wait_ge(s["v_sum"], b + 1)
                    if b >= 2:
                        v.wait_ge(s["p_T"], KC * (b - 1))
                        v.wait_ge(s[f"x3_out{b % 2}"], 16 * (b // 2))
                        v.wait_ge(s["g_xa"], b - 1)
                    layernorm(v, chain, g.lnw, g.rsum, hs[:, b % 2, :, :], s["v_norm"])


def ffn1(nc, A, g, out):
    ps, ident, xn, hs = g.ps, g.ident, g.xn, g.hs
    TU = 16
    stack = ExitStack()
    with stack:
        s = sems(stack, nc, "p_T a_T v_T p_hid a_g v_gl p_out v_sum v_chain v_norm g_chain g_hs g_res "
                 "x3_in0 x3_in1 y_out0 y_out1")
        w1_in, w2_in = g.pre["w1_in"], g.pre["w2_in"]
        w1_h = sb(stack, nc, "w1_h", [P, KC, HID], F32R)
        w1_l = sb(stack, nc, "w1_l", [P, KC, HID], F32R)
        w2_h = sb(stack, nc, "w2_h", [P, FC, D], F32R)
        w2_l = sb(stack, nc, "w2_l", [P, FC, D], F32R)
        G_h = sb(stack, nc, "G_h", [P, 2, FC, S], F32R)
        G_l = sb(stack, nc, "G_l", [P, 2, FC, S], F32R)
        G32 = sb(stack, nc, "G32", [P, 4, S])
        y_dram = out.rearrange("b (t p) d -> p b t d", p=P)
        x3 = g.x3_dram.rearrange("b (t p) d -> p b t d", p=P)
        block = stack.enter_context(nc.Block())
        LAST = BLOCKS - 1

        def target(u, w1, w2, x):
            if u < 4:
                return w2[:, 2 * u:2 * u + 2, :]
            if 8 <= u < 12:
                c, half = divmod(u - 8, 2)
                return w1[:, c, half * S:(half + 1) * S].rearrange("p (a b) -> p a b", a=2)
            b = {4: 3, 6: 0, 12: 1, 14: 2}[u - u % 2]
            return x[:, b, u % 2, :].rearrange("p (a b) -> p a b", a=2)

        @block.sync
        def _(sp):
            def load_w1(k):
                sp.dma_start(g.w1_raw[:, :, :], A["L1_ffn_W1"][k].rearrange("(c p) n -> p c n", p=P)
                             ).then_inc(w1_in, 16)

            def load_w2(k):
                sp.dma_start(g.w2_raw[:, :, :], A["L1_ffn_W2"][k].rearrange("(c p) n -> p c n", p=P)
                             ).then_inc(w2_in, 16)

            sp.wait_ge(s["p_T"], 4)
            load_w1(1)
            with sp.Fori(0, BLOCKS - 2) as i:
                sp.wait_ge(s["p_T"], i * TU + 8)
                load_w2(i + 1)
                sp.wait_ge(s["p_T"], i * TU + 16)
                load_w1(i + 2)
            sp.wait_ge(s["p_T"], (LAST - 1) * TU + 8)
            load_w2(LAST)
            sp.wait_ge(s["p_T"], (LAST - 1) * TU + 16)
            sp.dma_start(g.w1_raw[:, :, :].rearrange("p (b t) d -> p b t d", b=2), x3[:, 0:2, :, :]
                         ).then_inc(s["x3_in0"], 16)
            sp.wait_ge(s["p_T"], LAST * TU + 8)
            sp.dma_start(g.w2_raw[:, :, :].rearrange("p a (b d) -> p a b d", d=D), x3[:, 2:4, :, :]
                         ).then_inc(s["x3_in1"], 16)
            for b in range(B):
                sp.wait_ge(s["v_norm"], LAST * B + b + 2)
                sp.dma_start(y_dram[:, b, :, :], xn[:, b % 2, :, :]).then_inc(s[f"y_out{b % 2}"], 16)
            for b in range(2):
                sp.wait_ge(s[f"y_out{b}"], 16 * B // 2)

        @block.gpsimd
        def _(pool):
            chain = Chain(pool, s["g_chain"])
            pool.sem_inc(s["g_hs"], 2)
            pool.sem_inc(s["g_res"], B)
            with pool.Fori(0, LAST) as i:
                chain.enter(i, B)
                for b in range(B):
                    pool.wait_ge(s["v_norm"], i * B + b + 2)
                    pool.sem_inc(g.carrier["g_carrier"], 1)
                    chain.step(pool.tensor_tensor(xn[:, b % 2, :, :], xn[:, b % 2, :, :],
                                                  bcast(g.mlp_g[:, i, :], 1, [P, RT, D]), ALU.mult))
                    chain.settle()
                    pool.wait_ge(s["p_T"], i * TU + (4, 10, 12, 18)[b])
                    pool.sem_inc(g.carrier["g_carrier"], 1)
                    pool.tensor_tensor(hs[:, b % 2, :, :], xn[:, b % 2, :, :],
                                       bcast(g.mlp_b[:, i, :], 1, [P, RT, D]), ALU.add).then_inc(s["g_hs"], 1)
                    pool.wait_ge(s["g_hs"], i * B + b + 3)
                    pool.sem_inc(g.carrier["g_carrier"], 1)
                    pool.tensor_tensor(g.x_a[:, b * RT:(b + 1) * RT, :], hs[:, b % 2, :, :],
                                       bcast(g.mlp_b2[:, i + 1, :], 1, [P, RT, D]), ALU.add
                                       ).then_inc(s["g_res"], 1)

        @block.tensor
        def _(pe):
            def transpose_unit(i, u):
                first = isinstance(i, int) and i < 0
                number = u - 8 if first else i * TU + 4 + u
                if u in (4, 6, 12, 14):
                    pe.wait_ge(s["g_hs"], i * B + {4: 2, 6: 3, 12: 4, 14: 5}[u])
                elif u == 0:
                    pe.wait_ge(w2_in, (i + 1) * 16)
                elif u == 8:
                    pe.wait_ge(w1_in, 16 if first else (i + 2) * 16)
                if not first or number >= 1:
                    pe.wait_ge(s["v_T"], number)
                for k in range(4):
                    if u < 4:
                        f, c = 2 * u + k // KC, k % KC
                        src = g.w2_raw[:, c, f * P:(f + 1) * P]
                    elif 8 <= u < 12:
                        c, f = (u - 8) // 2, (u - 8) % 2 * 4 + k
                        src = g.w1_raw[:, f, c * P:(c + 1) * P]
                    else:
                        b, c = {4: 3, 6: 0, 12: 1, 14: 2}[u - u % 2], u % 2
                        src = hs[:, b % 2, k, c * P:(c + 1) * P]
                    mm = pe.transpose(ps[:, 6 + u % 2, k * P:(k + 1) * P], src, ident[:, :])
                mm.then_inc(s["p_T"], 1)

            def hidden(i, b, f):
                n = b * FC + f
                pe.wait_ge(s["a_g"], i * B * FC + n + 1)
                k = 0
                for c in range(KC):
                    for w, x in ((w1_h, g.xT_h), (w1_h, g.xT_l), (w1_l, g.xT_h)):
                        mm = pe.matmul(ps[:, n % 4, :], w[:, c, f * P:(f + 1) * P], x[:, b, c, :],
                                       start=(k == 0), stop=(k == 5))
                        k += 1
                mm.then_inc(s["p_hid"], 1)

            def output(i, b, between=()):
                pe.wait_ge(s["v_gl"], i * B * FC + b * FC + 12)
                pe.wait_ge(s["v_sum"], i * B + b + 1)
                for t in range(RT):
                    k = 0
                    for f in range(FC):
                        for x, w in ((G_h, w2_h), (G_h, w2_l), (G_l, w2_h)):
                            mm = pe.matmul(ps[:, 4 + t // 2, (t % 2) * D:(t % 2 + 1) * D],
                                           x[:, b % 2, f, t * P:(t + 1) * P], w[:, f, :],
                                           start=(k == 0), stop=(k == 3 * FC - 1))
                            k += 1
                    if t == RT - 1:
                        mm.then_inc(s["p_out"], 1)
                    if t < len(between):
                        transpose_unit(i, between[t])

            def turn(i, last):
                for f in range(FC):
                    if f == 0:
                        pe.wait_ge(s["v_T"], i * TU + 1)
                    hidden(i, 0, f)
                    if f % 2:
                        transpose_unit(i, f // 2)
                for u in (4, 5):
                    transpose_unit(i, u)
                pe.wait_ge(s["v_T"], i * TU + 3)
                for f in range(FC):
                    hidden(i, 1, f)
                pe.wait_ge(s["v_T"], i * TU + 9)
                output(i, 0)
                for f in range(FC):
                    hidden(i, 2, f)
                output(i, 1)
                if not last:
                    for u in (6, 7):
                        transpose_unit(i, u)
                pe.wait_ge(s["v_T"], i * TU + 11)
                for f in range(FC):
                    hidden(i, 3, f)
                output(i, 2, () if last else (8, 9, 10, 11))
                if not last:
                    for u in (12, 13):
                        transpose_unit(i, u)
                output(i, 3)
                if not last:
                    for u in (14, 15):
                        transpose_unit(i, u)

            for u in range(8, 12):
                transpose_unit(-1, u)
            pe.wait_ge(s["v_T"], 5)
            with pe.Fori(0, LAST) as i:
                turn(i, False)
            turn(LAST, True)

        @block.scalar
        def _(act):
            def high(i, u):
                act.wait_ge(s["p_T"], u - 7 if isinstance(i, int) and i < 0 else i * TU + u + 5)
                act.activation(target(u, w1_h, w2_h, g.xT_h), ps[:, 6 + u % 2, :].rearrange("p (a b) -> p a b", a=2),
                               ACT.Copy).then_inc(s["a_T"], 1)

            def gelu(i, b, f):
                n = b * FC + f
                bias = g.bias_col[:, bass.ds(4 + 2 * MC0 + i * FC + f, 1)]
                act.wait_ge(s["p_hid"], i * B * FC + n + 1)
                act.wait_ge(s["v_gl"], i * B * FC + n + 1)
                if f == 0:
                    act.wait_ge(s["p_out"], i * B + b + 1)
                act.sem_inc(g.carrier["a_carrier"], 1)
                act.activation(G32[:, n % 4, :], ps[:, n % 4, :], ACT.Gelu, bias=bias)
                act.activation(G_h[:, b % 2, f, :], ps[:, n % 4, :], ACT.Gelu, bias=bias).then_inc(s["a_g"], 1)

            def turn(i, last):
                for f in range(FC):
                    gelu(i, 0, f)
                    if f % 2:
                        high(i, f // 2)
                for u in (4, 5):
                    high(i, u)
                for b in (1, 2):
                    for f in range(FC):
                        gelu(i, b, f)
                if not last:
                    for u in (6, 7):
                        high(i, u)
                for f in range(FC):
                    gelu(i, 3, f)
                if not last:
                    for u in range(8, 16):
                        high(i, u)

            for u in range(8, 12):
                high(-1, u)
            with act.Fori(0, LAST) as i:
                turn(i, False)
            turn(LAST, True)

        @block.vector
        def _(v):
            chain = Chain(v, s["v_chain"])
            v.sem_inc(s["v_T"], 1)
            v.sem_inc(s["a_g"], 4)
            v.sem_inc(s["v_gl"], 4)
            v.sem_inc(s["p_out"], 2)
            v.sem_inc(s["v_sum"], 1)
            v.sem_inc(s["v_norm"], 1)

            def low(i, u):
                v.wait_ge(s["a_T"], u - 7 if isinstance(i, int) and i < 0 else i * TU + u + 5)
                v.tensor_tensor(target(u, w1_l, w2_l, g.xT_l), ps[:, 6 + u % 2, :].rearrange("p (a b) -> p a b", a=2),
                                target(u, w1_h, w2_h, g.xT_h).bitcast(F32), ALU.subtract).then_inc(s["v_T"], 1)

            def gelu_low(i, b, f):
                n = b * FC + f
                v.wait_ge(s["a_g"], i * B * FC + n + 5)
                v.tensor_tensor(G_l[:, b % 2, f, :], G32[:, n % 4, :], G_h[:, b % 2, f, :].bitcast(F32),
                                ALU.subtract).then_inc(s["v_gl"], 1)

            def residual(i, b):
                v.wait_ge(s["p_out"], i * B + b + 3)
                v.wait_ge(s["g_res"], i * B + b + 1)
                v.wait_ge(s["v_norm"], i * B + b + 1)
                v.tensor_tensor(g.rsum[:, :, :], ps[:, 4:6, :].rearrange("p a (b c) -> p (a b) c", c=D),
                                g.x_a[:, b * RT:(b + 1) * RT, :], ALU.add).then_inc(s["v_sum"], 1)

            def norm(i, b, last):
                v.wait_ge(s["v_sum"], i * B + b + 2)
                if last:
                    v.wait_ge(s[f"x3_in{b // 2}"], 16)
                    kept = (g.w1_raw[:, :, :] if b < 2 else
                            g.w2_raw[:, :, :].rearrange("p a (b d) -> p (a b) d", d=D))
                    chain.step(v.tensor_tensor(g.rsum[:, :, :], g.rsum[:, :, :],
                                               kept[:, b % 2 * RT:(b % 2 + 1) * RT, :], ALU.add))
                    chain.settle()
                if last and b >= 2:
                    v.wait_ge(s[f"y_out{b % 2}"], 16)
                else:
                    v.wait_ge(s["g_hs"], i * B + b + 1)
                layernorm(v, chain, g.lnw, g.rsum, xn[:, b % 2, :, :], s["v_norm"])

            def turn(i, last):
                for f in range(FC):
                    gelu_low(i, 0, f)
                    if f % 2:
                        low(i, f // 2)
                for u in (4, 5):
                    low(i, u)
                for f in range(FC):
                    gelu_low(i, 1, f)
                residual(i, 0)
                norm(i, 0, last)
                for f in range(FC):
                    gelu_low(i, 2, f)
                residual(i, 1)
                if not last:
                    for u in (6, 7):
                        low(i, u)
                norm(i, 1, last)
                for f in range(FC):
                    gelu_low(i, 3, f)
                if not last:
                    for u in (8, 9, 10, 11):
                        low(i, u)
                residual(i, 2)
                if not last:
                    for u in (12, 13):
                        low(i, u)
                norm(i, 2, last)
                residual(i, 3)
                if not last:
                    for u in (14, 15):
                        low(i, u)
                norm(i, 3, last)

            for u in range(8, 12):
                low(-1, u)
            with v.Fori(0, LAST) as i:
                chain.enter(i, 14 * B)
                turn(i, False)
            chain.leave(LAST)
            turn(LAST, True)


def shape_constants():
    q = np.arange(P)
    kmask = np.where(q[:, None] > q[None, :], np.float32(MASKED), np.float32(0))
    qmask = np.zeros((P, S), np.float32)
    qmask[:, S - P:] = kmask.T
    inv_freq = (np.float32(1.0) / np.float32(10000.0) ** (np.arange(0, 4, 2, dtype=np.float32) / np.float32(4)))
    angle = np.arange(S, dtype=np.float32)[:, None] * inv_freq[None, :].astype(np.float32)
    angle = np.concatenate([angle, angle], axis=1)
    sign = np.array([-1, -1, 1, 1], np.float32)
    rope = np.stack([np.cos(angle), np.sin(angle) * sign]).astype(np.float32)
    rope = rope.reshape(2, RT, P, 4).transpose(2, 0, 1, 3)
    heads = (q[:, None] // DH == q[None, :] // DH).astype(np.float32)
    column = (q[:, None] // DH == np.arange(P // DH)[None, :]).astype(np.float32)
    return {"c_ident": np.eye(P, dtype=np.float32), "c_kmask": kmask, "c_qmask": qmask,
            "c_rope": np.ascontiguousarray(rope), "c_blocks": np.concatenate([heads, column], axis=1)}


def kernel(**inputs):
    import concourse.bacc as bacc
    from concourse.bass_utils import run_bass_kernel_spmd

    nc = bacc.Bacc("TRN2", target_bir_lowering=False, num_devices=1)
    arrays, A = {}, {}
    used = {k: v for k, v in inputs.items() if k not in ("L1_attn_cos", "L1_attn_sin")}
    for name, value in {**used, **shape_constants()}.items():
        a = np.ascontiguousarray(value)
        arrays[name] = a
        A[name] = nc.dram_tensor(name, a.shape, mybir.dt.from_np(a.dtype), kind="ExternalInput").ap()
    out = nc.dram_tensor("out", (B, S, D), F32, kind="ExternalOutput").ap()
    build(nc, A, out)
    result = run_bass_kernel_spmd(nc, [arrays], core_ids=[0])
    return result.results[0]["out"]
```

```python
from contextlib import ExitStack

import numpy as np

import concourse.bass as bass
from concourse import mybir

ALU = mybir.AluOpType
ACT = mybir.ActivationFunctionType
AX = mybir.AxisListType
F32 = mybir.dt.float32
F32R = mybir.dt.float32r
I32 = mybir.dt.int32
BF16 = mybir.dt.bfloat16

P = 128
B, S, D = 4, 512, 256
RT = S // P
KC = D // P
NT = B * RT
H, DH = 16, 16
PAIRS = H // 2
SLOT = 64
STAGES = 4
M0 = 1024
MC0 = M0 // P
BLOCKS = 6
HID = 1024
FC = HID // P
EPS = 1e-5
MASKED = -1e30
RSQRT_MAGIC = 0x5F3759DF
ROUND_MAGIC = 1.5 * 2.0 ** 23
TWO_PI = (6.28125, float(np.float32(2 * np.pi - 6.28125)),
          float(2 * np.pi - 6.28125 - np.float64(np.float32(2 * np.pi - 6.28125))))
PI_F32 = float(np.float32(np.pi))


BIAS_COLS = 4 + 2 * MC0 + BLOCKS * FC
STAGE_ORDER = (1, 3, 0, 2)


class Chain:

    def __init__(self, eng, sem):
        self.eng, self.sem, self.base, self.n = eng, sem, 0, 0

    def step(self, instruction):
        instruction.then_inc(self.sem, 1)
        self.n += 1

    def settle(self):
        self.eng.wait_ge(self.sem, self.base + self.n)

    def enter(self, i, per):
        self.outer, self.per = self.base + self.n, per
        self.base, self.n = self.outer + i * per, 0

    def leave(self, times):
        assert self.n == self.per, (self.n, self.per)
        self.base, self.n = self.outer + times * self.per, 0


def bcast(ap, axis, shape):
    return ap.unsqueeze(axis).broadcast_to(shape)


LN_STEPS = 14


def layernorm_steps(v, chain, w, r, xn, done, free=None):
    stats, mv, var, y, t = w["stats"], w["mv"], w["var"], w["y"], w["t"]
    for k in range(RT):
        ins = v.bn_stats(stats[:, k, :], r[:, k, :])
    chain.step(ins)
    yield
    chain.settle()
    v.sem_inc(w["carrier"], 1)
    for k in range(RT):
        ins = v.bn_aggr(mv[:, k, :], stats[:, k, :])
    chain.step(ins)
    yield
    chain.settle()
    chain.step(v.tensor_scalar(var[:, :], mv[:, :, 1], EPS, None, ALU.add))
    yield
    chain.settle()
    chain.step(v.tensor_scalar(t[:, :].bitcast(I32), var[:, :].bitcast(I32), 1, None,
                               ALU.arith_shift_right))
    yield
    chain.settle()
    chain.step(v.tensor_scalar(y[:, :].bitcast(I32), t[:, :].bitcast(I32), -1.0,
                               float(RSQRT_MAGIC), ALU.mult, ALU.add))
    yield
    for _ in range(3):
        chain.settle()
        chain.step(v.tensor_tensor(t[:, :], y[:, :], y[:, :], ALU.mult))
        yield
        chain.settle()
        chain.step(v.scalar_tensor_tensor(t[:, :], t[:, :], -0.5, var[:, :], ALU.mult, ALU.mult))
        yield
        chain.settle()
        chain.step(v.scalar_tensor_tensor(y[:, :], t[:, :], 1.5, y[:, :], ALU.add, ALU.mult))
        yield
    chain.settle()
    if free:
        v.wait_ge(*free)
    for k in range(RT):
        ins = v.tensor_scalar(xn[:, k, :], r[:, k, :], mv[:, k, 0:1], y[:, k:k + 1],
                              ALU.subtract, ALU.mult)
    ins.then_inc(done, 1)


def layernorm(*args):
    for _ in layernorm_steps(*args):
        pass


class Shared:
    pass


def sb(stack, nc, name, shape, dt=F32):
    return stack.enter_context(nc.sbuf_tensor(name, shape, dt))


def sems(stack, nc, names):
    return {n: stack.enter_context(nc.semaphore(n)) for n in names.split()}


def build(nc, A, out):
    g = Shared()
    top = ExitStack()
    with top:
        g.ps = top.enter_context(nc.psum_tensor("ps", [P, 8, 512], F32))
        g.ident = sb(top, nc, "ident", [P, P])
        g.ident_r = sb(top, nc, "ident_r", [P, P], F32R)
        g.xT_h = sb(top, nc, "xT_h", [P, B, KC, S], F32R)
        g.xT_l = sb(top, nc, "xT_l", [P, B, KC, S], F32R)
        g.lnw = {"stats": sb(top, nc, "ln_stats", [P, RT, 6]), "mv": sb(top, nc, "ln_mv", [P, RT, 2]),
                 "var": sb(top, nc, "ln_var", [P, RT]), "y": sb(top, nc, "ln_y", [P, RT]),
                 "t": sb(top, nc, "ln_t", [P, RT])}
        g.carrier = sems(top, nc, "v_carrier a_carrier g_carrier")
        g.lnw["carrier"] = g.carrier["v_carrier"]
        g.xn = sb(top, nc, "xn", [P, 2, RT, D])
        g.hs = sb(top, nc, "hs", [P, 2, RT, D])
        g.rsum = sb(top, nc, "rsum", [P, RT, D])
        g.x_a = sb(top, nc, "x_a", [P, NT, D])
        g.bias_col = sb(top, nc, "bias_col", [P, BIAS_COLS])
        attention0(nc, A, g)
        g.w1_raw = sb(top, nc, "w1_raw", [P, FC, D])
        g.w2_raw = sb(top, nc, "w2_raw", [P, KC, HID])
        g.pre = sems(top, nc, "w1_in w2_in rows_in")
        g.mlp_g = sb(top, nc, "mlp_g", [P, BLOCKS - 1, D])
        g.mlp_b = sb(top, nc, "mlp_b", [P, BLOCKS - 1, D])
        g.mlp_b2 = sb(top, nc, "mlp_b2", [P, BLOCKS, D])
        g.x3_dram = nc.dram_tensor("x3_kept", (B, S, D), F32, kind="Internal").ap()
        with ExitStack() as wl1:
            g.x_b = sb(wl1, nc, "x_b", [P, NT, D])
            g.wq_h = sb(wl1, nc, "wq_h", [P, KC, D], F32R)
            g.wq_l = sb(wl1, nc, "wq_l", [P, KC, D], F32R)
            g.wkv_h = sb(wl1, nc, "wkv_h", [P, KC, 2 * D], F32R)
            g.wkv_l = sb(wl1, nc, "wkv_l", [P, KC, 2 * D], F32R)
            g.wo_h = sb(wl1, nc, "wo_h", [P, KC, D], F32R)
            g.wo_l = sb(wl1, nc, "wo_l", [P, KC, D], F32R)
            with ExitStack() as stage:
                g.stage_w_h = sb(stage, nc, "stage_w_h", [P, STAGES, KC, D], F32R)
                g.stage_w_l = sb(stage, nc, "stage_w_l", [P, STAGES, KC, D], F32R)
                g.stage_c = sb(stage, nc, "stage_c", [P, STAGES, D])
                g.stage_g = sb(stage, nc, "stage_g", [P, STAGES, D])
                g.stage_b = sb(stage, nc, "stage_b", [P, STAGES, D])
                g.gate_h = sb(stage, nc, "gate_h", [P, KC, 2 * D], F32R)
                g.gate_l = sb(stage, nc, "gate_l", [P, KC, 2 * D], F32R)
                prep(nc, A, g)
                gates(nc, A, g)
                stages(nc, A, g)
            attention1(nc, A, g)
        ffn1(nc, A, g, out)


def prep(nc, A, g):
    ps, ident, pre = g.ps, g.ident, g.pre
    stack = ExitStack()
    with stack:
        s = sems(stack, nc, "small_in gate_in l1_in0 l1_in1 l1_in2 l1_in3 ent_in pw_in path_in "
                        "p_bias p_wt p_ent p_prod v_bias v_chain v_m a_split a_ent a_trig "
                        "v_wt v_trig v_prod  a_h v_l")
        raw_gate = sb(stack, nc, "raw_gate", [P, KC, 2 * D])
        raw_l1 = g.hs[:, :, :, :].rearrange("p a (n c) d -> p (a n) c d", c=KC)
        raw_ent = g.xn[:, :, :, :].rearrange("p a b c -> p (a b c)").rearrange("p (c n) -> p c n", c=KC)
        raw_pw = g.w1_raw
        raw_path = sb(stack, nc, "raw_path", [P, 4, KC, D])
        ent_t = g.w2_raw[:, :, :].rearrange("p c n -> p (c n)").rearrange("p (m d) -> p m d", d=D)
        bias_rows = sb(stack, nc, "bias_rows", [4 + 16 + BLOCKS * FC, P])
        phase, turn, sin_half, sin_full = (
            g.x_b[:, 4 * n:4 * n + 4, :].rearrange("p a d -> p (a d)") for n in range(4))
        path_b = sb(stack, nc, "path_b", [P, 4, D])
        ent_pb = sb(stack, nc, "ent_pb", [P, 2, D])
        prod = sb(stack, nc, "prod", [P, KC, D])
        prod2 = sb(stack, nc, "prod2", [P, KC, D])
        rows = bias_rows.shape[0]
        block = stack.enter_context(nc.Block())

        @block.sync
        def _(sp):
            for name, at, n in (("L0_ffn_amp_b", 0, 2), ("L0_ffn_ph_b", 2, 2)):
                sp.dma_start(bias_rows[at:at + n, :],
                             A[name].rearrange("(c p) -> c p", p=P)).then_inc(s["small_in"], 16)
            sp.dma_start(bias_rows[4:20, :],
                         A["L0_ffn_ent_b"].rearrange("l (c p) -> (l c) p", p=P)).then_inc(s["small_in"], 16)
            sp.dma_start(bias_rows[20:rows, :],
                         A["L1_ffn_B1"].rearrange("l (c p) -> (l c) p", p=P)).then_inc(s["small_in"], 16)
            for n, name in enumerate(("L1_attn_Wq", "L1_attn_Wk", "L1_attn_Wv", "L1_attn_Wo")):
                sp.dma_start(raw_l1[:, n, :, :],
                             A[name].rearrange("(c p) n -> p c n", p=P)).then_inc(s[f"l1_in{n}"], 16)
            sp.dma_start(raw_ent[:, :, :],
                         A["L0_ffn_ent_w"][0].rearrange("(c p) n -> p c n", p=P)).then_inc(s["ent_in"], 16)
            sp.dma_start(raw_pw[:, :, :],
                         A["L0_ffn_ent_pw"][0].rearrange("(c p) n -> p c n", p=P)).then_inc(s["pw_in"], 16)
            sp.wait_ge(s["p_ent"], 4)
            sp.dma_start(raw_ent[:, :, :],
                         A["L0_ffn_ent_w"][1].rearrange("(c p) n -> p c n", p=P)).then_inc(s["ent_in"], 16)
            sp.wait_ge(s["p_prod"], 1)
            sp.dma_start(raw_pw[:, :, :],
                         A["L0_ffn_ent_pw"][1].rearrange("(c p) n -> p c n", p=P)).then_inc(s["pw_in"], 16)
            for tile, name in ((g.mlp_g, "L1_ffn_LN_G"), (g.mlp_b, "L1_ffn_LN_B"), (g.mlp_b2, "L1_ffn_B2")):
                sp.dma_start(tile[:, :, :], A[name].unsqueeze(0).broadcast_to([P, *A[name].shape])
                             ).then_inc(pre["rows_in"], 16)
            for n, name in enumerate(("ln3", "ln4")):
                for l in range(2):
                    for which in ("g", "b"):
                        sp.dma_start((g.stage_g if which == "g" else g.stage_b)[:, 2 * l + n, :],
                                     A[f"L0_ffn_{name}_{which}"][l:l + 1, :].broadcast_to([P, D])
                                     ).then_inc(pre["rows_in"], 16)

        @block.scalar
        def _(act):
            act.dma_start(phase, A["L0_ffn_phase"].rearrange("l w d -> (l w d)").unsqueeze(0)
                          .broadcast_to([P, 4 * D])).then_inc(s["path_in"], 16)
            act.dma_start(raw_gate[:, :, 0:D],
                          A["L0_ffn_amp_w"].rearrange("(c p) n -> p c n", p=P)).then_inc(s["gate_in"], 16)
            act.dma_start(raw_gate[:, :, D:2 * D],
                          A["L0_ffn_ph_w"].rearrange("(c p) n -> p c n", p=P)).then_inc(s["gate_in"], 16)
            for n in range(4):
                act.dma_start(raw_path[:, n, :, :], A["L0_ffn_path_w"][n // 2, n % 2]
                              .rearrange("(c p) n -> p c n", p=P)).then_inc(s["path_in"], 16)
            act.dma_start(path_b[:, :, :], A["L0_ffn_path_b"].rearrange("l w d -> (l w) d").unsqueeze(0)
                          .broadcast_to([P, 4, D])).then_inc(s["path_in"], 16)
            act.dma_start(ent_pb[:, :, :], A["L0_ffn_ent_pb"].unsqueeze(0)
                          .broadcast_to([P, 2, D])).then_inc(s["path_in"], 16)
            act.wait_ge(s["gate_in"], 32)
            act.activation(g.gate_h[:, :, :], raw_gate[:, :, :], ACT.Copy).then_inc(s["a_h"], 1)
            for n, (t, lo) in enumerate(((g.wq_h, 0), (g.wkv_h, 0), (g.wkv_h, D), (g.wo_h, 0))):
                act.wait_ge(s["p_wt"], n + 1)
                act.activation(t[:, :, lo:lo + D], ps[:, n, :].rearrange("p (c n) -> p c n", c=KC),
                               ACT.Copy).then_inc(s["a_h"], 1)
            for l in range(2):
                if l:
                    act.wait_ge(s["p_prod"], l)
                for n in range(4):
                    act.wait_ge(s["p_ent"], 4 * l + n + 1)
                    act.activation(ent_t[:, 2 * n:2 * n + 2, :],
                                   ps[:, 4 * (1 - l) + n, :].rearrange("p (c n) -> p c n", c=2),
                                   ACT.Copy).then_inc(s["a_ent"], 1)
            act.wait_ge(s["v_trig"], 1)
            act.activation(sin_half, turn, ACT.Sin, scale=0.5).then_inc(s["a_trig"], 1)
            act.activation(sin_full, turn, ACT.Sin).then_inc(s["a_trig"], 1)
            for n in range(STAGES):
                act.wait_ge(s["v_prod"], n + 1)
                act.activation(g.stage_w_h[:, STAGE_ORDER[n], :, :], (prod, prod2)[n % 2][:, :, :],
                               ACT.Copy).then_inc(s["a_split"], 1)

        @block.tensor
        def _(pe):
            pe.wait_ge(s["small_in"], 64)
            pe.transpose(ps[:, 4, 0:rows], bias_rows[:, :], ident[0:rows, 0:rows]).then_inc(s["p_bias"], 1)
            for n in range(4):
                pe.wait_ge(s[f"l1_in{n}"], 16)
                for c in range(KC):
                    for o in range(KC):
                        mm = pe.transpose(ps[:, n, c * D + o * P:c * D + (o + 1) * P],
                                          raw_l1[:, n, o, c * P:(c + 1) * P], ident[:, :])
                mm.then_inc(s["p_wt"], 1)
            for l in range(2):
                pe.wait_ge(s["ent_in"], 16 * (l + 1))
                if l:
                    pe.wait_ge(s["v_wt"], 4)
                else:
                    pe.wait_ge(s["v_bias"], 1)
                for n in range(4):
                    for j in range(2):
                        for c in range(KC):
                            m = 2 * n + j
                            mm = pe.transpose(ps[:, 4 * (1 - l) + n, j * D + c * P:j * D + (c + 1) * P],
                                              raw_ent[:, c, m * P:(m + 1) * P], ident[:, :])
                    mm.then_inc(s["p_ent"], 1)
                pe.wait_ge(s["pw_in"], 16 * (l + 1))
                pe.wait_ge(s["a_ent"], 4 * (l + 1))
                for c in range(KC):
                    for m in range(MC0):
                        mm = pe.matmul(ps[:, 4 + 2 * l, c * D:(c + 1) * D], ent_t[:, m, c * P:(c + 1) * P],
                                       raw_pw[:, m, :], start=(m == 0), stop=(m == MC0 - 1))
                pe.wait_ge(s["v_bias"], 1)
                for m in range(MC0):
                    col = 4 + l * MC0 + m
                    mm2 = pe.matmul(ps[:, 5 + 2 * l, 0:D], g.bias_col[:, col:col + 1].broadcast_to([P, P]),
                                    raw_pw[:, m, :], start=(m == 0), stop=(m == MC0 - 1))
                mm2.then_inc(s["p_prod"], 1)

        @block.vector
        def _(v):
            chain = Chain(v, s["v_chain"])
            v.wait_ge(s["a_h"], 1)
            v.wait_ge(s["gate_in"], 32)
            v.tensor_tensor(g.gate_l[:, :, :], raw_gate[:, :, :], g.gate_h[:, :, :].bitcast(F32),
                            ALU.subtract).then_inc(s["v_l"], 1)
            v.wait_ge(s["p_bias"], 1)
            v.tensor_copy(g.bias_col[:, :], ps[:, 4, 0:rows]).then_inc(s["v_bias"], 1)
            for n, (low, high, lo) in enumerate(((g.wq_l, g.wq_h, 0), (g.wkv_l, g.wkv_h, 0),
                                                 (g.wkv_l, g.wkv_h, D), (g.wo_l, g.wo_h, 0))):
                v.wait_ge(s["a_h"], 1 + n + 1)
                v.tensor_tensor(low[:, :, lo:lo + D], ps[:, n, :].rearrange("p (c n) -> p c n", c=KC),
                                high[:, :, lo:lo + D].bitcast(F32), ALU.subtract).then_inc(s["v_wt"], 1)
            v.wait_ge(s["path_in"], 16 * 7)
            chain.step(v.tensor_scalar(sin_half, phase, float(1 / (2 * np.pi)), ROUND_MAGIC,
                                       ALU.mult, ALU.add))
            chain.settle()
            chain.step(v.tensor_scalar(sin_full, sin_half, ROUND_MAGIC, None, ALU.subtract))
            chain.settle()
            before = phase
            for c in TWO_PI:
                chain.step(v.scalar_tensor_tensor(turn, sin_full, -c, before,
                                                  ALU.mult, ALU.add))
                chain.settle()
                before = turn
            v.tensor_scalar(turn, turn, PI_F32, -PI_F32, ALU.min, ALU.max).then_inc(s["v_trig"], 1)
            v.wait_ge(s["a_trig"], 2)
            chain.step(v.tensor_tensor(turn, sin_half, sin_half, ALU.mult))
            chain.settle()
            chain.step(v.scalar_tensor_tensor(turn, turn, -2.0, sin_full, ALU.mult, ALU.add))
            chain.settle()
            chain.step(v.tensor_scalar(turn, turn, 1.0, None, ALU.add))
            chain.settle()
            mod = turn.rearrange("p (n d) -> p n d", n=4)
            chain.step(v.tensor_tensor(path_b[:, :, :], path_b[:, :, :], mod, ALU.mult))
            chain.settle()
            for n in range(STAGES):
                dst = (prod, prod2)[n % 2]
                st = STAGE_ORDER[n]
                if n >= 2:
                    v.wait_ge(s["a_split"], n - 1)
                if n < 2:
                    l = n
                    m = [bcast(mod[:, 2 * l + w, :], 1, [P, KC, D]) for w in range(2)]
                    chain.step(v.tensor_tensor(raw_path[:, 2 * l, :, :], raw_path[:, 2 * l, :, :], m[0], ALU.mult))
                    chain.step(v.tensor_tensor(raw_path[:, 2 * l + 1, :, :], raw_path[:, 2 * l + 1, :, :], m[1],
                                               ALU.mult))
                    chain.settle()
                    chain.step(v.tensor_tensor(dst[:, :, :], raw_path[:, 2 * l, :, :],
                                               raw_path[:, 2 * l + 1, :, :], ALU.add))
                    v.tensor_tensor(g.stage_c[:, st, :], path_b[:, 2 * l, :], path_b[:, 2 * l + 1, :], ALU.add)
                else:
                    l = n - 2
                    v.wait_ge(s["p_prod"], l + 1)
                    chain.step(v.tensor_copy(dst[:, :, :],
                                             ps[:, 4 + 2 * l, :].rearrange("p (c n) -> p c n", c=KC)))
                    v.tensor_tensor(g.stage_c[:, st, :], ps[:, 5 + 2 * l, 0:D], ent_pb[:, l, :], ALU.add)
                chain.settle()
                for c in range(KC):
                    ins = v.tensor_tensor(dst[:, c, c * P:(c + 1) * P], dst[:, c, c * P:(c + 1) * P],
                                          ident[:, :], ALU.add)
                    chain.step(ins)
                chain.settle()
                v.sem_inc(s["v_prod"], 1)
                v.wait_ge(s["a_split"], n + 1)
                chain.step(v.tensor_tensor(g.stage_w_l[:, st, :, :], dst[:, :, :],
                                           g.stage_w_h[:, st, :, :].bitcast(F32), ALU.subtract))
            chain.settle()


J_ORDER = (0, 2, 1, 3)
UNIT_AT = ((0, 0, "project", 0), (0, 2, "project", 1), (0, 3, "stack", 0), (1, 0, "project", 2),
           (1, 1, "stack", 1), (1, 2, "project", 3), (1, 3, "stack", 2), (2, 1, "stack", 3))
PREVIOUS = ((2, 2, "att_T", 0), (2, 3, "att_T", 1), (3, 2, "out", 0), (3, 3, "out", 1),
            (6, 2, "next_T", 0), (6, 3, "next_T", 1))
AHEAD = ((3, 0, "x_T", 0), (3, 1, "x_T", 1))


def work_table(when):
    rows = [(p, r, kind, (1, t)) for p, r, kind, t in UNIT_AT]
    if when != "last":
        rows += [(p + 4, r, kind, (0, t)) for p, r, kind, t in UNIT_AT] + list(AHEAD)
    if when != "first":
        rows += PREVIOUS
    return {(p, r): (kind, arg) for p, r, kind, arg in sorted(rows, key=lambda row: row[:2])}


def exchange_list(when):
    table, uses = work_table(when), []
    for p in range(PAIRS):
        for r in range(RT):
            kind, arg = table.get((p, r), (None, None))
            if r == 1 and (p < PAIRS - 1 or when != "last"):
                uses.append(("neg", p + 1))
            if kind == "stack":
                uses.append((kind, arg))
            if r == 2 and p % 2 and (p > 1 or when != "first"):
                uses.append(("group", (p - 3) // 2))
    return uses


class Uses:

    def __init__(self, before, per_entry, after):
        self.before, self.after = before, after
        self.lists = {when: per_entry(when) for when in ("first", "loop", "last")}

    def number(self, i, when, key):
        if when == "before":
            return self.before.index(key) + 1
        if when == "first":
            return len(self.before) + self.lists["first"].index(key) + 1
        start = len(self.before) + len(self.lists["first"])
        if when == "after":
            return start + (B - 2) * len(self.lists["loop"]) + len(self.lists["last"]) + self.after.index(key) + 1
        return (i - 1) * len(self.lists["loop"]) + start + self.lists[when].index(key) + 1


WORK = Uses([("x_T", 0), ("x_T", 1)] + [(kind, (0, t)) for _, _, kind, t in UNIT_AT],
            lambda when: list(work_table(when).values()), [row[2:] for row in PREVIOUS])
EXCHANGE = Uses([("stack", (0, t)) for t in range(RT)] + [("neg", 0)], exchange_list, [("group", -1)])


def attention0(nc, A, g):
    ps, ident, ident_r, xn = g.ps, g.ident, g.ident_r, g.xn
    x_in, x_res = g.hs[:, 0, :, :], g.hs[:, 1, :, :]
    GROUPS = H // 4
    UH = H // 2
    UC = 3 * D // 2
    UP = UH // 2
    COLS = [S - P * i for i in range(RT)]
    OFF = [sum(COLS[:i]) for i in range(RT)]
    stack = ExitStack()
    with stack:
        s = sems(stack, nc, "const_in qkv_in out_in wsplit_h wsplit_l const_v mask_v x_in xres_in g_res g_ones "
                 "p_work v_work p_ex ex_read a_xT a_attT a_nT v_xT g_rope g_chain g_val a_stack v_stack "
                 "p_max v_max v_neg m_row0 m_row1 p_score a_exp p_out a_out v_chain v_norm g_x1")
        wqkv_h = sb(stack, nc, "wqkv_h", [P, KC, 3 * D], F32R)
        wqkv_l = sb(stack, nc, "wqkv_l", [P, KC, 3 * D], F32R)
        wout_h = sb(stack, nc, "wout_h", [P, KC, D], F32R)
        wout_l = sb(stack, nc, "wout_l", [P, KC, D], F32R)
        ident_b = sb(stack, nc, "ident_b", [P, P], BF16)
        mask_b = sb(stack, nc, "mask_b", [P, P], BF16)
        q_mask = sb(stack, nc, "q_mask", [P, S])
        k_mask = sb(stack, nc, "k_mask", [P, P])
        rope = sb(stack, nc, "rope", [P, 2, RT, 4])
        b_qkv = sb(stack, nc, "b_qkv", [P, 3 * D])
        b_out = sb(stack, nc, "b_out", [P, D])
        x_h = sb(stack, nc, "x_h", [P, KC, S], F32R)
        x_l = sb(stack, nc, "x_l", [P, KC, S], F32R)
        att_h = sb(stack, nc, "att_h", [P, KC, S], F32R)
        att_l = sb(stack, nc, "att_l", [P, KC, S], F32R)
        qkv = sb(stack, nc, "qkv", [P, RT, UC])
        turned = sb(stack, nc, "turned", [P, 2, 2 * UH * 4])
        q_stack = sb(stack, nc, "q_stack", [P, UH, SLOT], F32R)
        k_stack = sb(stack, nc, "k_stack", [P, UH, SLOT], F32R)
        qT = sb(stack, nc, "qT", [P, PAIRS, S], F32R)
        kT = sb(stack, nc, "kT", [P, PAIRS, S], F32R)
        val = sb(stack, nc, "val", [P, RT, H, 2 * DH])
        out_T = sb(stack, nc, "out_T", [P, S])
        neg_max = sb(stack, nc, "neg_max", [P, P], F32R)
        top_score = sb(stack, nc, "top_score", [P, 2, 2 * RT])
        neg_rows = sb(stack, nc, "neg_rows", [2 * RT, 2, P], F32R)
        probs = sb(stack, nc, "probs", [P, 2, 2, sum(COLS)])
        inv = sb(stack, nc, "inv", [P, RT, 4])
        att = sb(stack, nc, "att", [P, RT, D])
        flat = probs[:, :, :, :].rearrange("p a b c -> p (a b c)")
        raw_qkv = flat[:, 0:KC * 3 * D].rearrange("p (c n) -> p c n", c=KC)
        raw_out = flat[:, KC * 3 * D:KC * 4 * D].rearrange("p (c n) -> p c n", c=KC)
        x_dram = A["L0_attn_hidden_states"].rearrange("b (t p) d -> p b t d", p=P)
        work, outputs, exchange = ps[:, 5, :], ps[:, 6, :], ps[:, 7, :]
        block = stack.enter_context(nc.Block())

        def tile_number(i, u, t):
            return 2 * RT * (i if u else i + 1) + RT * u + t

        def entries(eng, entry):
            entry(0, "first")
            with eng.Fori(1, B - 1) as i:
                entry(i, "loop")
            entry(B - 1, "last")

        def score_bank(r, o):
            return 2 + (2 * r + o) % 3

        def wait(eng, sem, count):
            if not isinstance(count, int) or count > 0:
                eng.wait_ge(sem, count)

        @block.sync
        def _(sp):
            sp.dma_start(x_in, x_dram[:, 0, :, :]).then_inc(s["x_in"], 16)
            sp.dma_start(ident[:, :], A["c_ident"]).then_inc(s["const_in"], 16)
            sp.dma_start(q_mask[:, :], A["c_qmask"]).then_inc(s["const_in"], 16)
            sp.dma_start(k_mask[:, :], A["c_kmask"]).then_inc(s["const_in"], 16)
            sp.dma_start(rope[:, :, :, :], A["c_rope"]).then_inc(s["const_in"], 16)
            sp.dma_start(b_qkv[:, :], A["L0_attn_b_qkv"].unsqueeze(0).broadcast_to([P, 3 * D])
                         ).then_inc(s["const_in"], 16)
            sp.dma_start(b_out[:, :], A["L0_attn_b_out"].unsqueeze(0).broadcast_to([P, D])
                         ).then_inc(s["const_in"], 16)
            sp.dma_start(x_res, x_dram[:, 0, :, :]).then_inc(s["xres_in"], 16)

            def max_row(i, when, pair):
                sp.wait_ge(s["ex_read"], EXCHANGE.number(i, when, ("neg", pair)) + 1)
                p = pair % PAIRS
                for o in range(2):
                    row = o * SLOT + 3 * DH
                    sp.dma_start(qT[row:row + 1, p, :].bitcast(F32).rearrange("o (t c) -> o t c", t=RT),
                                 neg_rows[o * RT:(o + 1) * RT, p % 2, :].bitcast(F32)
                                 ).then_inc(s[f"m_row{p % 2}"], 16)

            def entry(i, when):
                if when != "last":
                    sp.wait_ge(s["v_xT"], i + 1)
                    sp.dma_start(x_in, x_dram[:, i + 1, :, :]).then_inc(s["x_in"], 16)
                for p in range(PAIRS):
                    if p < PAIRS - 1 or when != "last":
                        max_row(i, when, p + 1)
                    if p == 4 and when != "first":
                        sp.wait_ge(s["v_work"], WORK.number(i, when, ("out", 1)) + 1)
                        sp.dma_start(x_res, x_dram[:, i, :, :]).then_inc(s["xres_in"], 16)

            max_row(-1, "before", 0)
            entries(sp, entry)

        @block.gpsimd
        def _(pool):
            pool.memset(val[:, :, :, DH:2 * DH], 1.0).then_inc(s["g_ones"], 1)
            pool.wait_ge(s["const_in"], 96)
            chain = Chain(pool, s["g_chain"])

            def heads_of(t):
                return qkv[:, t, :].rearrange("p (h c d) -> p h c d", h=UH, c=3)

            def rotate(i, when, u, t):
                n = tile_number(i, u, t)
                pool.wait_ge(s["v_work"], WORK.number(i, when, ("project", (u, t))) + 1)
                wait(pool, s["g_rope"], n)
                r = heads_of(t)[:, :, 0:2, 0:4]
                by_cos = turned[:, 0, :].rearrange("p (h c d) -> p h c d", h=UH, c=2)
                by_sin = turned[:, 1, :].rearrange("p (h c d) -> p h c d", h=UH, c=2)

                def table(w, lo, hi):
                    return rope[:, w, t, lo:hi].unsqueeze(1).unsqueeze(1).broadcast_to([P, UH, 2, hi - lo])

                chain.step(pool.tensor_tensor(by_cos, r, table(0, 0, 4), ALU.mult))
                chain.step(pool.tensor_tensor(by_sin[:, :, :, 0:2], r[:, :, :, 2:4], table(1, 0, 2), ALU.mult))
                chain.step(pool.tensor_tensor(by_sin[:, :, :, 2:4], r[:, :, :, 0:2], table(1, 2, 4), ALU.mult))
                chain.settle()
                pool.tensor_tensor(r, by_cos, by_sin, ALU.add).then_inc(s["g_rope"], 1)

            def values(i, u, t):
                pool.tensor_copy(val[:, t, u * UH:(u + 1) * UH, 0:DH], heads_of(t)[:, :, 2, :]
                                 ).then_inc(s["g_val"], 1)

            def unit(i, when, u):
                rotate(i, when, u, 0)
                rotate(i, when, u, 1)
                wait(pool, s["p_out"], i * PAIRS + (0 if u else UP))
                pool.sem_inc(g.carrier["g_carrier"], 1)
                values(i, u, 0)
                values(i, u, 1)
                rotate(i, when, u, 2)
                values(i, u, 2)
                rotate(i, when, u, 3)
                values(i, u, 3)

            def keep(b):
                pool.wait_ge(s["v_norm"], b + 2)
                pool.sem_inc(g.carrier["g_carrier"], 1)
                pool.tensor_copy(g.x_a[:, bass.ts(b, RT), :], xn[:, 0, :, :]).then_inc(s["g_x1"], 1)

            def residual_bias(b):
                pool.wait_ge(s["xres_in"], 16 * b + 16)
                pool.tensor_tensor(x_res, x_res, bcast(b_out[:, :], 1, [P, RT, D]), ALU.add
                                   ).then_inc(s["g_res"], 1)

            def entry(i, when):
                if when == "loop":
                    chain.enter(i - 1, 2 * RT * 3)
                unit(i, when, 1)
                if when != "last":
                    unit(i, when, 0)
                if when != "first":
                    keep(i - 1)
                    residual_bias(i)
                if when == "loop":
                    chain.leave(B - 2)

            unit(-1, "before", 0)
            residual_bias(0)
            entries(pool, entry)
            keep(B - 1)

        @block.scalar
        def _(act):
            act.dma_start(raw_qkv, A["L0_attn_w_qkv"].rearrange("(c p) n -> p c n", p=P)
                          ).then_inc(s["qkv_in"], 16)
            act.dma_start(raw_out, A["L0_attn_w_out"].rearrange("(c p) n -> p c n", p=P)
                          ).then_inc(s["out_in"], 16)
            act.wait_ge(s["qkv_in"], 16)
            act.activation(wqkv_h[:, :, :], raw_qkv, ACT.Copy).then_inc(s["wsplit_h"], 1)
            act.wait_ge(s["out_in"], 16)
            act.activation(wout_h[:, :, :], raw_out, ACT.Copy).then_inc(s["wsplit_h"], 1)
            act.wait_ge(s["mask_v"], 1)

            def high(i, when, kind, arg):
                act.wait_ge(s["p_work"], WORK.number(i, when, (kind, arg)))
                if kind == "x_T":
                    act.activation(x_h[:, arg, :], work, ACT.Copy).then_inc(s["a_xT"], 1)
                elif kind == "att_T":
                    act.activation(att_h[:, arg, :], work, ACT.Copy).then_inc(s["a_attT"], 1)
                else:
                    act.sem_inc(g.carrier["a_carrier"], 1)
                    act.activation(g.xT_h[:, i - 1, arg, :], work, ACT.Copy).then_inc(s["a_nT"], 1)

            def stack_high(i, u, t):
                act.wait_ge(s["g_rope"], tile_number(i, u, t) + 1)
                heads = qkv[:, t, :].rearrange("p (h c d) -> p h c d", h=UH, c=3)
                act.activation(q_stack[:, :, :].rearrange("p h (n d) -> p h n d", d=DH)[:, :, 0:3:2, :],
                               bcast(heads[:, :, 0, :], 2, [P, UH, 2, DH]), ACT.Copy)
                act.activation(k_stack[:, :, :].rearrange("p h (n d) -> p h n d", d=DH)[:, :, 0:2, :],
                               bcast(heads[:, :, 1, :], 2, [P, UH, 2, DH]), ACT.Copy).then_inc(s["a_stack"], 1)

            def copy_q(i, when, u, t):
                act.wait_ge(s["p_ex"], EXCHANGE.number(i, when, ("stack", (u, t))))
                act.activation(qT[:, u * UP:(u + 1) * UP, t * P:(t + 1) * P],
                               exchange.rearrange("p (b c) -> p b c", c=P), ACT.Copy).then_inc(s["ex_read"], 1)

            def exponentials(i, p, r):
                j = J_ORDER[r]
                for o in range(2):
                    act.wait_ge(s["p_score"], ((i * PAIRS + p) * RT + r) * 2 + o + 1)
                    if r == 0 and o == 0:
                        wait(act, s["p_out"], i * PAIRS + p - 1)
                    act.activation(probs[:, p % 2, o, OFF[j]:OFF[j] + COLS[j]],
                                   ps[:, score_bank(r, o), 0:COLS[j]], ACT.Exp).then_inc(s["a_exp"], 1)

            def copy_outputs(i, when, q, use):
                act.wait_ge(s["p_out"], i * PAIRS + 2 * q + 2)
                act.wait_ge(s["p_ex"], EXCHANGE.number(i, when, use))
                act.activation(out_T[:, :], outputs, ACT.Copy).then_inc(s["a_out"], 1)

            def entry(i, when):
                table = work_table(when)
                before = (None, None)
                for p in range(PAIRS):
                    for r in range(RT):
                        exponentials(i, p, r)
                        if r == RT - 1 and p % 2 == 0 and (p or when != "first"):
                            copy_outputs(i, when, p // 2 - 1, ("neg", p + 1))
                        kind, arg = table.get((p, r), (None, None))
                        if kind == "stack":
                            copy_q(i, when, *arg)
                        elif kind in ("x_T", "att_T", "next_T"):
                            high(i, when, kind, arg)
                        if before[0] == "project":
                            stack_high(i, *before[1])
                        before = (kind, arg)

            for c in range(KC):
                high(-1, "before", "x_T", c)
            for t in range(RT):
                stack_high(-1, 0, t)
                copy_q(-1, "before", 0, t)
            entries(act, entry)
            copy_outputs(B - 1, "last", GROUPS - 1, ("group", GROUPS - 2))
            for kind in ("att_T", "next_T"):
                for c in range(KC):
                    high(B, "after", kind, c)

        @block.tensor
        def _(pe):
            pe.wait_ge(s["const_in"], 96)

            def max_pass(i, p, t, unit_at):
                if p % UP == 0:
                    pe.wait_ge(s["v_work"], WORK.number(*unit_at, ("stack", (p // UP, t))) + 1)
                    pe.wait_ge(s["ex_read"], EXCHANGE.number(*unit_at, ("stack", (p // UP, t))) + 1)
                for o in range(2):
                    n = (i * PAIRS + p) * 2 * RT + 2 * t + o
                    rows = slice(o * SLOT, (o + 1) * SLOT)
                    pe.wait_ge(s["v_max"], n + 1)
                    pe.matmul(ps[:, o, 0:(t + 1) * P], qT[rows, p, t * P:(t + 1) * P],
                              kT[rows, p, 0:(t + 1) * P], start=True, stop=True).then_inc(s["p_max"], 1)

            def score_pass(i, p, r):
                j = J_ORDER[r]
                if r == 0:
                    pe.wait_ge(s[f"m_row{p % 2}"], 32 * (i * (PAIRS // 2) + p // 2 + 1))
                for o in range(2):
                    n, rows = ((i * PAIRS + p) * RT + r) * 2 + o, slice(o * SLOT, (o + 1) * SLOT)
                    wait(pe, s["a_exp"], n - (1 if 2 * r + o < 2 else 2))
                    bank = score_bank(r, o)
                    pe.matmul(ps[:, bank, 0:COLS[j]], kT[rows, p, j * P:(j + 1) * P],
                              qT[rows, p, j * P:S], start=True, stop=False)
                    pe.matmul(ps[:, bank, 0:P], ident_b[:, :], mask_b[:, :], start=False, stop=True
                              ).then_inc(s["p_score"], 1)

            def value_pass(i, p, r):
                j = J_ORDER[r]
                if r == 0 and p % 2 == 0:
                    pe.wait_ge(s["a_out"], i * GROUPS + p // 2 + 1)
                if r == 0 and p % UP == 0:
                    pe.wait_ge(s["g_val"], 2 * RT * i + (p // UP + 1) * RT)
                pe.wait_ge(s["a_exp"], 2 * ((i * PAIRS + p) * RT + r + 1))
                for o in range(2):
                    rows = 2 * DH * (2 * (p % 2) + o)
                    mm = pe.matmul(outputs[rows:rows + 2 * DH, j * P:S], val[:, j, 2 * p + o, :],
                                   probs[:, p % 2, o, OFF[j]:OFF[j] + COLS[j]], start=(r == 0), stop=(r == RT - 1))
                if r == RT - 1:
                    mm.then_inc(s["p_out"], 1)

            def max_rows(i, when, p, pair):
                pe.wait_ge(s["v_neg"], pair + 3)
                pe.wait_ge(s["ex_read"], EXCHANGE.number(i, when, ("neg", p)))
                pe.transpose(exchange[:, 0:P].bitcast(F32R), neg_max[:, :], ident_r[:, :]).then_inc(s["p_ex"], 1)

            def transpose_outputs(i, when, q):
                pe.wait_ge(s["a_out"], i * GROUPS + q + 2)
                pe.wait_ge(s["ex_read"], EXCHANGE.number(i, when, ("group", q if when != "after" else -1)))
                for t in range(RT):
                    mm = pe.transpose(exchange[:, t * P:(t + 1) * P], out_T[:, t * P:(t + 1) * P], ident[:, :])
                mm.then_inc(s["p_ex"], 1)

            def use_work(i, when, kind, arg):
                pe.wait_ge(s["v_work"], WORK.number(i, when, (kind, arg)))
                if kind == "project":
                    u, t = arg
                    n = 0
                    for c in range(KC):
                        for x, w in ((x_h, wqkv_h), (x_h, wqkv_l), (x_l, wqkv_h)):
                            mm = pe.matmul(work[:, 0:UC], x[:, c, t * P:(t + 1) * P],
                                           w[:, c, u * UC:(u + 1) * UC], start=(n == 0), stop=(n == 5))
                            n += 1
                elif kind == "stack":
                    u, t = arg
                    pe.wait_ge(s["v_stack"], tile_number(i, u, t) + 1)
                    for p in range(UP):
                        mm = pe.transpose(work[:, p * P:(p + 1) * P].bitcast(F32R),
                                          k_stack[:, 2 * p:2 * p + 2, :].rearrange("p a b -> p (a b)"), ident_r[:, :])
                elif kind == "out":
                    for t in (2 * arg, 2 * arg + 1):
                        n = 0
                        for c in range(KC):
                            for x, w in ((att_h, wout_h), (att_h, wout_l), (att_l, wout_h)):
                                mm = pe.matmul(work[:, (t % 2) * D:(t % 2 + 1) * D],
                                               x[:, c, t * P:(t + 1) * P], w[:, c, :], start=(n == 0), stop=(n == 5))
                                n += 1
                else:
                    if kind == "x_T":
                        pe.wait_ge(s["x_in"], 16 * (i + 2))
                        src = x_in
                    elif kind == "att_T":
                        pe.wait_ge(s["ex_read"], EXCHANGE.number(i, when, ("group", -1)) + 1)
                        src = att
                    else:
                        pe.wait_ge(s["v_norm"], i + 1)
                        src = xn[:, 0, :, :]
                    for t in range(RT):
                        mm = pe.transpose(work[:, t * P:(t + 1) * P], src[:, t, arg * P:(arg + 1) * P], ident[:, :])
                mm.then_inc(s["p_work"], 1)
                if kind == "stack":
                    pe.wait_ge(s["ex_read"], EXCHANGE.number(i, when, (kind, arg)))
                    for p in range(UP):
                        mm = pe.transpose(exchange[:, p * P:(p + 1) * P].bitcast(F32R),
                                          q_stack[:, 2 * p:2 * p + 2, :].rearrange("p a b -> p (a b)"), ident_r[:, :])
                    mm.then_inc(s["p_ex"], 1)

            def entry(i, when):
                table = work_table(when)
                for p in range(PAIRS):
                    for r in range(RT):
                        if p + 2 < PAIRS:
                            max_pass(i, p + 2, r, (i, when))
                        elif when != "last":
                            max_pass(i + 1, p + 2 - PAIRS, r, (i, when))
                        if r == 1 and (p < PAIRS - 1 or when != "last"):
                            max_rows(i, when, p + 1, i * PAIRS + p + 1)
                        score_pass(i, p, r)
                        if p:
                            value_pass(i, p - 1, r)
                        elif when != "first":
                            value_pass(i - 1, PAIRS - 1, r)
                        if (p, r) in table:
                            use_work(i, when, *table[p, r])
                        if r == 2 and p % 2 and (p > 1 or when != "first"):
                            transpose_outputs(i, when, (p - 3) // 2)

            use_work(-1, "before", "x_T", 0)
            use_work(-1, "before", "x_T", 1)
            pe.wait_ge(s["wsplit_l"], 2)
            pe.wait_ge(s["const_v"], 1)
            pe.wait_ge(s["g_ones"], 1)
            for _, _, kind, t in UNIT_AT:
                use_work(-1, "before", kind, (0, t))
            for p in range(2):
                for t in range(RT):
                    max_pass(0, p, t, (-1, "before"))
                    if p and t == 1:
                        max_rows(-1, "before", 0, 0)
            entries(pe, entry)
            for r in range(RT):
                value_pass(B - 1, PAIRS - 1, r)
            transpose_outputs(B - 1, "after", GROUPS - 1)
            for _, _, kind, arg in PREVIOUS:
                use_work(B, "after", kind, arg)

        @block.vector
        def _(v):
            chain = Chain(v, s["v_chain"])
            for name in ("v_work", "ex_read", "a_out", "v_norm", "g_x1"):
                v.sem_inc(s[name], 1)
            v.sem_inc(s["v_max"], 2)
            v.sem_inc(s["v_neg"], 2)
            v.wait_ge(s["const_in"], 96)
            v.tensor_copy(ident_r[:, :], ident[:, :])
            v.tensor_copy(ident_b[:, :], ident[:, :])
            v.tensor_copy(mask_b[:, :], k_mask[:, :]).then_inc(s["const_v"], 1)
            v.memset(neg_max[:, :].bitcast(F32), 0.0)
            v.memset(q_stack[:, :, 3 * DH:SLOT].bitcast(F32), 0.0)
            chain.step(v.memset(k_stack[:, :, 3 * DH:SLOT].bitcast(F32), 0.0))
            chain.settle()
            v.memset(k_stack[:, :, 3 * DH:3 * DH + 1].bitcast(F32), 1.0).then_inc(s["mask_v"], 1)

            def maximum(i, p, t):
                if t == 0:
                    v.wait_ge(s["v_neg"], i * PAIRS + p + 1)
                for o in range(2):
                    v.wait_ge(s["p_max"], (i * PAIRS + p) * 2 * RT + 2 * t + o + 1)
                    v.sem_inc(g.carrier["v_carrier"], 1)
                    v.tensor_tensor_reduce(
                        ps[:, o, 0:(t + 1) * P], ps[:, o, 0:(t + 1) * P], q_mask[:, S - (t + 1) * P:S],
                        1.0, MASKED, ALU.add, ALU.max,
                        top_score[:, p % 2, o * RT + t:o * RT + t + 1]).then_inc(s["v_max"], 1)

            def negate(i, p):
                v.wait_ge(s["v_max"], (i * PAIRS + p + 1) * 2 * RT + 2)
                v.tensor_scalar(neg_max[:, 0:2 * RT], top_score[:, p % 2, :], -1.0, None,
                                ALU.mult).then_inc(s["v_neg"], 1)

            def take_rows(i, when, key, pair, half):
                v.wait_ge(s["p_ex"], EXCHANGE.number(i, when, ("neg", key)))
                wait(v, s[f"m_row{pair}"], 32 * half)
                v.tensor_copy(neg_rows[:, pair, :], ps[0:2 * RT, 7, 0:P]).then_inc(s["ex_read"], 1)

            def take_outputs(i, when, q):
                v.wait_ge(s["p_ex"], EXCHANGE.number(i, when, ("group", q if when != "after" else -1)))
                o = exchange.rearrange("p (t h d) -> p t h d", t=RT, h=4)
                chain.step(v.reciprocal(inv[:, :, :], o[:, :, :, DH]))
                chain.settle()
                q = q % GROUPS
                v.tensor_tensor(
                    att[:, :, 4 * q * DH:4 * (q + 1) * DH].rearrange("p t (h d) -> p t h d", h=4),
                    o[:, :, :, 0:DH], bcast(inv[:, :, :], 3, [P, RT, 4, DH]), ALU.mult).then_inc(s["ex_read"], 1)

            def low(i, when, kind, c):
                b = i + 1 if kind == "x_T" else i - 1
                v.wait_ge(s[{"x_T": "a_xT", "att_T": "a_attT", "next_T": "a_nT"}[kind]], KC * b + c + 1)
                if kind == "x_T":
                    high, dst = x_h[:, c, :], x_l[:, c, :]
                elif kind == "att_T":
                    high, dst = att_h[:, c, :], att_l[:, c, :]
                else:
                    high, dst = g.xT_h[:, b, c, :], g.xT_l[:, b, c, :]
                v.tensor_tensor(dst, work, high.bitcast(F32), ALU.subtract).then_inc(s["v_work"], 1)
                if kind == "x_T" and c == KC - 1:
                    v.sem_inc(s["v_xT"], 1)

            def stack_low(i, u, t):
                v.wait_ge(s["a_stack"], tile_number(i, u, t) + 1)
                heads = qkv[:, t, :].rearrange("p (h c d) -> p h c d", h=UH, c=3)
                v.tensor_tensor(q_stack[:, :, DH:2 * DH], heads[:, :, 0, :],
                                q_stack[:, :, 0:DH].bitcast(F32), ALU.subtract)
                v.tensor_tensor(k_stack[:, :, 2 * DH:3 * DH], heads[:, :, 1, :],
                                k_stack[:, :, 0:DH].bitcast(F32), ALU.subtract).then_inc(s["v_stack"], 1)

            def take_work(i, when, kind, arg):
                v.wait_ge(s["p_work"], WORK.number(i, when, (kind, arg)))
                if kind == "project":
                    u, t = arg
                    n = tile_number(i, u, t)
                    wait(v, s["v_stack"], n - RT + 1)
                    wait(v, s["g_val"], n - RT + 1)
                    v.tensor_tensor(qkv[:, t, :], work[:, 0:UC], b_qkv[:, u * UC:(u + 1) * UC], ALU.add
                                    ).then_inc(s["v_work"], 1)
                elif kind == "stack":
                    u, t = arg
                    v.tensor_copy(kT[:, u * UP:(u + 1) * UP, t * P:(t + 1) * P],
                                  work.rearrange("p (b c) -> p b c", c=P)).then_inc(s["v_work"], 1)
                else:
                    v.wait_ge(s["g_res"], i)
                    v.wait_ge(s["v_norm"], i)
                    v.tensor_tensor(g.rsum[:, 2 * arg:2 * arg + 2, :], work.rearrange("p (b c) -> p b c", c=D),
                                    x_res[:, 2 * arg:2 * arg + 2, :], ALU.add).then_inc(s["v_work"], 1)

            def normalise(i, when):
                v.wait_ge(s["v_work"], WORK.number(i, when, ("out", 1)) + 1)
                yield from layernorm_steps(v, chain, g.lnw, g.rsum, xn[:, 0, :, :], s["v_norm"],
                                           (s["g_x1"], i))

            def entry(i, when):
                table = work_table(when)
                slots = [(p, r) for p in range(PAIRS) for r in range(RT)]
                norm = iter(())
                steps = GROUPS + LN_STEPS
                if when == "loop":
                    chain.enter(i - 1, steps)
                for n, (p, r) in enumerate(slots):
                    if p + 2 < PAIRS:
                        maximum(i, p + 2, r)
                    elif when != "last":
                        maximum(i + 1, p + 2 - PAIRS, r)
                    if r == 1 and (p < PAIRS - 1 or when != "last"):
                        q = p + 1
                        take_rows(i, when, q, q % 2, i * (PAIRS // 2) + q // 2)
                    kind, arg = table.get(slots[n - 1], (None, None)) if n else (None, None)
                    if kind in ("x_T", "att_T", "next_T"):
                        low(i, when, kind, arg)
                    kind, arg = table.get(slots[n - 2], (None, None)) if n >= 2 else (None, None)
                    if kind == "project":
                        stack_low(i, *arg)
                    kind, arg = table.get((p, r), (None, None))
                    if kind in ("project", "stack", "out"):
                        take_work(i, when, kind, arg)
                    if r == 2 and p % 2 and (p > 1 or when != "first"):
                        take_outputs(i, when, (p - 3) // 2)
                    if r == RT - 1:
                        if p + 2 < PAIRS:
                            negate(i, p + 2)
                        elif when != "last":
                            negate(i + 1, p + 2 - PAIRS)
                    if (p, r) == (4, 0) and when != "first":
                        norm = normalise(i, when)
                    next(norm, None)
                    next(norm, None)
                assert next(norm, None) is None
                if when == "loop":
                    chain.leave(B - 2)

            for c in range(KC):
                low(-1, "before", "x_T", c)
            v.wait_ge(s["wsplit_h"], 1)
            v.tensor_tensor(wqkv_l[:, :, :], raw_qkv, wqkv_h[:, :, :].bitcast(F32),
                            ALU.subtract).then_inc(s["wsplit_l"], 1)
            v.wait_ge(s["wsplit_h"], 2)
            v.tensor_tensor(wout_l[:, :, :], raw_out, wout_h[:, :, :].bitcast(F32),
                            ALU.subtract).then_inc(s["wsplit_l"], 1)
            for n, (_, _, kind, t) in enumerate(UNIT_AT):
                if kind == "stack":
                    stack_low(-1, 0, t)
                take_work(-1, "before", kind, (0, t))
            for p in range(2):
                for t in range(RT):
                    maximum(0, p, t)
                    if p and t == 1:
                        take_rows(-1, "before", 0, 0, 0)
                negate(0, p)
            entries(v, entry)
            take_outputs(B - 1, "after", GROUPS - 1)
            for c in range(KC):
                low(B, "after", "att_T", c)
            for half in range(2):
                take_work(B, "after", "out", half)
            for _ in normalise(B, "after"):
                pass
            for c in range(KC):
                low(B, "after", "next_T", c)
            chain.settle()


def gates(nc, A, g):
    ps = g.ps
    stack = ExitStack()
    with stack:
        s = sems(stack, nc, "p_gate a_gate a_trig v_h v_chain a_hh v_hl")
        amp = sb(stack, nc, "amp", [P, B, KC, S])
        tanh = sb(stack, nc, "tanh", [P, B, KC, S])
        half = g.x_b[:, :, :].rearrange("p (b n) d -> p b (n d)", b=B).rearrange("p b (c s) -> p b c s", c=KC)
        block = stack.enter_context(nc.Block())

        @block.sync
        def _(sp):
            sp.dma_start(g.w1_raw[:, :, :],
                         A["L1_ffn_W1"][0].rearrange("(c p) n -> p c n", p=P)).then_inc(g.pre["w1_in"], 16)
            sp.dma_start(g.w2_raw[:, :, :],
                         A["L1_ffn_W2"][0].rearrange("(c p) n -> p c n", p=P)).then_inc(g.pre["w2_in"], 16)

        @block.tensor
        def _(pe):
            for b in range(B):
                for w in range(2):
                    for m in range(KC):
                        n = (b * 2 + w) * KC + m
                        if n >= 8:
                            pe.wait_ge(s["a_gate"], n - 7)
                        k = 0
                        for c in range(KC):
                            cols = slice(w * D + m * P, w * D + (m + 1) * P)
                            for wt, x in ((g.gate_h, g.xT_h), (g.gate_h, g.xT_l), (g.gate_l, g.xT_h)):
                                mm = pe.matmul(ps[:, n % 8, :], wt[:, c, cols], x[:, b, c, :],
                                               start=(k == 0), stop=(k == 5))
                                k += 1
                        mm.then_inc(s["p_gate"], 1)

        @block.scalar
        def _(act):
            for b in range(B):
                for w, (func, dst) in enumerate(((ACT.Sigmoid, amp), (ACT.Tanh, tanh))):
                    for m in range(KC):
                        n = (b * 2 + w) * KC + m
                        act.wait_ge(s["p_gate"], n + 1)
                        act.activation(dst[:, b, m, :], ps[:, n % 8, :], func,
                                       bias=g.bias_col[:, 2 * w + m:2 * w + m + 1]).then_inc(s["a_gate"], 1)
            for b in range(B):
                act.wait_ge(s["a_gate"], (b + 1) * 4)
                act.activation(half[:, b, :, :], tanh[:, b, :, :], ACT.Sin, scale=PI_F32 / 2
                               ).then_inc(s["a_trig"], 1)
                act.wait_ge(s["a_trig"], 2 * b + 1)
                act.activation(tanh[:, b, :, :], tanh[:, b, :, :], ACT.Sin, scale=PI_F32
                               ).then_inc(s["a_trig"], 1)
            for b in range(B):
                act.wait_ge(s["v_h"], b + 1)
                act.activation(g.xT_h[:, b, :, :], amp[:, b, :, :], ACT.Copy).then_inc(s["a_hh"], 1)

        @block.vector
        def _(v):
            chain = Chain(v, s["v_chain"])
            for b in range(B):
                v.wait_ge(s["a_trig"], 2 * b + 2)
                chain.step(v.tensor_tensor(half[:, b, :, :], half[:, b, :, :], half[:, b, :, :], ALU.mult))
                chain.settle()
                chain.step(v.scalar_tensor_tensor(half[:, b, :, :], half[:, b, :, :], -2.0, tanh[:, b, :, :],
                                                  ALU.mult, ALU.add))
                chain.settle()
                v.scalar_tensor_tensor(amp[:, b, :, :], half[:, b, :, :], 1.0, amp[:, b, :, :],
                                       ALU.add, ALU.mult).then_inc(s["v_h"], 1)
                if b:
                    v.wait_ge(s["a_hh"], b)
                    v.tensor_tensor(g.xT_l[:, b - 1, :, :], amp[:, b - 1, :, :],
                                    g.xT_h[:, b - 1, :, :].bitcast(F32), ALU.subtract).then_inc(s["v_hl"], 1)
            v.wait_ge(s["a_hh"], B)
            v.tensor_tensor(g.xT_l[:, B - 1, :, :], amp[:, B - 1, :, :],
                            g.xT_h[:, B - 1, :, :].bitcast(F32), ALU.subtract).then_inc(s["v_hl"], 1)


def stages(nc, A, g):
    ps, ident, xn, hs = g.ps, g.ident, g.xn, g.hs
    stack = ExitStack()
    with stack:
        s = sems(stack, nc, "p_lin v_sum v_norm g_hs p_T a_th v_tl v_chain g_chain v_norm2 g_x2")
        block = stack.enter_context(nc.Block())


        @block.tensor
        def _(pe):
            def linear(st, b):
                pe.wait_ge(s["v_tl"], st * 2 * B + 2 * (b + 1))
                pe.wait_ge(s["v_sum"], st * B + (4, 2, 3, 5)[b])
                for t in range(RT):
                    n = 0
                    for c in range(KC):
                        for x, w in ((g.xT_h, g.stage_w_h), (g.xT_h, g.stage_w_l), (g.xT_l, g.stage_w_h)):
                            mm = pe.matmul(ps[:, 2 * (b % 3) + t // 2, (t % 2) * D:(t % 2 + 1) * D],
                                           x[:, b, c, t * P:(t + 1) * P], w[:, st, c, :],
                                           start=(n == 0), stop=(n == 5))
                            n += 1
                mm.then_inc(s["p_lin"], 1)

            def transposes(st, b, src, ready, count):
                pe.wait_ge(ready, count)
                pe.wait_ge(s["v_tl"], st * 2 * B + 2 * b + 2 * B)
                for c in range(KC):
                    for t in range(RT):
                        mm = pe.transpose(ps[:, 6 + c, t * P:(t + 1) * P], src[:, b % 2, t, c * P:(c + 1) * P],
                                          ident[:, :])
                    mm.then_inc(s["p_T"], 1)

            with pe.Fori(0, STAGES - 1) as st:
                for b in range(B):
                    linear(st, b)
                for b in range(B):
                    transposes(st, b, hs, s["g_hs"], st * B + b + 3)
            for b in range(B):
                linear(STAGES - 1, b)
            for b in range(B):
                transposes(STAGES - 1, b, xn, s["v_norm2"], b + 1)

        @block.scalar
        def _(act):
            def high(st, b):
                for c in range(KC):
                    act.wait_ge(s["p_T"], st * 2 * B + 2 * b + c + 1 + 4)
                    act.activation(g.xT_h[:, b, c, :], ps[:, 6 + c, :], ACT.Copy).then_inc(s["a_th"], 1)

            with act.Fori(0, STAGES - 1) as st:
                for b in range(B):
                    high(st, b)
            for b in range(B):
                high(STAGES - 1, b)

        @block.gpsimd
        def _(pool):
            chain = Chain(pool, s["g_chain"])
            pool.wait_ge(g.pre["rows_in"], 16 * 11)

            def affine(st, b):
                pool.wait_ge(s["v_norm"], st * B + b + 2)
                pool.sem_inc(g.carrier["g_carrier"], 1)
                chain.step(pool.tensor_tensor(xn[:, b % 2, :, :], xn[:, b % 2, :, :],
                                              bcast(g.stage_g[:, st, :], 1, [P, RT, D]), ALU.mult))
                chain.settle()

            def shift(st, b):
                pool.sem_inc(g.carrier["g_carrier"], 1)
                pool.tensor_tensor(hs[:, b % 2, :, :], xn[:, b % 2, :, :],
                                   bcast(g.stage_b[:, st, :], 1, [P, RT, D]), ALU.add).then_inc(s["g_hs"], 1)

            with pool.Fori(0, STAGES - 1) as st:
                chain.enter(st, B)
                for b in range(B):
                    affine(st, b)
                    pool.wait_ge(s["p_T"], st * 2 * B + 2 * b + 2)
                    shift(st, b)
            chain.leave(STAGES - 1)
            for b in range(B):
                affine(STAGES - 1, b)
                if b < 2:
                    pool.wait_ge(s["p_T"], (STAGES - 1) * 2 * B + 2 * b + 2)
                else:
                    pool.wait_ge(s["v_norm2"], b - 1)
                shift(STAGES - 1, b)
                pool.wait_ge(s["v_norm2"], b + 1)
                pool.tensor_copy(g.x_b[:, b * RT:(b + 1) * RT, :], xn[:, b % 2, :, :]).then_inc(s["g_x2"], 1)

        @block.vector
        def _(v):
            chain = Chain(v, s["v_chain"])
            v.sem_inc(s["v_tl"], 2 * B)
            v.sem_inc(s["v_sum"], B)
            v.sem_inc(s["v_norm"], 1)
            v.sem_inc(s["g_hs"], 2)
            v.sem_inc(s["p_T"], 4)

            def norm(st, b, extra=()):
                v.wait_ge(s["p_lin"], st * B + b + 1)
                bank = 2 * (b % 3)
                v.wait_ge(s["v_norm"], st * B + b + 1)
                chain.step(v.tensor_tensor(g.rsum[:, :, :],
                                           ps[:, bank:bank + 2, :].rearrange("p a (b c) -> p (a b) c", c=D),
                                           bcast(g.stage_c[:, st, :], 1, [P, RT, D]), ALU.add))
                chain.settle()
                v.sem_inc(s["v_sum"], 1)
                v.wait_ge(s["g_hs"], st * B + b + 1)
                for sem, count in extra:
                    v.wait_ge(sem, count)
                layernorm(v, chain, g.lnw, g.rsum, xn[:, b % 2, :, :], s["v_norm"])

            def low(st, b):
                for c in range(KC):
                    v.wait_ge(s["a_th"], st * 2 * B + 2 * b + c + 1)
                    v.tensor_tensor(g.xT_l[:, b, c, :], ps[:, 6 + c, :], g.xT_h[:, b, c, :].bitcast(F32),
                                    ALU.subtract).then_inc(s["v_tl"], 1)

            with v.Fori(0, STAGES - 1) as st:
                chain.enter(st, 15 * B)
                for b in range(B):
                    norm(st, b)
                    if b:
                        low(st, b - 1)
                low(st, B - 1)
            chain.leave(STAGES - 1)
            st = STAGES - 1
            for b in range(B):
                if b:
                    v.wait_ge(s["v_norm2"], b)
                norm(st, b, [(s["g_x2"], b - 1), (s["p_T"], st * 2 * B + 2 * b + 2)] if b >= 2 else [])
                v.wait_ge(s["v_norm"], st * B + b + 2)
                v.wait_ge(s["g_hs"], st * B + b + 3)
                chain.step(v.tensor_tensor(g.rsum[:, :, :], hs[:, b % 2, :, :],
                                           g.x_a[:, b * RT:(b + 1) * RT, :], ALU.add))
                chain.settle()
                layernorm(v, chain, g.lnw, g.rsum, xn[:, b % 2, :, :], s["v_norm2"])
                if b:
                    low(st, b - 1)
            low(st, B - 1)


def attention1(nc, A, g):
    ps, ident, hs = g.ps, g.ident, g.hs
    UNITS = KC + RT
    NUM = P + P // DH
    stack = ExitStack()
    with stack:
        s = sems(stack, nc, "blocks_in g_ones p_unit a_exp a_v v_unit p_kv v_bd p_num v_att v_z "
                 "p_attT a_th v_tl p_proj v_sum v_chain v_norm g_xa x3_out0 x3_out1 p_T a_xh v_xl")
        blocks = sb(stack, nc, "blocks", [P, NUM])
        q = sb(stack, nc, "q", [P, 2, KC, S])
        k = sb(stack, nc, "k", [P, 2, RT, D])
        v1 = sb(stack, nc, "v1", [P, 2, RT, KC, P + 1])
        ex = sb(stack, nc, "ex", [P, 2, S])
        pos = sb(stack, nc, "pos", [P, 2, S])
        bd = sb(stack, nc, "bd", [P, KC, NUM])
        z = sb(stack, nc, "z", [P, 2, KC, P // DH])
        att = sb(stack, nc, "att1", [P, RT, D])
        att_h = sb(stack, nc, "att1_h", [P, KC, S], F32R)
        att_l = sb(stack, nc, "att1_l", [P, KC, S], F32R)
        block = stack.enter_context(nc.Block())

        @block.sync
        def _(sp):
            sp.dma_start(blocks[:, :], A["c_blocks"]).then_inc(s["blocks_in"], 16)
            for b in range(B):
                sp.wait_ge(s["v_norm"], b + 1)
                sp.dma_start(g.x3_dram[b].rearrange("(t p) d -> p t d", p=P), hs[:, b % 2, :, :]
                             ).then_inc(s[f"x3_out{b % 2}"], 16)
            sp.wait_ge(s["x3_out0"], 16 * B // 2)
            sp.wait_ge(s["x3_out1"], 16 * B // 2)

        @block.gpsimd
        def _(pool):
            pool.memset(v1[:, :, :, :, P:P + 1], 1.0).then_inc(s["g_ones"], 1)
            for b in range(B):
                pool.wait_ge(s["v_norm"], b + 1)
                pool.tensor_tensor(g.x_a[:, b * RT:(b + 1) * RT, :], hs[:, b % 2, :, :],
                                   bcast(g.mlp_b2[:, 0, :], 1, [P, RT, D]), ALU.add).then_inc(s["g_xa"], 1)

        @block.tensor
        def _(pe):
            pe.wait_ge(s["g_ones"], 1)

            def unit(b, j):
                n = b * UNITS + j
                if n >= 3:
                    pe.wait_ge(s["a_exp"], n - 2)
                    if (n - 3) % UNITS >= KC:
                        pe.wait_ge(s["a_v"], (n - 3) // UNITS * RT + (n - 3) % UNITS - KC + 1)
                i = 0
                for c in range(KC):
                    if j < KC:
                        cols = slice(j * P, (j + 1) * P)
                        parts = ((g.wq_h[:, c, cols], g.xT_h[:, b, c, :]), (g.wq_h[:, c, cols], g.xT_l[:, b, c, :]),
                                 (g.wq_l[:, c, cols], g.xT_h[:, b, c, :]))
                    else:
                        cols = slice((j - KC) * P, (j - KC + 1) * P)
                        parts = ((g.xT_h[:, b, c, cols], g.wkv_h[:, c, :]), (g.xT_h[:, b, c, cols], g.wkv_l[:, c, :]),
                                 (g.xT_l[:, b, c, cols], g.wkv_h[:, c, :]))
                    for lhsT, rhs in parts:
                        mm = pe.matmul(ps[:, n % 3, :], lhsT, rhs, start=(i == 0), stop=(i == 5))
                        i += 1
                mm.then_inc(s["p_unit"], 1)

            def key_values(b):
                pe.wait_ge(s["v_unit"], (b + 1) * UNITS)
                pe.wait_ge(s["a_v"], (b + 1) * RT)
                if b:
                    pe.wait_ge(s["v_att"], 2 * b)
                for m in range(KC):
                    for t in range(RT):
                        mm = pe.matmul(ps[:, 3, m * D:m * D + P + 1], k[:, b % 2, t, m * P:(m + 1) * P],
                                       v1[:, b % 2, t, m, :], start=(t == 0), stop=(t == RT - 1))
                mm.then_inc(s["p_kv"], 1)

            def numerators(b, half):
                if half == 0:
                    pe.wait_ge(s["v_bd"], b + 1)
                else:
                    pe.wait_ge(s["v_att"], 2 * b + 1)
                for t in (2 * half, 2 * half + 1):
                    for m in range(KC):
                        mm = pe.matmul(ps[:, 3 + t % 2, m * NUM:(m + 1) * NUM], q[:, b % 2, m, t * P:(t + 1) * P],
                                       bd[:, m, :], start=True, stop=True)
                mm.then_inc(s["p_num"], 1)

            def transpose_attention(b):
                pe.wait_ge(s["v_att"], 2 * b + 2)
                if b:
                    pe.wait_ge(s["v_sum"], b)
                for c in range(KC):
                    for t in range(RT):
                        mm = pe.transpose(ps[:, 5 + c, t * P:(t + 1) * P], att[:, t, c * P:(c + 1) * P], ident[:, :])
                    mm.then_inc(s["p_attT"], 1)

            def project(b):
                pe.wait_ge(s["v_tl"], KC * (b + 1))
                for t in range(RT):
                    n = 0
                    for c in range(KC):
                        for x, w in ((att_h, g.wo_h), (att_h, g.wo_l), (att_l, g.wo_h)):
                            mm = pe.matmul(ps[:, 5 + t // 2, (t % 2) * D:(t % 2 + 1) * D],
                                           x[:, c, t * P:(t + 1) * P], w[:, c, :], start=(n == 0), stop=(n == 5))
                            n += 1
                mm.then_inc(s["p_proj"], 1)

            def transpose_next(b, c):
                pe.wait_ge(s["v_norm"], b + 1)
                if b + c:
                    pe.wait_ge(s["v_xl"], KC * b + c)
                for t in range(RT):
                    mm = pe.transpose(ps[:, 7, t * P:(t + 1) * P], hs[:, b % 2, t, c * P:(c + 1) * P], ident[:, :])
                mm.then_inc(s["p_T"], 1)

            for step in range(B + 2):
                if 0 <= step - 2:
                    transpose_attention(step - 2)
                if step < B:
                    for j in range(UNITS):
                        unit(step, j)
                if 0 <= step - 1 < B:
                    key_values(step - 1)
                if 0 <= step - 2:
                    project(step - 2)
                for half in range(2):
                    if 0 <= step - 1 < B:
                        numerators(step - 1, half)
                    if 0 <= step - 3:
                        transpose_next(step - 3, half)

        @block.scalar
        def _(act):
            for step in range(B + 2):
                if 0 <= step - 2:
                    b = step - 2
                    for c in range(KC):
                        act.wait_ge(s["p_attT"], KC * b + c + 1)
                        if b:
                            act.wait_ge(s["p_proj"], b)
                        act.activation(att_h[:, c, :], ps[:, 5 + c, :], ACT.Copy).then_inc(s["a_th"], 1)
                if step < B:
                    b = step
                    for j in range(UNITS):
                        n = b * UNITS + j
                        width = S if j < KC else D
                        act.wait_ge(s["p_unit"], n + 1)
                        if n >= 2:
                            act.wait_ge(s["v_unit"], n - 1)
                        act.activation(ex[:, n % 2, 0:width], ps[:, n % 3, 0:width], ACT.Exp)
                        act.activation(pos[:, n % 2, 0:width], ps[:, n % 3, 0:width], ACT.Relu
                                       ).then_inc(s["a_exp"], 1)
                        if j >= KC:
                            if b >= 2:
                                act.wait_ge(s["p_kv"], b - 1)
                            act.activation(v1[:, b % 2, j - KC, :, 0:P],
                                           ps[:, n % 3, D:2 * D].rearrange("p (m n) -> p m n", m=KC),
                                           ACT.Copy).then_inc(s["a_v"], 1)
                if 0 <= step - 3:
                    b = step - 3
                    for c in range(KC):
                        act.wait_ge(s["p_T"], KC * b + c + 1)
                        act.activation(g.xT_h[:, b, c, :], ps[:, 7, :], ACT.Copy).then_inc(s["a_xh"], 1)

        @block.vector
        def _(v):
            chain = Chain(v, s["v_chain"])
            v.wait_ge(s["blocks_in"], 16)

            def unit(b, j):
                n = b * UNITS + j
                width = S if j < KC else D
                v.wait_ge(s["a_exp"], n + 1)
                if b >= 2:
                    if j < KC:
                        v.wait_ge(s["p_num"], 2 * (b - 1))
                    else:
                        v.wait_ge(s["p_kv"], b - 1)
                dst = q[:, b % 2, j, :] if j < KC else k[:, b % 2, j - KC, :]
                v.scalar_tensor_tensor(dst, ex[:, n % 2, 0:width], 1.0, pos[:, n % 2, 0:width],
                                       ALU.min, ALU.add).then_inc(s["v_unit"], 1)

            def block_diagonal(b):
                v.wait_ge(s["p_kv"], b + 1)
                if b:
                    v.wait_ge(s["p_num"], 2 * b)
                kv = ps[:, 3, :].rearrange("p (m n) -> p m n", m=KC)
                v.tensor_tensor(bd[:, :, 0:P], kv[:, :, 0:P], bcast(blocks[:, 0:P], 1, [P, KC, P]), ALU.mult)
                v.tensor_tensor(bd[:, :, P:NUM], kv[:, :, P:P + 1].broadcast_to([P, KC, NUM - P]),
                                bcast(blocks[:, P:NUM], 1, [P, KC, NUM - P]), ALU.mult).then_inc(s["v_bd"], 1)

            def normalise(b, half):
                v.wait_ge(s["p_num"], 2 * b + half + 1)
                if b + half:
                    v.wait_ge(s["v_att"], 2 * b + half)
                o = ps[:, 3:5, 0:KC * NUM].rearrange("p t (m n) -> p t m n", m=KC)
                v.tensor_scalar(z[:, :, :, :], o[:, :, :, P:NUM], 1e-6, None, ALU.add).then_inc(s["v_z"], 1)
                v.wait_ge(s["v_z"], 2 * (2 * b + half) + 1)
                v.reciprocal(z[:, :, :, :], z[:, :, :, :]).then_inc(s["v_z"], 1)
                v.wait_ge(s["v_z"], 2 * (2 * b + half) + 2)
                if b:
                    v.wait_ge(s["p_attT"], KC * b)
                for i in range(2):
                    ins = v.tensor_tensor(
                        att[:, 2 * half + i, :].rearrange("p (m h d) -> p m h d", m=KC, d=DH),
                        o[:, i, :, 0:P].rearrange("p m (h d) -> p m h d", d=DH),
                        bcast(z[:, i, :, :], 3, [P, KC, P // DH, DH]), ALU.mult)
                ins.then_inc(s["v_att"], 1)

            for step in range(B + 2):
                if 0 <= step - 2:
                    b = step - 2
                    for c in range(KC):
                        v.wait_ge(s["a_th"], KC * b + c + 1)
                        v.tensor_tensor(att_l[:, c, :], ps[:, 5 + c, :], att_h[:, c, :].bitcast(F32),
                                        ALU.subtract).then_inc(s["v_tl"], 1)
                if step < B:
                    for j in range(UNITS):
                        unit(step, j)
                if 0 <= step - 1 < B:
                    block_diagonal(step - 1)
                if 0 <= step - 2:
                    b = step - 2
                    v.wait_ge(s["p_proj"], b + 1)
                    if b:
                        v.wait_ge(s["v_norm"], b)
                    v.tensor_tensor(g.rsum[:, :, :], ps[:, 5:7, :].rearrange("p a (b c) -> p (a b) c", c=D),
                                    g.x_b[:, b * RT:(b + 1) * RT, :], ALU.add).then_inc(s["v_sum"], 1)
                for half in range(2):
                    if 0 <= step - 1 < B:
                        normalise(step - 1, half)
                    if 0 <= step - 3:
                        v.wait_ge(s["a_xh"], KC * (step - 3) + half + 1)
                        v.tensor_tensor(g.xT_l[:, step - 3, half, :], ps[:, 7, :],
                                        g.xT_h[:, step - 3, half, :].bitcast(F32),
                                        ALU.subtract).then_inc(s["v_xl"], 1)
                if 0 <= step - 2:
                    b = step - 2
                    v.wait_ge(s["v_sum"], b + 1)
                    if b >= 2:
                        v.wait_ge(s["p_T"], KC * (b - 1))
                        v.wait_ge(s[f"x3_out{b % 2}"], 16 * (b // 2))
                        v.wait_ge(s["g_xa"], b - 1)
                    layernorm(v, chain, g.lnw, g.rsum, hs[:, b % 2, :, :], s["v_norm"])


def ffn1(nc, A, g, out):
    ps, ident, xn, hs = g.ps, g.ident, g.xn, g.hs
    TU = 16
    stack = ExitStack()
    with stack:
        s = sems(stack, nc, "p_T a_T v_T p_hid a_g v_gl p_out v_sum v_chain v_norm g_chain g_hs g_res "
                 "x3_in0 x3_in1 y_out0 y_out1")
        w1_in, w2_in = g.pre["w1_in"], g.pre["w2_in"]
        w1_h = sb(stack, nc, "w1_h", [P, KC, HID], F32R)
        w1_l = sb(stack, nc, "w1_l", [P, KC, HID], F32R)
        w2_h = sb(stack, nc, "w2_h", [P, FC, D], F32R)
        w2_l = sb(stack, nc, "w2_l", [P, FC, D], F32R)
        G_h = sb(stack, nc, "G_h", [P, 2, FC, S], F32R)
        G_l = sb(stack, nc, "G_l", [P, 2, FC, S], F32R)
        G32 = sb(stack, nc, "G32", [P, 4, S])
        y_dram = out.rearrange("b (t p) d -> p b t d", p=P)
        x3 = g.x3_dram.rearrange("b (t p) d -> p b t d", p=P)
        block = stack.enter_context(nc.Block())
        LAST = BLOCKS - 1

        def target(u, w1, w2, x):
            if u < 4:
                return w2[:, 2 * u:2 * u + 2, :]
            if 8 <= u < 12:
                c, half = divmod(u - 8, 2)
                return w1[:, c, half * S:(half + 1) * S].rearrange("p (a b) -> p a b", a=2)
            b = {4: 3, 6: 0, 12: 1, 14: 2}[u - u % 2]
            return x[:, b, u % 2, :].rearrange("p (a b) -> p a b", a=2)

        @block.sync
        def _(sp):
            def load_w1(k):
                sp.dma_start(g.w1_raw[:, :, :], A["L1_ffn_W1"][k].rearrange("(c p) n -> p c n", p=P)
                             ).then_inc(w1_in, 16)

            def load_w2(k):
                sp.dma_start(g.w2_raw[:, :, :], A["L1_ffn_W2"][k].rearrange("(c p) n -> p c n", p=P)
                             ).then_inc(w2_in, 16)

            sp.wait_ge(s["p_T"], 4)
            load_w1(1)
            with sp.Fori(0, BLOCKS - 2) as i:
                sp.wait_ge(s["p_T"], i * TU + 8)
                load_w2(i + 1)
                sp.wait_ge(s["p_T"], i * TU + 16)
                load_w1(i + 2)
            sp.wait_ge(s["p_T"], (LAST - 1) * TU + 8)
            load_w2(LAST)
            sp.wait_ge(s["p_T"], (LAST - 1) * TU + 16)
            sp.dma_start(g.w1_raw[:, :, :].rearrange("p (b t) d -> p b t d", b=2), x3[:, 0:2, :, :]
                         ).then_inc(s["x3_in0"], 16)
            sp.wait_ge(s["p_T"], LAST * TU + 8)
            sp.dma_start(g.w2_raw[:, :, :].rearrange("p a (b d) -> p a b d", d=D), x3[:, 2:4, :, :]
                         ).then_inc(s["x3_in1"], 16)
            for b in range(B):
                sp.wait_ge(s["v_norm"], LAST * B + b + 2)
                sp.dma_start(y_dram[:, b, :, :], xn[:, b % 2, :, :]).then_inc(s[f"y_out{b % 2}"], 16)
            for b in range(2):
                sp.wait_ge(s[f"y_out{b}"], 16 * B // 2)

        @block.gpsimd
        def _(pool):
            chain = Chain(pool, s["g_chain"])
            pool.sem_inc(s["g_hs"], 2)
            pool.sem_inc(s["g_res"], B)
            with pool.Fori(0, LAST) as i:
                chain.enter(i, B)
                for b in range(B):
                    pool.wait_ge(s["v_norm"], i * B + b + 2)
                    pool.sem_inc(g.carrier["g_carrier"], 1)
                    chain.step(pool.tensor_tensor(xn[:, b % 2, :, :], xn[:, b % 2, :, :],
                                                  bcast(g.mlp_g[:, i, :], 1, [P, RT, D]), ALU.mult))
                    chain.settle()
                    pool.wait_ge(s["p_T"], i * TU + (4, 10, 12, 18)[b])
                    pool.sem_inc(g.carrier["g_carrier"], 1)
                    pool.tensor_tensor(hs[:, b % 2, :, :], xn[:, b % 2, :, :],
                                       bcast(g.mlp_b[:, i, :], 1, [P, RT, D]), ALU.add).then_inc(s["g_hs"], 1)
                    pool.wait_ge(s["g_hs"], i * B + b + 3)
                    pool.sem_inc(g.carrier["g_carrier"], 1)
                    pool.tensor_tensor(g.x_a[:, b * RT:(b + 1) * RT, :], hs[:, b % 2, :, :],
                                       bcast(g.mlp_b2[:, i + 1, :], 1, [P, RT, D]), ALU.add
                                       ).then_inc(s["g_res"], 1)

        @block.tensor
        def _(pe):
            def transpose_unit(i, u):
                first = isinstance(i, int) and i < 0
                number = u - 8 if first else i * TU + 4 + u
                if u in (4, 6, 12, 14):
                    pe.wait_ge(s["g_hs"], i * B + {4: 2, 6: 3, 12: 4, 14: 5}[u])
                elif u == 0:
                    pe.wait_ge(w2_in, (i + 1) * 16)
                elif u == 8:
                    pe.wait_ge(w1_in, 16 if first else (i + 2) * 16)
                if not first or number >= 1:
                    pe.wait_ge(s["v_T"], number)
                for k in range(4):
                    if u < 4:
                        f, c = 2 * u + k // KC, k % KC
                        src = g.w2_raw[:, c, f * P:(f + 1) * P]
                    elif 8 <= u < 12:
                        c, f = (u - 8) // 2, (u - 8) % 2 * 4 + k
                        src = g.w1_raw[:, f, c * P:(c + 1) * P]
                    else:
                        b, c = {4: 3, 6: 0, 12: 1, 14: 2}[u - u % 2], u % 2
                        src = hs[:, b % 2, k, c * P:(c + 1) * P]
                    mm = pe.transpose(ps[:, 6 + u % 2, k * P:(k + 1) * P], src, ident[:, :])
                mm.then_inc(s["p_T"], 1)

            def hidden(i, b, f):
                n = b * FC + f
                pe.wait_ge(s["a_g"], i * B * FC + n + 1)
                k = 0
                for c in range(KC):
                    for w, x in ((w1_h, g.xT_h), (w1_h, g.xT_l), (w1_l, g.xT_h)):
                        mm = pe.matmul(ps[:, n % 4, :], w[:, c, f * P:(f + 1) * P], x[:, b, c, :],
                                       start=(k == 0), stop=(k == 5))
                        k += 1
                mm.then_inc(s["p_hid"], 1)

            def output(i, b, between=()):
                pe.wait_ge(s["v_gl"], i * B * FC + b * FC + 12)
                pe.wait_ge(s["v_sum"], i * B + b + 1)
                for t in range(RT):
                    k = 0
                    for f in range(FC):
                        for x, w in ((G_h, w2_h), (G_h, w2_l), (G_l, w2_h)):
                            mm = pe.matmul(ps[:, 4 + t // 2, (t % 2) * D:(t % 2 + 1) * D],
                                           x[:, b % 2, f, t * P:(t + 1) * P], w[:, f, :],
                                           start=(k == 0), stop=(k == 3 * FC - 1))
                            k += 1
                    if t == RT - 1:
                        mm.then_inc(s["p_out"], 1)
                    if t < len(between):
                        transpose_unit(i, between[t])

            def turn(i, last):
                for f in range(FC):
                    if f == 0:
                        pe.wait_ge(s["v_T"], i * TU + 1)
                    hidden(i, 0, f)
                    if f % 2:
                        transpose_unit(i, f // 2)
                for u in (4, 5):
                    transpose_unit(i, u)
                pe.wait_ge(s["v_T"], i * TU + 3)
                for f in range(FC):
                    hidden(i, 1, f)
                pe.wait_ge(s["v_T"], i * TU + 9)
                output(i, 0)
                for f in range(FC):
                    hidden(i, 2, f)
                output(i, 1)
                if not last:
                    for u in (6, 7):
                        transpose_unit(i, u)
                pe.wait_ge(s["v_T"], i * TU + 11)
                for f in range(FC):
                    hidden(i, 3, f)
                output(i, 2, () if last else (8, 9, 10, 11))
                if not last:
                    for u in (12, 13):
                        transpose_unit(i, u)
                output(i, 3)
                if not last:
                    for u in (14, 15):
                        transpose_unit(i, u)

            for u in range(8, 12):
                transpose_unit(-1, u)
            pe.wait_ge(s["v_T"], 5)
            with pe.Fori(0, LAST) as i:
                turn(i, False)
            turn(LAST, True)

        @block.scalar
        def _(act):
            def high(i, u):
                act.wait_ge(s["p_T"], u - 7 if isinstance(i, int) and i < 0 else i * TU + u + 5)
                act.activation(target(u, w1_h, w2_h, g.xT_h), ps[:, 6 + u % 2, :].rearrange("p (a b) -> p a b", a=2),
                               ACT.Copy).then_inc(s["a_T"], 1)

            def gelu(i, b, f):
                n = b * FC + f
                bias = g.bias_col[:, bass.ds(4 + 2 * MC0 + i * FC + f, 1)]
                act.wait_ge(s["p_hid"], i * B * FC + n + 1)
                act.wait_ge(s["v_gl"], i * B * FC + n + 1)
                if f == 0:
                    act.wait_ge(s["p_out"], i * B + b + 1)
                act.sem_inc(g.carrier["a_carrier"], 1)
                act.activation(G32[:, n % 4, :], ps[:, n % 4, :], ACT.Gelu, bias=bias)
                act.activation(G_h[:, b % 2, f, :], ps[:, n % 4, :], ACT.Gelu, bias=bias).then_inc(s["a_g"], 1)

            def turn(i, last):
                for f in range(FC):
                    gelu(i, 0, f)
                    if f % 2:
                        high(i, f // 2)
                for u in (4, 5):
                    high(i, u)
                for b in (1, 2):
                    for f in range(FC):
                        gelu(i, b, f)
                if not last:
                    for u in (6, 7):
                        high(i, u)
                for f in range(FC):
                    gelu(i, 3, f)
                if not last:
                    for u in range(8, 16):
                        high(i, u)

            for u in range(8, 12):
                high(-1, u)
            with act.Fori(0, LAST) as i:
                turn(i, False)
            turn(LAST, True)

        @block.vector
        def _(v):
            chain = Chain(v, s["v_chain"])
            v.sem_inc(s["v_T"], 1)
            v.sem_inc(s["a_g"], 4)
            v.sem_inc(s["v_gl"], 4)
            v.sem_inc(s["p_out"], 2)
            v.sem_inc(s["v_sum"], 1)
            v.sem_inc(s["v_norm"], 1)

            def low(i, u):
                v.wait_ge(s["a_T"], u - 7 if isinstance(i, int) and i < 0 else i * TU + u + 5)
                v.tensor_tensor(target(u, w1_l, w2_l, g.xT_l), ps[:, 6 + u % 2, :].rearrange("p (a b) -> p a b", a=2),
                                target(u, w1_h, w2_h, g.xT_h).bitcast(F32), ALU.subtract).then_inc(s["v_T"], 1)

            def gelu_low(i, b, f):
                n = b * FC + f
                v.wait_ge(s["a_g"], i * B * FC + n + 5)
                v.tensor_tensor(G_l[:, b % 2, f, :], G32[:, n % 4, :], G_h[:, b % 2, f, :].bitcast(F32),
                                ALU.subtract).then_inc(s["v_gl"], 1)

            def residual(i, b):
                v.wait_ge(s["p_out"], i * B + b + 3)
                v.wait_ge(s["g_res"], i * B + b + 1)
                v.wait_ge(s["v_norm"], i * B + b + 1)
                v.tensor_tensor(g.rsum[:, :, :], ps[:, 4:6, :].rearrange("p a (b c) -> p (a b) c", c=D),
                                g.x_a[:, b * RT:(b + 1) * RT, :], ALU.add).then_inc(s["v_sum"], 1)

            def norm(i, b, last):
                v.wait_ge(s["v_sum"], i * B + b + 2)
                if last:
                    v.wait_ge(s[f"x3_in{b // 2}"], 16)
                    kept = (g.w1_raw[:, :, :] if b < 2 else
                            g.w2_raw[:, :, :].rearrange("p a (b d) -> p (a b) d", d=D))
                    chain.step(v.tensor_tensor(g.rsum[:, :, :], g.rsum[:, :, :],
                                               kept[:, b % 2 * RT:(b % 2 + 1) * RT, :], ALU.add))
                    chain.settle()
                if last and b >= 2:
                    v.wait_ge(s[f"y_out{b % 2}"], 16)
                else:
                    v.wait_ge(s["g_hs"], i * B + b + 1)
                layernorm(v, chain, g.lnw, g.rsum, xn[:, b % 2, :, :], s["v_norm"])

            def turn(i, last):
                for f in range(FC):
                    gelu_low(i, 0, f)
                    if f % 2:
                        low(i, f // 2)
                for u in (4, 5):
                    low(i, u)
                for f in range(FC):
                    gelu_low(i, 1, f)
                residual(i, 0)
                norm(i, 0, last)
                for f in range(FC):
                    gelu_low(i, 2, f)
                residual(i, 1)
                if not last:
                    for u in (6, 7):
                        low(i, u)
                norm(i, 1, last)
                for f in range(FC):
                    gelu_low(i, 3, f)
                if not last:
                    for u in (8, 9, 10, 11):
                        low(i, u)
                residual(i, 2)
                if not last:
                    for u in (12, 13):
                        low(i, u)
                norm(i, 2, last)
                residual(i, 3)
                if not last:
                    for u in (14, 15):
                        low(i, u)
                norm(i, 3, last)

            for u in range(8, 12):
                low(-1, u)
            with v.Fori(0, LAST) as i:
                chain.enter(i, 14 * B)
                turn(i, False)
            chain.leave(LAST)
            turn(LAST, True)


def shape_constants():
    q = np.arange(P)
    kmask = np.where(q[:, None] > q[None, :], np.float32(MASKED), np.float32(0))
    qmask = np.zeros((P, S), np.float32)
    qmask[:, S - P:] = kmask.T
    inv_freq = (np.float32(1.0) / np.float32(10000.0) ** (np.arange(0, 4, 2, dtype=np.float32) / np.float32(4)))
    angle = np.arange(S, dtype=np.float32)[:, None] * inv_freq[None, :].astype(np.float32)
    angle = np.concatenate([angle, angle], axis=1)
    sign = np.array([-1, -1, 1, 1], np.float32)
    rope = np.stack([np.cos(angle), np.sin(angle) * sign]).astype(np.float32)
    rope = rope.reshape(2, RT, P, 4).transpose(2, 0, 1, 3)
    heads = (q[:, None] // DH == q[None, :] // DH).astype(np.float32)
    column = (q[:, None] // DH == np.arange(P // DH)[None, :]).astype(np.float32)
    return {"c_ident": np.eye(P, dtype=np.float32), "c_kmask": kmask, "c_qmask": qmask,
            "c_rope": np.ascontiguousarray(rope), "c_blocks": np.concatenate([heads, column], axis=1)}


def kernel(**inputs):
    import concourse.bacc as bacc
    from concourse.bass_utils import run_bass_kernel_spmd

    nc = bacc.Bacc("TRN2", target_bir_lowering=False, num_devices=1)
    arrays, A = {}, {}
    used = {k: v for k, v in inputs.items() if k not in ("L1_attn_cos", "L1_attn_sin")}
    for name, value in {**used, **shape_constants()}.items():
        a = np.ascontiguousarray(value)
        arrays[name] = a
        A[name] = nc.dram_tensor(name, a.shape, mybir.dt.from_np(a.dtype), kind="ExternalInput").ap()
    out = nc.dram_tensor("out", (B, S, D), F32, kind="ExternalOutput").ap()
    build(nc, A, out)
    result = run_bass_kernel_spmd(nc, [arrays], core_ids=[0])
    return result.results[0]["out"]
```

```python
from contextlib import ExitStack

import numpy as np

import concourse.bass as bass
from concourse import mybir

ALU = mybir.AluOpType
ACT = mybir.ActivationFunctionType
F32 = mybir.dt.float32
F32R = mybir.dt.float32r
I32 = mybir.dt.int32
BF16 = mybir.dt.bfloat16

P = 128
B, S, D = 4, 512, 256
RT = S // P
KC = D // P
NT = B * RT
H, DH = 16, 16
PAIRS = H // 2
SLOT = 64
STAGES = 4
M0 = 1024
MC0 = M0 // P
BLOCKS = 6
HID = 1024
FC = HID // P
EPS = 1e-5
MASKED = -1e30
RSQRT_MAGIC = 0x5F3759DF
ROUND_MAGIC = 1.5 * 2.0 ** 23
TWO_PI = (6.28125, float(np.float32(2 * np.pi - 6.28125)),
          float(2 * np.pi - 6.28125 - np.float64(np.float32(2 * np.pi - 6.28125))))
PI_F32 = float(np.float32(np.pi))

BIAS_COLS = 4 + 2 * MC0 + BLOCKS * FC
STAGE_ORDER = (1, 3, 0, 2)


class Chain:

    def __init__(self, eng, sem):
        self.eng, self.sem, self.base, self.n = eng, sem, 0, 0

    def step(self, instruction):
        instruction.then_inc(self.sem, 1)
        self.n += 1

    def settle(self):
        self.eng.wait_ge(self.sem, self.base + self.n)

    def enter(self, i, per):
        self.outer, self.per = self.base + self.n, per
        self.base, self.n = self.outer + i * per, 0

    def leave(self, times):
        assert self.n == self.per, (self.n, self.per)
        self.base, self.n = self.outer + times * self.per, 0


def bcast(ap, axis, shape):
    return ap.unsqueeze(axis).broadcast_to(shape)


RSTD_STEPS = 14


def rstd_steps(v, chain, w, tiles, y):
    stats, mv, var, t = w["stats"], w["mv"], w["var"], w["t"]
    for k in range(RT):
        ins = v.bn_stats(stats[:, k, :], tiles[k])
    chain.step(ins)
    yield
    chain.settle()
    v.sem_inc(w["carrier"], 1)
    for k in range(RT):
        ins = v.bn_aggr(mv[:, k, :], stats[:, k, :])
    chain.step(ins)
    yield
    chain.settle()
    chain.step(v.tensor_scalar(var[:, :], mv[:, :, 1], EPS, None, ALU.add))
    yield
    chain.settle()
    chain.step(v.tensor_scalar(t[:, :].bitcast(I32), var[:, :].bitcast(I32), 1, None,
                               ALU.arith_shift_right))
    yield
    chain.settle()
    chain.step(v.tensor_scalar(y.bitcast(I32), t[:, :].bitcast(I32), -1.0, float(RSQRT_MAGIC), ALU.mult, ALU.add))
    yield
    for _ in range(3):
        chain.settle()
        chain.step(v.tensor_tensor(t[:, :], y, y, ALU.mult))
        yield
        chain.settle()
        chain.step(v.scalar_tensor_tensor(t[:, :], t[:, :], -0.5, var[:, :], ALU.mult, ALU.mult))
        yield
        chain.settle()
        chain.step(v.scalar_tensor_tensor(y, t[:, :], 1.5, y, ALU.add, ALU.mult))
        yield


def layernorm_steps(v, chain, w, r, xn, done, free=None):
    y = w["y"]
    yield from rstd_steps(v, chain, w, [r[:, k, :] for k in range(RT)], y[:, :])
    chain.settle()
    if free:
        v.wait_ge(*free)
    for k in range(RT):
        ins = v.tensor_scalar(xn[:, k, :], r[:, k, :], w["mv"][:, k, 0:1], y[:, k:k + 1],
                              ALU.subtract, ALU.mult)
    ins.then_inc(done, 1)


def layernorm(*args):
    for _ in layernorm_steps(*args):
        pass


class Shared:
    pass


def sb(stack, nc, name, shape, dt=F32):
    return stack.enter_context(nc.sbuf_tensor(name, shape, dt))


def sems(stack, nc, names):
    return {n: stack.enter_context(nc.semaphore(n)) for n in names.split()}


def build(nc, A, out):
    g = Shared()
    top = ExitStack()
    with top:
        g.ps = top.enter_context(nc.psum_tensor("ps", [P, 8, 512], F32))
        g.ident = sb(top, nc, "ident", [P, P])
        g.ident_r = sb(top, nc, "ident_r", [P, P], F32R)
        g.xT_h = sb(top, nc, "xT_h", [P, B, KC, S], F32R)
        g.xT_l = sb(top, nc, "xT_l", [P, B, KC, S], F32R)
        g.lnw = {"stats": sb(top, nc, "ln_stats", [P, RT, 6]), "mv": sb(top, nc, "ln_mv", [P, RT, 2]),
                 "var": sb(top, nc, "ln_var", [P, RT]), "y": sb(top, nc, "ln_y", [P, RT]),
                 "t": sb(top, nc, "ln_t", [P, RT])}
        g.carrier = sems(top, nc, "v_carrier a_carrier g_carrier")
        g.lnw["carrier"] = g.carrier["v_carrier"]
        g.xn = sb(top, nc, "xn", [P, 2, RT, D])
        g.hs = sb(top, nc, "hs", [P, 2, RT, D])
        g.rsum = sb(top, nc, "rsum", [P, RT, D])
        g.x_a = sb(top, nc, "x_a", [P, NT, D])
        g.bias_col = sb(top, nc, "bias_col", [P, BIAS_COLS])
        g.w1_raw = sb(top, nc, "w1_raw", [P, KC, HID])
        g.w2_raw = sb(top, nc, "w2_raw", [P, FC, D])
        g.pre = sems(top, nc, "w1_in w2_in rows_in")
        attention0(nc, A, g)
        g.w1_h = sb(top, nc, "w1_h", [P, KC, HID], F32R)
        g.w1_l = sb(top, nc, "w1_l", [P, KC, HID], F32R)
        g.mlp_g = sb(top, nc, "mlp_g", [P, BLOCKS - 1, D])
        g.mlp_b = sb(top, nc, "mlp_b", [P, BLOCKS - 1, D])
        g.mlp_b2 = sb(top, nc, "mlp_b2", [P, BLOCKS, D])
        g.x3_dram = nc.dram_tensor("x3_kept", (B, S, D), F32, kind="Internal").ap()
        with ExitStack() as wl1:
            g.x_b = sb(wl1, nc, "x_b", [P, NT, D])
            g.wq_h = sb(wl1, nc, "wq_h", [P, KC, D], F32R)
            g.wq_l = sb(wl1, nc, "wq_l", [P, KC, D], F32R)
            g.wkv_h = sb(wl1, nc, "wkv_h", [P, KC, 2 * D], F32R)
            g.wkv_l = sb(wl1, nc, "wkv_l", [P, KC, 2 * D], F32R)
            g.wo_h = sb(wl1, nc, "wo_h", [P, KC, D], F32R)
            g.wo_l = sb(wl1, nc, "wo_l", [P, KC, D], F32R)
            with ExitStack() as stage:
                g.stage_w_h, g.stage_w_l = (
                    w[:, :, :].rearrange("p a (s d) -> p (a s) d", d=D).rearrange("p (s c) d -> p s c d", c=KC)
                    for w in (g.w1_h, g.w1_l))
                g.stage_c_h = sb(stage, nc, "stage_c_h", [P, STAGES, D], F32R)
                g.stage_c_l = sb(stage, nc, "stage_c_l", [P, STAGES, D], F32R)
                g.first_row = sb(stage, nc, "first_row", [P, P], F32R)
                g.stage_g = sb(stage, nc, "stage_g", [P, STAGES, D])
                g.stage_b = sb(stage, nc, "stage_b", [P, STAGES, D])
                g.gate_h = sb(stage, nc, "gate_h", [P, KC, 2 * D], F32R)
                g.gate_l = sb(stage, nc, "gate_l", [P, KC, 2 * D], F32R)
                prep(nc, A, g)
                wave_ffn(nc, A, g)
            attention1(nc, A, g)
        ffn1(nc, A, g, out)


def prep(nc, A, g):
    ps, ident, pre = g.ps, g.ident, g.pre
    stack = ExitStack()
    with stack:
        s = sems(stack, nc, "small_in gate_in l1_in ent_in path_in phase_in "
                        "p_bias p_prod v_bias v_chain a_split a_trig "
                        "v_trig v_prod v_c g_zero a_h v_l")
        raw_gate = sb(stack, nc, "raw_gate", [P, KC, 2 * D])
        raw_l1 = g.hs[:, :, :, :].rearrange("p a (n c) d -> p (a n) c d", c=KC)
        ent_t = (g.w2_raw, g.xn[:, :, :, :].rearrange("p a t d -> p (a t) d"))
        raw_pw = (g.w1_raw[:, :, :].rearrange("p c (m d) -> p (c m) d", d=D), sb(stack, nc, "raw_pw1", [P, MC0, D]))
        raw_path = sb(stack, nc, "raw_path", [P, 4, KC, D])
        bias_rows = sb(stack, nc, "bias_rows", [4 + 16 + BLOCKS * FC, P])
        phase, turn, sin_half, sin_full = (
            g.x_b[:, 4 * n:4 * n + 4, :].rearrange("p a d -> p (a d)") for n in range(4))
        path_b = sb(stack, nc, "path_b", [P, 4, D])
        ent_pb = sb(stack, nc, "ent_pb", [P, 2, D])
        stage_c = sb(stack, nc, "stage_c", [P, STAGES, D])
        prod, prod2 = g.rsum[:, 0:KC, :], g.rsum[:, KC:2 * KC, :]
        rows = bias_rows.shape[0]
        L1_SPLIT = (((g.wq_h, g.wq_l), 0), ((g.wkv_h, g.wkv_l), 0), ((g.wkv_h, g.wkv_l), D), ((g.wo_h, g.wo_l), 0))
        block = stack.enter_context(nc.Block())

        @block.sync
        def _(sp):
            for name, at, n in (("L0_ffn_amp_b", 0, 2), ("L0_ffn_ph_b", 2, 2)):
                sp.dma_start(bias_rows[at:at + n, :],
                             A[name].rearrange("(c p) -> c p", p=P)).then_inc(s["small_in"], 16)
            sp.dma_start(bias_rows[4:20, :],
                         A["L0_ffn_ent_b"].rearrange("l (c p) -> (l c) p", p=P)).then_inc(s["small_in"], 16)
            sp.dma_start(bias_rows[20:rows, :],
                         A["L1_ffn_B1"].rearrange("l (c p) -> (l c) p", p=P)).then_inc(s["small_in"], 16)
            sp.dma_start(ent_t[1][:, :, :], A["L0_ffn_ent_w_T"][1].rearrange("(c p) n -> p c n", p=P)
                         ).then_inc(s["ent_in"], 16)
            sp.dma_start(raw_pw[1][:, :, :], A["L0_ffn_ent_pw"][1].rearrange("(c p) n -> p c n", p=P)
                         ).then_inc(s["ent_in"], 16)
            for n, name in enumerate(("L1_attn_Wq", "L1_attn_Wk", "L1_attn_Wv", "L1_attn_Wo")):
                sp.dma_start(raw_l1[:, n, :, :],
                             A[name + "_T"].rearrange("(c p) n -> p c n", p=P)).then_inc(s["l1_in"], 16)
            for tile, name in ((g.mlp_g, "L1_ffn_LN_G"), (g.mlp_b, "L1_ffn_LN_B"), (g.mlp_b2, "L1_ffn_B2")):
                sp.dma_start(tile[:, :, :], A[name].unsqueeze(0).broadcast_to([P, *A[name].shape])
                             ).then_inc(pre["rows_in"], 16)
            for n, name in enumerate(("ln3", "ln4")):
                for l in range(2):
                    for which in ("g", "b"):
                        sp.dma_start((g.stage_g if which == "g" else g.stage_b)[:, 2 * l + n, :],
                                     A[f"L0_ffn_{name}_{which}"][l:l + 1, :].broadcast_to([P, D])
                                     ).then_inc(pre["rows_in"], 16)

        @block.scalar
        def _(act):
            act.dma_start(phase, A["L0_ffn_phase"].rearrange("l w d -> (l w d)").unsqueeze(0)
                          .broadcast_to([P, 4 * D])).then_inc(s["phase_in"], 16)
            act.dma_start(raw_gate[:, :, 0:D],
                          A["L0_ffn_amp_w"].rearrange("(c p) n -> p c n", p=P)).then_inc(s["gate_in"], 16)
            act.dma_start(raw_gate[:, :, D:2 * D],
                          A["L0_ffn_ph_w"].rearrange("(c p) n -> p c n", p=P)).then_inc(s["gate_in"], 16)
            for n in range(4):
                act.dma_start(raw_path[:, n, :, :], A["L0_ffn_path_w"][n // 2, n % 2]
                              .rearrange("(c p) n -> p c n", p=P)).then_inc(s["path_in"], 16)
            act.dma_start(path_b[:, :, :], A["L0_ffn_path_b"].rearrange("l w d -> (l w) d").unsqueeze(0)
                          .broadcast_to([P, 4, D])).then_inc(s["path_in"], 16)
            act.dma_start(ent_pb[:, :, :], A["L0_ffn_ent_pb"].unsqueeze(0)
                          .broadcast_to([P, 2, D])).then_inc(s["path_in"], 16)
            act.wait_ge(s["gate_in"], 32)
            act.activation(g.gate_h[:, :, :], raw_gate[:, :, :], ACT.Copy).then_inc(s["a_h"], 1)
            act.wait_ge(s["v_trig"], 1)
            act.activation(sin_half, turn, ACT.Sin, scale=0.5).then_inc(s["a_trig"], 1)
            act.activation(sin_full, turn, ACT.Sin).then_inc(s["a_trig"], 1)
            for n in range(STAGES):
                if n == 2:
                    act.wait_ge(s["l1_in"], 64)
                    for k, (t, lo) in enumerate(L1_SPLIT):
                        act.activation(t[0][:, :, lo:lo + D], raw_l1[:, k, :, :], ACT.Copy).then_inc(s["a_h"], 1)
                act.wait_ge(s["v_prod"], n + 1)
                act.activation(g.stage_w_h[:, STAGE_ORDER[n], :, :], (prod, prod2)[n % 2][:, :, :],
                               ACT.Copy).then_inc(s["a_split"], 1)
            act.wait_ge(s["v_c"], 1)
            act.activation(g.stage_c_h[:, :, :], stage_c[:, :, :], ACT.Copy).then_inc(s["a_split"], 1)

        @block.gpsimd
        def _(pool):
            pool.memset(g.first_row[:, :].bitcast(F32), 0.0).then_inc(s["g_zero"], 1)
            pool.wait_ge(s["g_zero"], 1)
            pool.memset(g.first_row[0:1, :].bitcast(F32), 1.0).then_inc(s["g_zero"], 1)

        @block.tensor
        def _(pe):
            for l in range(2):
                if l:
                    pe.wait_ge(s["ent_in"], 32)
                else:
                    pe.wait_ge(pre["w1_in"], 16)
                    pe.wait_ge(pre["w2_in"], 16)
                for c in range(KC):
                    for m in range(MC0):
                        pe.matmul(ps[:, 4 + 2 * l, c * D:(c + 1) * D], ent_t[l][:, m, c * P:(c + 1) * P],
                                  raw_pw[l][:, m, :], start=(m == 0), stop=(m == MC0 - 1))
                if l == 0:
                    pe.wait_ge(s["small_in"], 64)
                    pe.transpose(ps[:, 0, 0:rows], bias_rows[:, :], ident[0:rows, 0:rows]).then_inc(s["p_bias"], 1)
                    pe.wait_ge(s["v_bias"], 1)
                for m in range(MC0):
                    col = 4 + l * MC0 + m
                    mm = pe.matmul(ps[:, 5 + 2 * l, 0:D], g.bias_col[:, col:col + 1].broadcast_to([P, P]),
                                   raw_pw[l][:, m, :], start=(m == 0), stop=(m == MC0 - 1))
                mm.then_inc(s["p_prod"], 1)

        @block.vector
        def _(v):
            chain = Chain(v, s["v_chain"])
            v.wait_ge(s["phase_in"], 16)
            chain.step(v.tensor_scalar(sin_half, phase, float(1 / (2 * np.pi)), ROUND_MAGIC,
                                       ALU.mult, ALU.add))
            chain.settle()
            chain.step(v.tensor_scalar(sin_full, sin_half, ROUND_MAGIC, None, ALU.subtract))
            chain.settle()
            before = phase
            for c in TWO_PI:
                chain.step(v.scalar_tensor_tensor(turn, sin_full, -c, before,
                                                  ALU.mult, ALU.add))
                chain.settle()
                before = turn
            v.tensor_scalar(turn, turn, PI_F32, -PI_F32, ALU.min, ALU.max).then_inc(s["v_trig"], 1)
            v.wait_ge(s["a_h"], 1)
            v.wait_ge(s["gate_in"], 32)
            v.tensor_tensor(g.gate_l[:, :, :], raw_gate[:, :, :], g.gate_h[:, :, :].bitcast(F32),
                            ALU.subtract).then_inc(s["v_l"], 1)
            v.wait_ge(s["p_bias"], 1)
            v.tensor_copy(g.bias_col[:, :], ps[:, 0, 0:rows]).then_inc(s["v_bias"], 1)
            v.wait_ge(s["a_trig"], 2)
            chain.step(v.tensor_tensor(turn, sin_half, sin_half, ALU.mult))
            chain.settle()
            chain.step(v.scalar_tensor_tensor(turn, turn, -2.0, sin_full, ALU.mult, ALU.add))
            chain.settle()
            chain.step(v.tensor_scalar(turn, turn, 1.0, None, ALU.add))
            chain.settle()
            mod = turn.rearrange("p (n d) -> p n d", n=4)
            v.wait_ge(s["path_in"], 16 * 6)
            chain.step(v.tensor_tensor(path_b[:, :, :], path_b[:, :, :], mod, ALU.mult))
            chain.settle()
            for n in range(STAGES):
                dst = (prod, prod2)[n % 2]
                st = STAGE_ORDER[n]
                if n >= 2:
                    v.wait_ge(s["a_split"], n - 1)
                if n < 2:
                    l = n
                    m = [bcast(mod[:, 2 * l + w, :], 1, [P, KC, D]) for w in range(2)]
                    chain.step(v.tensor_tensor(raw_path[:, 2 * l, :, :], raw_path[:, 2 * l, :, :], m[0], ALU.mult))
                    chain.step(v.tensor_tensor(raw_path[:, 2 * l + 1, :, :], raw_path[:, 2 * l + 1, :, :], m[1],
                                               ALU.mult))
                    chain.settle()
                    chain.step(v.tensor_tensor(dst[:, :, :], raw_path[:, 2 * l, :, :],
                                               raw_path[:, 2 * l + 1, :, :], ALU.add))
                    v.tensor_tensor(stage_c[:, st, :], path_b[:, 2 * l, :], path_b[:, 2 * l + 1, :], ALU.add)
                else:
                    l = n - 2
                    if l == 0:
                        for k, ((high, low), lo) in enumerate(L1_SPLIT):
                            v.wait_ge(s["a_h"], 1 + k + 1)
                            v.tensor_tensor(low[:, :, lo:lo + D], raw_l1[:, k, :, :], high[:, :, lo:lo + D].bitcast(F32),
                                            ALU.subtract).then_inc(s["v_l"], 1)
                    v.wait_ge(s["p_prod"], l + 1)
                    chain.step(v.tensor_copy(dst[:, :, :],
                                             ps[:, 4 + 2 * l, :].rearrange("p (c n) -> p c n", c=KC)))
                    v.tensor_tensor(stage_c[:, st, :], ps[:, 5 + 2 * l, 0:D], ent_pb[:, l, :], ALU.add)
                chain.settle()
                for c in range(KC):
                    ins = v.tensor_tensor(dst[:, c, c * P:(c + 1) * P], dst[:, c, c * P:(c + 1) * P],
                                          ident[:, :], ALU.add)
                    chain.step(ins)
                chain.settle()
                v.sem_inc(s["v_prod"], 1)
                v.wait_ge(s["a_split"], n + 1)
                chain.step(v.tensor_tensor(g.stage_w_l[:, st, :, :], dst[:, :, :],
                                           g.stage_w_h[:, st, :, :].bitcast(F32), ALU.subtract))
            chain.settle()
            v.sem_inc(s["v_c"], 1)
            v.wait_ge(s["a_split"], STAGES + 1)
            v.tensor_tensor(g.stage_c_l[:, :, :], stage_c[:, :, :], g.stage_c_h[:, :, :].bitcast(F32),
                            ALU.subtract).then_inc(s["v_l"], 1)


J_ORDER = (0, 3, 1, 2)
UNIT_AT = ((0, 0, "project", 0), (0, 2, "project", 1), (0, 3, "stack", 0), (1, 0, "project", 2),
           (1, 1, "stack", 1), (1, 2, "project", 3), (1, 3, "stack", 2), (2, 1, "stack", 3))
PREVIOUS = ((2, 2, "att_T", 0), (2, 3, "att_T", 1), (3, 2, "out", 0), (3, 3, "out", 1),
            (6, 2, "next_T", 0), (6, 3, "next_T", 1))
AHEAD = ((3, 0, "x_T", 0), (3, 1, "x_T", 1))


def work_table(when):
    rows = [(p, r, kind, (1, t)) for p, r, kind, t in UNIT_AT]
    if when != "last":
        rows += [(p + 4, r, kind, (0, t)) for p, r, kind, t in UNIT_AT] + list(AHEAD)
    if when != "first":
        rows += PREVIOUS
    return {(p, r): (kind, arg) for p, r, kind, arg in sorted(rows, key=lambda row: row[:2])}


def exchange_list(when):
    table, uses = work_table(when), []
    for p in range(PAIRS):
        for r in range(RT):
            kind, arg = table.get((p, r), (None, None))
            if r == 1 and (p < PAIRS - 1 or when != "last"):
                uses.append(("neg", p + 1))
            if kind == "stack":
                uses.append((kind, arg))
            if r == 2 and p % 2 and (p > 1 or when != "first"):
                uses.append(("group", (p - 3) // 2))
    return uses


class Uses:

    def __init__(self, before, per_entry, after):
        self.before, self.after = before, after
        self.lists = {when: per_entry(when) for when in ("first", "loop", "last")}

    def number(self, i, when, key):
        if when == "before":
            return self.before.index(key) + 1
        if when == "first":
            return len(self.before) + self.lists["first"].index(key) + 1
        start = len(self.before) + len(self.lists["first"])
        if when == "after":
            return start + (B - 2) * len(self.lists["loop"]) + len(self.lists["last"]) + self.after.index(key) + 1
        return (i - 1) * len(self.lists["loop"]) + start + self.lists[when].index(key) + 1


WORK = Uses([("x_T", 0), ("x_T", 1)] + [(kind, (0, t)) for _, _, kind, t in UNIT_AT],
            lambda when: list(work_table(when).values()), [row[2:] for row in PREVIOUS])
EXCHANGE = Uses([("stack", (0, t)) for t in range(RT)] + [("neg", 0)], exchange_list, [("group", -1)])


def attention0(nc, A, g):
    ps, ident, ident_r, xn = g.ps, g.ident, g.ident_r, g.xn
    x_in, x_res = g.hs[:, 0, :, :], g.hs[:, 1, :, :]
    GROUPS = H // 4
    UH = H // 2
    UC = 3 * D // 2
    UP = UH // 2
    COLS = [S - P * i for i in range(RT)]
    OFF = [sum(COLS[:i]) for i in range(RT)]
    stack = ExitStack()
    with stack:
        s = sems(stack, nc, "const_in qkv_in out_in wsplit_h wsplit_l const_v mask_v x_in xres_in g_res g_ones "
                 "p_work v_work p_ex ex_read a_xT a_attT a_nT v_xT g_rope g_chain g_val a_stack v_stack "
                 "p_max v_max v_neg m_row0 m_row1 p_score a_exp p_out a_out v_chain v_norm g_x1")
        wqkv_h = sb(stack, nc, "wqkv_h", [P, KC, 3 * D], F32R)
        wqkv_l = sb(stack, nc, "wqkv_l", [P, KC, 3 * D], F32R)
        wout_h = sb(stack, nc, "wout_h", [P, KC, D], F32R)
        wout_l = sb(stack, nc, "wout_l", [P, KC, D], F32R)
        ident_b = sb(stack, nc, "ident_b", [P, P], BF16)
        mask_b = sb(stack, nc, "mask_b", [P, P], BF16)
        q_mask = sb(stack, nc, "q_mask", [P, S])
        k_mask = sb(stack, nc, "k_mask", [P, P])
        rope = sb(stack, nc, "rope", [P, 2, RT, 4])
        b_qkv = sb(stack, nc, "b_qkv", [P, 3 * D])
        b_out = sb(stack, nc, "b_out", [P, D])
        x_h = sb(stack, nc, "x_h", [P, KC, S], F32R)
        x_l = sb(stack, nc, "x_l", [P, KC, S], F32R)
        att_h = sb(stack, nc, "att_h", [P, KC, S], F32R)
        att_l = sb(stack, nc, "att_l", [P, KC, S], F32R)
        qkv = sb(stack, nc, "qkv", [P, RT, UC])
        turned = sb(stack, nc, "turned", [P, 2, 2 * UH * 4])
        q_stack = sb(stack, nc, "q_stack", [P, UH, SLOT], F32R)
        k_stack = sb(stack, nc, "k_stack", [P, UH, SLOT], F32R)
        qT = sb(stack, nc, "qT", [P, PAIRS, S], F32R)
        kT = sb(stack, nc, "kT", [P, PAIRS, S], F32R)
        val = sb(stack, nc, "val", [P, RT, H, 2 * DH])
        out_T = sb(stack, nc, "out_T", [P, S])
        neg_max = sb(stack, nc, "neg_max", [P, P], F32R)
        top_score = sb(stack, nc, "top_score", [P, 2, 2 * RT])
        neg_rows = sb(stack, nc, "neg_rows", [2 * RT, 2, P], F32R)
        probs = sb(stack, nc, "probs", [P, 2, 2, sum(COLS)])
        inv = sb(stack, nc, "inv", [P, RT, 4])
        att = sb(stack, nc, "att", [P, RT, D])
        flat = probs[:, :, :, :].rearrange("p a b c -> p (a b c)")
        raw_qkv = flat[:, 0:KC * 3 * D].rearrange("p (c n) -> p c n", c=KC)
        raw_out = flat[:, KC * 3 * D:KC * 4 * D].rearrange("p (c n) -> p c n", c=KC)
        x_dram = A["L0_attn_hidden_states"].rearrange("b (t p) d -> p b t d", p=P)
        work, outputs, exchange = ps[:, 5, :], ps[:, 6, :], ps[:, 7, :]
        block = stack.enter_context(nc.Block())

        def tile_number(i, u, t):
            return 2 * RT * (i if u else i + 1) + RT * u + t

        def entries(eng, entry):
            entry(0, "first")
            with eng.Fori(1, B - 1) as i:
                entry(i, "loop")
            entry(B - 1, "last")

        def score_bank(r, o):
            return 2 + (2 * r + o) % 3

        def wait(eng, sem, count):
            if not isinstance(count, int) or count > 0:
                eng.wait_ge(sem, count)

        @block.sync
        def _(sp):
            sp.dma_start(x_in, x_dram[:, 0, :, :]).then_inc(s["x_in"], 16)
            sp.dma_start(ident[:, :], A["c_ident"]).then_inc(s["const_in"], 16)
            sp.dma_start(q_mask[:, :], A["c_qmask"]).then_inc(s["const_in"], 16)
            sp.dma_start(k_mask[:, :], A["c_kmask"]).then_inc(s["const_in"], 16)
            sp.dma_start(rope[:, :, :, :], A["c_rope"]).then_inc(s["const_in"], 16)
            sp.dma_start(b_qkv[:, :], A["L0_attn_b_qkv"].unsqueeze(0).broadcast_to([P, 3 * D])
                         ).then_inc(s["const_in"], 16)
            sp.dma_start(b_out[:, :], A["L0_attn_b_out"].unsqueeze(0).broadcast_to([P, D])
                         ).then_inc(s["const_in"], 16)
            sp.dma_start(x_res, x_dram[:, 0, :, :]).then_inc(s["xres_in"], 16)
            sp.dma_start(g.w2_raw[:, :, :], A["L0_ffn_ent_w_T"][0].rearrange("(c p) n -> p c n", p=P)
                         ).then_inc(g.pre["w2_in"], 16)
            sp.dma_start(g.w1_raw[:, :, :].rearrange("p c (m d) -> p (c m) d", d=D),
                           A["L0_ffn_ent_pw"][0].rearrange("(c p) n -> p c n", p=P)).then_inc(g.pre["w1_in"], 16)

            def max_row(i, when, pair):
                sp.wait_ge(s["ex_read"], EXCHANGE.number(i, when, ("neg", pair)) + 1)
                p = pair % PAIRS
                for o in range(2):
                    row = o * SLOT + 3 * DH
                    sp.dma_start(qT[row:row + 1, p, :].bitcast(F32).rearrange("o (t c) -> o t c", t=RT),
                                 neg_rows[o * RT:(o + 1) * RT, p % 2, :].bitcast(F32)
                                 ).then_inc(s[f"m_row{p % 2}"], 16)

            def entry(i, when):
                if when != "last":
                    sp.wait_ge(s["v_xT"], i + 1)
                    sp.dma_start(x_in, x_dram[:, i + 1, :, :]).then_inc(s["x_in"], 16)
                for p in range(PAIRS):
                    if p < PAIRS - 1 or when != "last":
                        max_row(i, when, p + 1)
                    if p == 4 and when != "first":
                        sp.wait_ge(s["v_work"], WORK.number(i, when, ("out", 1)) + 1)
                        sp.dma_start(x_res, x_dram[:, i, :, :]).then_inc(s["xres_in"], 16)

            max_row(-1, "before", 0)
            entries(sp, entry)

        @block.gpsimd
        def _(pool):
            pool.memset(val[:, :, :, DH:2 * DH], 1.0).then_inc(s["g_ones"], 1)
            pool.wait_ge(s["const_in"], 96)
            chain = Chain(pool, s["g_chain"])

            def heads_of(t):
                return qkv[:, t, :].rearrange("p (h c d) -> p h c d", h=UH, c=3)

            def rotate(i, when, u, t):
                n = tile_number(i, u, t)
                pool.wait_ge(s["v_work"], WORK.number(i, when, ("project", (u, t))) + 1)
                wait(pool, s["g_rope"], n)
                r = heads_of(t)[:, :, 0:2, 0:4]
                by_cos = turned[:, 0, :].rearrange("p (h c d) -> p h c d", h=UH, c=2)
                by_sin = turned[:, 1, :].rearrange("p (h c d) -> p h c d", h=UH, c=2)

                def table(w, lo, hi):
                    return rope[:, w, t, lo:hi].unsqueeze(1).unsqueeze(1).broadcast_to([P, UH, 2, hi - lo])

                chain.step(pool.tensor_tensor(by_cos, r, table(0, 0, 4), ALU.mult))
                chain.step(pool.tensor_tensor(by_sin[:, :, :, 0:2], r[:, :, :, 2:4], table(1, 0, 2), ALU.mult))
                chain.step(pool.tensor_tensor(by_sin[:, :, :, 2:4], r[:, :, :, 0:2], table(1, 2, 4), ALU.mult))
                chain.settle()
                pool.tensor_tensor(r, by_cos, by_sin, ALU.add).then_inc(s["g_rope"], 1)

            def values(i, u, t):
                pool.tensor_copy(val[:, t, u * UH:(u + 1) * UH, 0:DH], heads_of(t)[:, :, 2, :]
                                 ).then_inc(s["g_val"], 1)

            def unit(i, when, u):
                rotate(i, when, u, 0)
                rotate(i, when, u, 1)
                wait(pool, s["p_out"], i * PAIRS + (0 if u else UP))
                pool.sem_inc(g.carrier["g_carrier"], 1)
                values(i, u, 0)
                values(i, u, 1)
                rotate(i, when, u, 2)
                values(i, u, 2)
                rotate(i, when, u, 3)
                values(i, u, 3)

            def keep(b):
                pool.wait_ge(s["v_norm"], b + 2)
                pool.sem_inc(g.carrier["g_carrier"], 1)
                pool.tensor_copy(g.x_a[:, bass.ts(b, RT), :], xn[:, 0, :, :]).then_inc(s["g_x1"], 1)

            def residual_bias(b):
                pool.wait_ge(s["xres_in"], 16 * b + 16)
                pool.tensor_tensor(x_res, x_res, bcast(b_out[:, :], 1, [P, RT, D]), ALU.add
                                   ).then_inc(s["g_res"], 1)

            def entry(i, when):
                if when == "loop":
                    chain.enter(i - 1, 2 * RT * 3)
                unit(i, when, 1)
                if when != "last":
                    unit(i, when, 0)
                if when != "first":
                    keep(i - 1)
                    residual_bias(i)
                if when == "loop":
                    chain.leave(B - 2)

            unit(-1, "before", 0)
            residual_bias(0)
            entries(pool, entry)
            keep(B - 1)

        @block.scalar
        def _(act):
            act.dma_start(raw_qkv, A["L0_attn_w_qkv"].rearrange("(c p) n -> p c n", p=P)
                          ).then_inc(s["qkv_in"], 16)
            act.dma_start(raw_out, A["L0_attn_w_out"].rearrange("(c p) n -> p c n", p=P)
                          ).then_inc(s["out_in"], 16)
            act.wait_ge(s["qkv_in"], 16)
            act.activation(wqkv_h[:, :, :], raw_qkv, ACT.Copy).then_inc(s["wsplit_h"], 1)
            act.wait_ge(s["out_in"], 16)
            act.activation(wout_h[:, :, :], raw_out, ACT.Copy).then_inc(s["wsplit_h"], 1)
            act.wait_ge(s["mask_v"], 1)

            def high(i, when, kind, arg):
                act.wait_ge(s["p_work"], WORK.number(i, when, (kind, arg)))
                if kind == "x_T":
                    act.activation(x_h[:, arg, :], work, ACT.Copy).then_inc(s["a_xT"], 1)
                elif kind == "att_T":
                    act.activation(att_h[:, arg, :], work, ACT.Copy).then_inc(s["a_attT"], 1)
                else:
                    act.sem_inc(g.carrier["a_carrier"], 1)
                    act.activation(g.xT_h[:, i - 1, arg, :], work, ACT.Copy).then_inc(s["a_nT"], 1)

            def stack_high(i, u, t):
                act.wait_ge(s["g_rope"], tile_number(i, u, t) + 1)
                heads = qkv[:, t, :].rearrange("p (h c d) -> p h c d", h=UH, c=3)
                act.activation(q_stack[:, :, :].rearrange("p h (n d) -> p h n d", d=DH)[:, :, 0:3:2, :],
                               bcast(heads[:, :, 0, :], 2, [P, UH, 2, DH]), ACT.Copy)
                act.activation(k_stack[:, :, :].rearrange("p h (n d) -> p h n d", d=DH)[:, :, 0:2, :],
                               bcast(heads[:, :, 1, :], 2, [P, UH, 2, DH]), ACT.Copy).then_inc(s["a_stack"], 1)

            def copy_q(i, when, u, t):
                act.wait_ge(s["p_ex"], EXCHANGE.number(i, when, ("stack", (u, t))))
                act.activation(qT[:, u * UP:(u + 1) * UP, t * P:(t + 1) * P],
                               exchange.rearrange("p (b c) -> p b c", c=P), ACT.Copy).then_inc(s["ex_read"], 1)

            def exponentials(i, p, r):
                j = J_ORDER[r]
                for o in range(2):
                    act.wait_ge(s["p_score"], ((i * PAIRS + p) * RT + r) * 2 + o + 1)
                    if r == 0 and o == 0:
                        wait(act, s["p_out"], i * PAIRS + p - 1)
                    act.activation(probs[:, p % 2, o, OFF[j]:OFF[j] + COLS[j]],
                                   ps[:, score_bank(r, o), 0:COLS[j]], ACT.Exp).then_inc(s["a_exp"], 1)

            def copy_outputs(i, when, q, use):
                act.wait_ge(s["p_out"], i * PAIRS + 2 * q + 2)
                act.wait_ge(s["p_ex"], EXCHANGE.number(i, when, use))
                act.activation(out_T[:, :], outputs, ACT.Copy).then_inc(s["a_out"], 1)

            def entry(i, when):
                table = work_table(when)
                before = (None, None)
                for p in range(PAIRS):
                    for r in range(RT):
                        exponentials(i, p, r)
                        if r == RT - 1 and p % 2 == 0 and (p or when != "first"):
                            copy_outputs(i, when, p // 2 - 1, ("neg", p + 1))
                        kind, arg = table.get((p, r), (None, None))
                        if kind == "stack":
                            copy_q(i, when, *arg)
                        elif kind in ("x_T", "att_T", "next_T"):
                            high(i, when, kind, arg)
                        if before[0] == "project":
                            stack_high(i, *before[1])
                        before = (kind, arg)

            for c in range(KC):
                high(-1, "before", "x_T", c)
            for t in range(RT):
                stack_high(-1, 0, t)
                copy_q(-1, "before", 0, t)
            entries(act, entry)
            copy_outputs(B - 1, "last", GROUPS - 1, ("group", GROUPS - 2))
            for kind in ("att_T", "next_T"):
                for c in range(KC):
                    high(B, "after", kind, c)

        @block.tensor
        def _(pe):
            pe.wait_ge(s["const_in"], 96)

            def max_pass(i, p, t, unit_at):
                if p % UP == 0:
                    pe.wait_ge(s["v_work"], WORK.number(*unit_at, ("stack", (p // UP, t))) + 1)
                    pe.wait_ge(s["ex_read"], EXCHANGE.number(*unit_at, ("stack", (p // UP, t))) + 1)
                for o in range(2):
                    n = (i * PAIRS + p) * 2 * RT + 2 * t + o
                    rows = slice(o * SLOT, (o + 1) * SLOT)
                    pe.wait_ge(s["v_max"], n + 1)
                    pe.matmul(ps[:, o, 0:(t + 1) * P], qT[rows, p, t * P:(t + 1) * P],
                              kT[rows, p, 0:(t + 1) * P], start=True, stop=True).then_inc(s["p_max"], 1)

            def score_pass(i, p, r):
                j = J_ORDER[r]
                if r == 0:
                    pe.wait_ge(s[f"m_row{p % 2}"], 32 * (i * (PAIRS // 2) + p // 2 + 1))
                for o in range(2):
                    n, rows = ((i * PAIRS + p) * RT + r) * 2 + o, slice(o * SLOT, (o + 1) * SLOT)
                    wait(pe, s["a_exp"], n - (1 if 2 * r + o < 2 else 2))
                    bank = score_bank(r, o)
                    pe.matmul(ps[:, bank, 0:COLS[j]], kT[rows, p, j * P:(j + 1) * P],
                              qT[rows, p, j * P:S], start=True, stop=False)
                    pe.matmul(ps[:, bank, 0:P], ident_b[:, :], mask_b[:, :], start=False, stop=True
                              ).then_inc(s["p_score"], 1)

            def value_pass(i, p, r):
                j = J_ORDER[r]
                if r == 0 and p % 2 == 0:
                    pe.wait_ge(s["a_out"], i * GROUPS + p // 2 + 1)
                if r == 0 and p % UP == 0:
                    pe.wait_ge(s["g_val"], 2 * RT * i + (p // UP + 1) * RT)
                pe.wait_ge(s["a_exp"], 2 * ((i * PAIRS + p) * RT + r + 1))
                for o in range(2):
                    rows = 2 * DH * (2 * (p % 2) + o)
                    mm = pe.matmul(outputs[rows:rows + 2 * DH, j * P:S], val[:, j, 2 * p + o, :],
                                   probs[:, p % 2, o, OFF[j]:OFF[j] + COLS[j]], start=(r == 0), stop=(r == RT - 1))
                if r == RT - 1:
                    mm.then_inc(s["p_out"], 1)

            def max_rows(i, when, p, pair):
                pe.wait_ge(s["v_neg"], pair + 3)
                pe.wait_ge(s["ex_read"], EXCHANGE.number(i, when, ("neg", p)))
                pe.transpose(exchange[:, 0:P].bitcast(F32R), neg_max[:, :], ident_r[:, :]).then_inc(s["p_ex"], 1)

            def transpose_outputs(i, when, q):
                pe.wait_ge(s["a_out"], i * GROUPS + q + 2)
                pe.wait_ge(s["ex_read"], EXCHANGE.number(i, when, ("group", q if when != "after" else -1)))
                for t in range(RT):
                    mm = pe.transpose(exchange[:, t * P:(t + 1) * P], out_T[:, t * P:(t + 1) * P], ident[:, :])
                mm.then_inc(s["p_ex"], 1)

            def use_work(i, when, kind, arg):
                pe.wait_ge(s["v_work"], WORK.number(i, when, (kind, arg)))
                if kind == "project":
                    u, t = arg
                    n = 0
                    for c in range(KC):
                        for x, w in ((x_h, wqkv_h), (x_h, wqkv_l), (x_l, wqkv_h)):
                            mm = pe.matmul(work[:, 0:UC], x[:, c, t * P:(t + 1) * P],
                                           w[:, c, u * UC:(u + 1) * UC], start=(n == 0), stop=(n == 5))
                            n += 1
                elif kind == "stack":
                    u, t = arg
                    pe.wait_ge(s["v_stack"], tile_number(i, u, t) + 1)
                    for p in range(UP):
                        mm = pe.transpose(work[:, p * P:(p + 1) * P].bitcast(F32R),
                                          k_stack[:, 2 * p:2 * p + 2, :].rearrange("p a b -> p (a b)"), ident_r[:, :])
                elif kind == "out":
                    for t in (2 * arg, 2 * arg + 1):
                        n = 0
                        for c in range(KC):
                            for x, w in ((att_h, wout_h), (att_h, wout_l), (att_l, wout_h)):
                                mm = pe.matmul(work[:, (t % 2) * D:(t % 2 + 1) * D],
                                               x[:, c, t * P:(t + 1) * P], w[:, c, :], start=(n == 0), stop=(n == 5))
                                n += 1
                else:
                    if kind == "x_T":
                        pe.wait_ge(s["x_in"], 16 * (i + 2))
                        src = x_in
                    elif kind == "att_T":
                        pe.wait_ge(s["ex_read"], EXCHANGE.number(i, when, ("group", -1)) + 1)
                        src = att
                    else:
                        pe.wait_ge(s["v_norm"], i + 1)
                        src = xn[:, 0, :, :]
                    for t in range(RT):
                        mm = pe.transpose(work[:, t * P:(t + 1) * P], src[:, t, arg * P:(arg + 1) * P], ident[:, :])
                mm.then_inc(s["p_work"], 1)
                if kind == "stack":
                    pe.wait_ge(s["ex_read"], EXCHANGE.number(i, when, (kind, arg)))
                    for p in range(UP):
                        mm = pe.transpose(exchange[:, p * P:(p + 1) * P].bitcast(F32R),
                                          q_stack[:, 2 * p:2 * p + 2, :].rearrange("p a b -> p (a b)"), ident_r[:, :])
                    mm.then_inc(s["p_ex"], 1)

            def entry(i, when):
                table = work_table(when)
                for p in range(PAIRS):
                    for r in range(RT):
                        if p + 2 < PAIRS:
                            max_pass(i, p + 2, r, (i, when))
                        elif when != "last":
                            max_pass(i + 1, p + 2 - PAIRS, r, (i, when))
                        if r == 1 and (p < PAIRS - 1 or when != "last"):
                            max_rows(i, when, p + 1, i * PAIRS + p + 1)
                        score_pass(i, p, r)
                        if p:
                            value_pass(i, p - 1, r)
                        elif when != "first":
                            value_pass(i - 1, PAIRS - 1, r)
                        if (p, r) in table:
                            use_work(i, when, *table[p, r])
                        if r == 2 and p % 2 and (p > 1 or when != "first"):
                            transpose_outputs(i, when, (p - 3) // 2)

            use_work(-1, "before", "x_T", 0)
            use_work(-1, "before", "x_T", 1)
            pe.wait_ge(s["wsplit_l"], 2)
            pe.wait_ge(s["const_v"], 1)
            pe.wait_ge(s["g_ones"], 1)
            for _, _, kind, t in UNIT_AT:
                use_work(-1, "before", kind, (0, t))
            for p in range(2):
                for t in range(RT):
                    max_pass(0, p, t, (-1, "before"))
                    if p and t == 1:
                        max_rows(-1, "before", 0, 0)
            entries(pe, entry)
            for r in range(RT):
                value_pass(B - 1, PAIRS - 1, r)
            transpose_outputs(B - 1, "after", GROUPS - 1)
            for _, _, kind, arg in PREVIOUS:
                use_work(B, "after", kind, arg)

        @block.vector
        def _(v):
            chain = Chain(v, s["v_chain"])
            for name in ("v_work", "ex_read", "a_out", "v_norm", "g_x1"):
                v.sem_inc(s[name], 1)
            v.sem_inc(s["v_max"], 2)
            v.sem_inc(s["v_neg"], 2)
            v.wait_ge(s["const_in"], 96)
            v.tensor_copy(ident_r[:, :], ident[:, :])
            v.tensor_copy(ident_b[:, :], ident[:, :])
            v.tensor_copy(mask_b[:, :], k_mask[:, :]).then_inc(s["const_v"], 1)
            v.memset(neg_max[:, :].bitcast(F32), 0.0)
            v.memset(q_stack[:, :, 3 * DH:SLOT].bitcast(F32), 0.0)
            chain.step(v.memset(k_stack[:, :, 3 * DH:SLOT].bitcast(F32), 0.0))
            chain.settle()
            v.memset(k_stack[:, :, 3 * DH:3 * DH + 1].bitcast(F32), 1.0).then_inc(s["mask_v"], 1)

            def maximum(i, p, t):
                if t == 0:
                    v.wait_ge(s["v_neg"], i * PAIRS + p + 1)
                for o in range(2):
                    v.wait_ge(s["p_max"], (i * PAIRS + p) * 2 * RT + 2 * t + o + 1)
                    v.sem_inc(g.carrier["v_carrier"], 1)
                    v.tensor_tensor_reduce(
                        ps[:, o, 0:(t + 1) * P], ps[:, o, 0:(t + 1) * P], q_mask[:, S - (t + 1) * P:S],
                        1.0, MASKED, ALU.add, ALU.max,
                        top_score[:, p % 2, o * RT + t:o * RT + t + 1]).then_inc(s["v_max"], 1)

            def negate(i, p):
                v.wait_ge(s["v_max"], (i * PAIRS + p + 1) * 2 * RT + 2)
                v.tensor_scalar(neg_max[:, 0:2 * RT], top_score[:, p % 2, :], -1.0, None,
                                ALU.mult).then_inc(s["v_neg"], 1)

            def take_rows(i, when, key, pair, half):
                v.wait_ge(s["p_ex"], EXCHANGE.number(i, when, ("neg", key)))
                wait(v, s[f"m_row{pair}"], 32 * half)
                v.tensor_copy(neg_rows[:, pair, :], ps[0:2 * RT, 7, 0:P]).then_inc(s["ex_read"], 1)

            def take_outputs(i, when, q):
                v.wait_ge(s["p_ex"], EXCHANGE.number(i, when, ("group", q if when != "after" else -1)))
                o = exchange.rearrange("p (t h d) -> p t h d", t=RT, h=4)
                chain.step(v.reciprocal(inv[:, :, :], o[:, :, :, DH]))
                chain.settle()
                q = q % GROUPS
                v.tensor_tensor(
                    att[:, :, 4 * q * DH:4 * (q + 1) * DH].rearrange("p t (h d) -> p t h d", h=4),
                    o[:, :, :, 0:DH], bcast(inv[:, :, :], 3, [P, RT, 4, DH]), ALU.mult).then_inc(s["ex_read"], 1)

            def low(i, when, kind, c):
                b = i + 1 if kind == "x_T" else i - 1
                v.wait_ge(s[{"x_T": "a_xT", "att_T": "a_attT", "next_T": "a_nT"}[kind]], KC * b + c + 1)
                if kind == "x_T":
                    high, dst = x_h[:, c, :], x_l[:, c, :]
                elif kind == "att_T":
                    high, dst = att_h[:, c, :], att_l[:, c, :]
                else:
                    high, dst = g.xT_h[:, b, c, :], g.xT_l[:, b, c, :]
                v.tensor_tensor(dst, work, high.bitcast(F32), ALU.subtract).then_inc(s["v_work"], 1)
                if kind == "x_T" and c == KC - 1:
                    v.sem_inc(s["v_xT"], 1)

            def stack_low(i, u, t):
                v.wait_ge(s["a_stack"], tile_number(i, u, t) + 1)
                heads = qkv[:, t, :].rearrange("p (h c d) -> p h c d", h=UH, c=3)
                v.tensor_tensor(q_stack[:, :, DH:2 * DH], heads[:, :, 0, :],
                                q_stack[:, :, 0:DH].bitcast(F32), ALU.subtract)
                v.tensor_tensor(k_stack[:, :, 2 * DH:3 * DH], heads[:, :, 1, :],
                                k_stack[:, :, 0:DH].bitcast(F32), ALU.subtract).then_inc(s["v_stack"], 1)

            def take_work(i, when, kind, arg):
                v.wait_ge(s["p_work"], WORK.number(i, when, (kind, arg)))
                if kind == "project":
                    u, t = arg
                    n = tile_number(i, u, t)
                    wait(v, s["v_stack"], n - RT + 1)
                    wait(v, s["g_val"], n - RT + 1)
                    v.tensor_tensor(qkv[:, t, :], work[:, 0:UC], b_qkv[:, u * UC:(u + 1) * UC], ALU.add
                                    ).then_inc(s["v_work"], 1)
                elif kind == "stack":
                    u, t = arg
                    v.tensor_copy(kT[:, u * UP:(u + 1) * UP, t * P:(t + 1) * P],
                                  work.rearrange("p (b c) -> p b c", c=P)).then_inc(s["v_work"], 1)
                else:
                    v.wait_ge(s["g_res"], i)
                    v.wait_ge(s["v_norm"], i)
                    v.tensor_tensor(g.rsum[:, 2 * arg:2 * arg + 2, :], work.rearrange("p (b c) -> p b c", c=D),
                                    x_res[:, 2 * arg:2 * arg + 2, :], ALU.add).then_inc(s["v_work"], 1)

            def normalise(i, when):
                v.wait_ge(s["v_work"], WORK.number(i, when, ("out", 1)) + 1)
                yield from layernorm_steps(v, chain, g.lnw, g.rsum, xn[:, 0, :, :], s["v_norm"],
                                           (s["g_x1"], i))

            def entry(i, when):
                table = work_table(when)
                slots = [(p, r) for p in range(PAIRS) for r in range(RT)]
                norm = iter(())
                steps = GROUPS + RSTD_STEPS
                if when == "loop":
                    chain.enter(i - 1, steps)
                for n, (p, r) in enumerate(slots):
                    if p + 2 < PAIRS:
                        maximum(i, p + 2, r)
                    elif when != "last":
                        maximum(i + 1, p + 2 - PAIRS, r)
                    if r == 1 and (p < PAIRS - 1 or when != "last"):
                        q = p + 1
                        take_rows(i, when, q, q % 2, i * (PAIRS // 2) + q // 2)
                    kind, arg = table.get(slots[n - 1], (None, None)) if n else (None, None)
                    if kind in ("x_T", "att_T", "next_T"):
                        low(i, when, kind, arg)
                    kind, arg = table.get(slots[n - 2], (None, None)) if n >= 2 else (None, None)
                    if kind == "project":
                        stack_low(i, *arg)
                    kind, arg = table.get((p, r), (None, None))
                    if kind in ("project", "stack", "out"):
                        take_work(i, when, kind, arg)
                    if r == 2 and p % 2 and (p > 1 or when != "first"):
                        take_outputs(i, when, (p - 3) // 2)
                    if r == RT - 1:
                        if p + 2 < PAIRS:
                            negate(i, p + 2)
                        elif when != "last":
                            negate(i + 1, p + 2 - PAIRS)
                    if (p, r) == (4, 0) and when != "first":
                        norm = normalise(i, when)
                    next(norm, None)
                    next(norm, None)
                assert next(norm, None) is None
                if when == "loop":
                    chain.leave(B - 2)

            for c in range(KC):
                low(-1, "before", "x_T", c)
            v.wait_ge(s["wsplit_h"], 1)
            v.tensor_tensor(wqkv_l[:, :, :], raw_qkv, wqkv_h[:, :, :].bitcast(F32),
                            ALU.subtract).then_inc(s["wsplit_l"], 1)
            v.wait_ge(s["wsplit_h"], 2)
            v.tensor_tensor(wout_l[:, :, :], raw_out, wout_h[:, :, :].bitcast(F32),
                            ALU.subtract).then_inc(s["wsplit_l"], 1)
            for n, (_, _, kind, t) in enumerate(UNIT_AT):
                if kind == "stack":
                    stack_low(-1, 0, t)
                take_work(-1, "before", kind, (0, t))
            for p in range(2):
                for t in range(RT):
                    maximum(0, p, t)
                    if p and t == 1:
                        take_rows(-1, "before", 0, 0, 0)
                negate(0, p)
            entries(v, entry)
            take_outputs(B - 1, "after", GROUPS - 1)
            for c in range(KC):
                low(B, "after", "att_T", c)
            for half in range(2):
                take_work(B, "after", "out", half)
            for _ in normalise(B, "after"):
                pass
            for c in range(KC):
                low(B, "after", "next_T", c)
            chain.settle()


def wave_ffn(nc, A, g):
    ps, ident, xn, hs = g.ps, g.ident, g.xn, g.hs
    LAST = STAGES - 1
    stack = ExitStack()
    with stack:
        s = sems(stack, nc, "p_gate a_gate a_trig v_h a_hh g_xl p_lin v_scale a_norm g_chain g_hs p_T a_th v_tl "
                 "v_chain v_res v_scale2 a_norm2")
        amp = sb(stack, nc, "amp", [P, B, KC, S])
        tanh = sb(stack, nc, "tanh", [P, B, KC, S])
        scale = sb(stack, nc, "scale", [P, 2, RT])
        shift = sb(stack, nc, "shift", [P, 2, RT])
        half = g.x_b[:, :, :].rearrange("p (b n) d -> p b (n d)", b=B).rearrange("p b (c s) -> p b c s", c=KC)
        block = stack.enter_context(nc.Block())

        def banks(b):
            return [ps[:, 2 * b + k // 2, (k % 2) * D:(k % 2 + 1) * D] for k in range(RT)]

        def sums(b):
            return amp[:, b, :, :].rearrange("p c s -> p (c s)").rearrange("p (t d) -> p t d", d=D)

        TURN = ((0, (0, 3)), (1, (1, 0)), (2, (1, 1)), (3, (1, 2)))

        @block.sync
        def _(sp):
            sp.dma_start(g.w1_raw[:, :, :],
                         A["L1_ffn_W1_T"][0].rearrange("(c p) n -> p c n", p=P)).then_inc(g.pre["w1_in"], 16)
            sp.dma_start(g.w2_raw[:, :, :],
                         A["L1_ffn_W2_T"][0].rearrange("(c p) n -> p c n", p=P)).then_inc(g.pre["w2_in"], 16)

        @block.tensor
        def _(pe):
            for b in range(B):
                for w in range(2):
                    for m in range(KC):
                        n = (b * 2 + w) * KC + m
                        if n >= 8:
                            pe.wait_ge(s["a_gate"], n - 7)
                        k = 0
                        for c in range(KC):
                            cols = slice(w * D + m * P, w * D + (m + 1) * P)
                            for wt, x in ((g.gate_h, g.xT_h), (g.gate_h, g.xT_l), (g.gate_l, g.xT_h)):
                                mm = pe.matmul(ps[:, n % 8, :], wt[:, c, cols], x[:, b, c, :],
                                               start=(k == 0), stop=(k == 5))
                                k += 1
                        mm.then_inc(s["p_gate"], 1)
            pe.wait_ge(s["a_gate"], 4 * B)

            def linear(st, b, gates=False):
                if gates:
                    pe.wait_ge(s["g_xl"], b + 1)
                else:
                    pe.wait_ge(s["v_tl"], st * 2 * B + 2 * (b + 1))
                for t in range(RT):
                    n = 0
                    for c in range(KC):
                        for x, w in ((g.xT_h, g.stage_w_h), (g.xT_h, g.stage_w_l), (g.xT_l, g.stage_w_h)):
                            pe.matmul(banks(b)[t], x[:, b, c, t * P:(t + 1) * P], w[:, st, c, :],
                                      start=(n == 0), stop=False)
                            n += 1
                    for row in (g.stage_c_h, g.stage_c_l):
                        mm = pe.matmul(banks(b)[t], g.first_row[:, :], row[:, st, :],
                                       start=False, stop=(row is g.stage_c_l))
                mm.then_inc(s["p_lin"], 1)

            def transposes(st, b, src, ready, count):
                pe.wait_ge(ready, count)
                for c in range(KC):
                    for t in range(RT):
                        mm = pe.transpose(ps[:, 2 * b + c, t * P:(t + 1) * P], src[:, t, c * P:(c + 1) * P], ident[:, :])
                    mm.then_inc(s["p_T"], 1)

            for b in range(B - 1):
                linear(0, b, True)
            pe.wait_ge(s["g_xl"], B)
            with pe.Fori(0, LAST) as st:
                for b, (later, done) in TURN:
                    transposes(st, b, hs[:, b % 2, :, :], s["g_hs"], st * B + b + 3)
                    linear(st + later, done)
            linear(LAST, B - 1)
            for b in range(B):
                transposes(LAST, b, g.x_b[:, b * RT:(b + 1) * RT, :], s["a_norm2"], b + 1)

        @block.scalar
        def _(act):
            for b in range(B):
                for w, (func, dst) in enumerate(((ACT.Sigmoid, amp), (ACT.Tanh, tanh))):
                    for m in range(KC):
                        n = (b * 2 + w) * KC + m
                        act.wait_ge(s["p_gate"], n + 1)
                        act.activation(dst[:, b, m, :], ps[:, n % 8, :], func,
                                       bias=g.bias_col[:, 2 * w + m:2 * w + m + 1]).then_inc(s["a_gate"], 1)
            for b in range(B):
                act.wait_ge(s["a_gate"], (b + 1) * 4)
                act.activation(half[:, b, :, :], tanh[:, b, :, :], ACT.Sin, scale=PI_F32 / 2
                               ).then_inc(s["a_trig"], 1)
                act.wait_ge(s["a_trig"], 3 * b + 1)
                act.activation(tanh[:, b, :, :], tanh[:, b, :, :], ACT.Sin, scale=PI_F32
                               ).then_inc(s["a_trig"], 1)
                act.activation(half[:, b, :, :], half[:, b, :, :], ACT.Square).then_inc(s["a_trig"], 1)
                if b:
                    act.wait_ge(s["v_h"], b)
                    act.activation(g.xT_h[:, b - 1, :, :], amp[:, b - 1, :, :], ACT.Copy).then_inc(s["a_hh"], 1)
            act.wait_ge(s["v_h"], B)
            act.activation(g.xT_h[:, B - 1, :, :], amp[:, B - 1, :, :], ACT.Copy).then_inc(s["a_hh"], 1)

            def normalise(st, b):
                act.wait_ge(s["v_scale"], st * B + b + 1)
                act.wait_ge(s["g_hs"], st * B + b + 1)
                for k in range(RT):
                    ins = act.activation(xn[:, b % 2, k, :], banks(b)[k], ACT.Identity,
                                         bias=shift[:, b % 2, k:k + 1], scale=scale[:, b % 2, k:k + 1])
                ins.then_inc(s["a_norm"], 1)

            def high(st, b):
                for c in range(KC):
                    act.wait_ge(s["p_T"], st * 2 * B + 2 * b + c + 1 + 4)
                    act.activation(g.xT_h[:, b, c, :], ps[:, 2 * b + c, :], ACT.Copy).then_inc(s["a_th"], 1)

            for b in range(B - 1):
                normalise(0, b)
            with act.Fori(0, LAST) as st:
                high(st, 0)
                for n, (_, (later, done)) in enumerate(TURN):
                    if n + 1 < B:
                        high(st, n + 1)
                    normalise(st + later, done)
            normalise(LAST, B - 1)
            for b in range(B):
                act.wait_ge(s["v_scale2"], b + 1)
                for k in range(RT):
                    ins = act.activation(g.x_b[:, b * RT + k, :], sums(b)[:, k, :], ACT.Identity,
                                         bias=shift[:, b % 2, k:k + 1], scale=scale[:, b % 2, k:k + 1])
                ins.then_inc(s["a_norm2"], 1)
                if b:
                    high(LAST, b - 1)
            high(LAST, B - 1)

        @block.gpsimd
        def _(pool):
            chain = Chain(pool, s["g_chain"])
            pool.wait_ge(g.pre["rows_in"], 16 * 11)
            for b in range(B):
                pool.wait_ge(s["a_hh"], b + 1)
                pool.tensor_tensor(g.xT_l[:, b, :, :], amp[:, b, :, :], g.xT_h[:, b, :, :].bitcast(F32),
                                   ALU.subtract).then_inc(s["g_xl"], 1)

            def affine(st, b):
                pool.wait_ge(s["a_norm"], st * B + b + 1 + B)
                pool.sem_inc(g.carrier["g_carrier"], 1)
                chain.step(pool.tensor_tensor(xn[:, b % 2, :, :], xn[:, b % 2, :, :],
                                              bcast(g.stage_g[:, st, :], 1, [P, RT, D]), ALU.mult))
                chain.settle()
                if isinstance(st, int) and b >= 2:
                    pool.wait_ge(s["v_res"], b - 1)
                else:
                    pool.wait_ge(s["p_T"], st * 2 * B + 2 * b + 2)
                pool.sem_inc(g.carrier["g_carrier"], 1)
                pool.tensor_tensor(hs[:, b % 2, :, :], xn[:, b % 2, :, :],
                                   bcast(g.stage_b[:, st, :], 1, [P, RT, D]), ALU.add).then_inc(s["g_hs"], 1)

            with pool.Fori(0, LAST) as st:
                chain.enter(st, B)
                for b in range(B):
                    affine(st, b)
            chain.leave(LAST)
            for b in range(B):
                affine(LAST, b)

        @block.vector
        def _(v):
            chain = Chain(v, s["v_chain"])
            v.sem_inc(s["v_tl"], 2 * B)
            v.sem_inc(s["a_norm"], B)
            v.sem_inc(s["g_hs"], 2)
            v.sem_inc(s["p_T"], 4)
            for b in range(B):
                v.wait_ge(s["a_trig"], 3 * b + 3)
                chain.step(v.scalar_tensor_tensor(half[:, b, :, :], half[:, b, :, :], -2.0, tanh[:, b, :, :],
                                                  ALU.mult, ALU.add))
                chain.settle()
                v.scalar_tensor_tensor(amp[:, b, :, :], half[:, b, :, :], 1.0, amp[:, b, :, :],
                                       ALU.add, ALU.mult).then_inc(s["v_h"], 1)

            def statistics(tiles, slot, done):
                for _ in rstd_steps(v, chain, g.lnw, tiles, scale[:, slot, :]):
                    pass
                chain.settle()
                v.scalar_tensor_tensor(shift[:, slot, :], g.lnw["mv"][:, :, 0], -1.0, scale[:, slot, :],
                                       ALU.mult, ALU.mult).then_inc(done, 1)

            def moments(st, b):
                v.wait_ge(s["p_lin"], st * B + b + 1)
                if not isinstance(st, int) or st or b:
                    v.wait_ge(s["v_scale"], st * B + b)
                v.wait_ge(s["a_norm"], st * B + b + B - 1)
                statistics(banks(b), b % 2, s["v_scale"])

            def low(st, b):
                for c in range(KC):
                    v.wait_ge(s["a_th"], st * 2 * B + 2 * b + c + 1)
                    v.tensor_tensor(g.xT_l[:, b, c, :], ps[:, 2 * b + c, :], g.xT_h[:, b, c, :].bitcast(F32),
                                    ALU.subtract).then_inc(s["v_tl"], 1)

            for b in range(B - 1):
                moments(0, b)
            with v.Fori(0, LAST) as st:
                chain.enter(st, RSTD_STEPS * B)
                for b, (later, done) in TURN:
                    low(st, b)
                    moments(st + later, done)
            chain.leave(LAST)
            moments(LAST, B - 1)
            v.wait_ge(s["v_scale"], STAGES * B)
            v.wait_ge(s["a_norm"], STAGES * B + B)
            for b in range(B):
                v.wait_ge(s["g_hs"], LAST * B + b + 3)
                v.tensor_tensor(sums(b), hs[:, b % 2, :, :], g.x_a[:, b * RT:(b + 1) * RT, :],
                                ALU.add).then_inc(s["v_res"], 1)
                v.wait_ge(s["v_res"], b + 1)
                if b:
                    v.wait_ge(s["v_scale2"], b)
                if b >= 2:
                    v.wait_ge(s["a_norm2"], b - 1)
                statistics([sums(b)[:, k, :] for k in range(RT)], b % 2, s["v_scale2"])
                if b >= 2:
                    low(LAST, b - 2)
            low(LAST, B - 2)
            low(LAST, B - 1)


def attention1(nc, A, g):
    ps, ident, hs = g.ps, g.ident, g.hs
    UNITS = KC + RT
    NUM = P + P // DH
    stack = ExitStack()
    with stack:
        s = sems(stack, nc, "blocks_in g_ones p_unit a_exp a_v v_unit p_kv v_bd p_num v_att v_z "
                 "p_attT a_th v_tl p_proj v_sum v_chain v_norm g_xa x3_out0 x3_out1 p_T a_xh v_xl a_w")
        blocks = sb(stack, nc, "blocks", [P, NUM])
        q = sb(stack, nc, "q", [P, 2, KC, S])
        k = sb(stack, nc, "k", [P, 2, RT, D])
        v1 = sb(stack, nc, "v1", [P, 2, RT, KC, P + 1])
        ex = sb(stack, nc, "ex", [P, 2, S])
        pos = sb(stack, nc, "pos", [P, 2, S])
        bd = sb(stack, nc, "bd", [P, KC, NUM])
        z = sb(stack, nc, "z", [P, 2, KC, P // DH])
        att = sb(stack, nc, "att1", [P, RT, D])
        att_h = sb(stack, nc, "att1_h", [P, KC, S], F32R)
        att_l = sb(stack, nc, "att1_l", [P, KC, S], F32R)
        block = stack.enter_context(nc.Block())

        @block.sync
        def _(sp):
            sp.dma_start(blocks[:, :], A["c_blocks"]).then_inc(s["blocks_in"], 16)
            for b in range(B - 1):
                sp.wait_ge(s["v_norm"], b + 1)
                sp.dma_start(g.x3_dram[b].rearrange("(t p) d -> p t d", p=P), hs[:, b % 2, :, :]
                             ).then_inc(s[f"x3_out{b % 2}"], 16)
            sp.wait_ge(s["x3_out0"], 16 * (B // 2))
            sp.wait_ge(s["x3_out1"], 16 * (B // 2 - 1))

        @block.gpsimd
        def _(pool):
            pool.memset(v1[:, :, :, :, P:P + 1], 1.0).then_inc(s["g_ones"], 1)
            for b in range(B - 1):
                pool.wait_ge(s["v_norm"], b + 1)
                pool.tensor_tensor(g.x_a[:, b * RT:(b + 1) * RT, :], hs[:, b % 2, :, :],
                                   bcast(g.mlp_b2[:, 0, :], 1, [P, RT, D]), ALU.add).then_inc(s["g_xa"], 1)

        @block.tensor
        def _(pe):
            pe.wait_ge(s["g_ones"], 1)

            def unit(b, j):
                n = b * UNITS + j
                if n >= 3:
                    pe.wait_ge(s["a_exp"], n - 2)
                    if (n - 3) % UNITS >= KC:
                        pe.wait_ge(s["a_v"], (n - 3) // UNITS * RT + (n - 3) % UNITS - KC + 1)
                i = 0
                for c in range(KC):
                    if j < KC:
                        cols = slice(j * P, (j + 1) * P)
                        parts = ((g.wq_h[:, c, cols], g.xT_h[:, b, c, :]), (g.wq_h[:, c, cols], g.xT_l[:, b, c, :]),
                                 (g.wq_l[:, c, cols], g.xT_h[:, b, c, :]))
                    else:
                        cols = slice((j - KC) * P, (j - KC + 1) * P)
                        parts = ((g.xT_h[:, b, c, cols], g.wkv_h[:, c, :]), (g.xT_h[:, b, c, cols], g.wkv_l[:, c, :]),
                                 (g.xT_l[:, b, c, cols], g.wkv_h[:, c, :]))
                    for lhsT, rhs in parts:
                        mm = pe.matmul(ps[:, n % 3, :], lhsT, rhs, start=(i == 0), stop=(i == 5))
                        i += 1
                mm.then_inc(s["p_unit"], 1)

            def key_values(b):
                pe.wait_ge(s["v_unit"], (b + 1) * UNITS)
                pe.wait_ge(s["a_v"], (b + 1) * RT)
                if b:
                    pe.wait_ge(s["v_att"], 2 * b)
                for m in range(KC):
                    for t in range(RT):
                        mm = pe.matmul(ps[:, 3, m * D:m * D + P + 1], k[:, b % 2, t, m * P:(m + 1) * P],
                                       v1[:, b % 2, t, m, :], start=(t == 0), stop=(t == RT - 1))
                mm.then_inc(s["p_kv"], 1)

            def numerators(b, half):
                if half == 0:
                    pe.wait_ge(s["v_bd"], b + 1)
                else:
                    pe.wait_ge(s["v_att"], 2 * b + 1)
                for t in (2 * half, 2 * half + 1):
                    for m in range(KC):
                        mm = pe.matmul(ps[:, 3 + t % 2, m * NUM:(m + 1) * NUM], q[:, b % 2, m, t * P:(t + 1) * P],
                                       bd[:, m, :], start=True, stop=True)
                mm.then_inc(s["p_num"], 1)

            def transpose_attention(b):
                pe.wait_ge(s["v_att"], 2 * b + 2)
                if b:
                    pe.wait_ge(s["v_sum"], b)
                for c in range(KC):
                    for t in range(RT):
                        mm = pe.transpose(ps[:, 5 + c, t * P:(t + 1) * P], att[:, t, c * P:(c + 1) * P], ident[:, :])
                    mm.then_inc(s["p_attT"], 1)

            def project(b):
                pe.wait_ge(s["v_tl"], KC * (b + 1))
                for t in range(RT):
                    n = 0
                    for c in range(KC):
                        for x, w in ((att_h, g.wo_h), (att_h, g.wo_l), (att_l, g.wo_h)):
                            mm = pe.matmul(ps[:, 5 + t // 2, (t % 2) * D:(t % 2 + 1) * D],
                                           x[:, c, t * P:(t + 1) * P], w[:, c, :], start=(n == 0), stop=(n == 5))
                            n += 1
                mm.then_inc(s["p_proj"], 1)

            def transpose_next(b, c):
                pe.wait_ge(s["v_norm"], b + 1)
                if b + c:
                    pe.wait_ge(s["v_xl"], KC * b + c)
                for t in range(RT):
                    mm = pe.transpose(ps[:, 7, t * P:(t + 1) * P], hs[:, b % 2, t, c * P:(c + 1) * P], ident[:, :])
                mm.then_inc(s["p_T"], 1)

            for step in range(B + 2):
                if 0 <= step - 2:
                    transpose_attention(step - 2)
                if step < B:
                    for j in range(UNITS):
                        unit(step, j)
                if 0 <= step - 1 < B:
                    key_values(step - 1)
                if 0 <= step - 2:
                    project(step - 2)
                for half in range(2):
                    if 0 <= step - 1 < B:
                        numerators(step - 1, half)
                    if 0 <= step - 3:
                        transpose_next(step - 3, half)

        @block.scalar
        def _(act):
            for step in range(B + 2):
                if 0 <= step - 2:
                    b = step - 2
                    for c in range(KC):
                        act.wait_ge(s["p_attT"], KC * b + c + 1)
                        if b:
                            act.wait_ge(s["p_proj"], b)
                        act.activation(att_h[:, c, :], ps[:, 5 + c, :], ACT.Copy).then_inc(s["a_th"], 1)
                if step < B:
                    b = step
                    for j in range(UNITS):
                        n = b * UNITS + j
                        width = S if j < KC else D
                        act.wait_ge(s["p_unit"], n + 1)
                        if n >= 2:
                            act.wait_ge(s["v_unit"], n - 1)
                        act.activation(ex[:, n % 2, 0:width], ps[:, n % 3, 0:width], ACT.Exp)
                        act.activation(pos[:, n % 2, 0:width], ps[:, n % 3, 0:width], ACT.Relu
                                       ).then_inc(s["a_exp"], 1)
                        if j >= KC:
                            if b >= 2:
                                act.wait_ge(s["p_kv"], b - 1)
                            act.activation(v1[:, b % 2, j - KC, :, 0:P],
                                           ps[:, n % 3, D:2 * D].rearrange("p (m n) -> p m n", m=KC),
                                           ACT.Copy).then_inc(s["a_v"], 1)
                if step == B + 1:
                    act.wait_ge(g.pre["w1_in"], 32)
                    for c in range(KC):
                        act.activation(g.w1_h[:, c, :], g.w1_raw[:, c, :], ACT.Copy).then_inc(s["a_w"], 1)
                if 0 <= step - 3:
                    b = step - 3
                    for c in range(KC):
                        act.wait_ge(s["p_T"], KC * b + c + 1)
                        act.activation(g.xT_h[:, b, c, :], ps[:, 7, :], ACT.Copy).then_inc(s["a_xh"], 1)

        @block.vector
        def _(v):
            chain = Chain(v, s["v_chain"])
            v.wait_ge(s["blocks_in"], 16)

            def unit(b, j):
                n = b * UNITS + j
                width = S if j < KC else D
                v.wait_ge(s["a_exp"], n + 1)
                if b >= 2:
                    if j < KC:
                        v.wait_ge(s["p_num"], 2 * (b - 1))
                    else:
                        v.wait_ge(s["p_kv"], b - 1)
                dst = q[:, b % 2, j, :] if j < KC else k[:, b % 2, j - KC, :]
                v.scalar_tensor_tensor(dst, ex[:, n % 2, 0:width], 1.0, pos[:, n % 2, 0:width],
                                       ALU.min, ALU.add).then_inc(s["v_unit"], 1)

            def block_diagonal(b):
                v.wait_ge(s["p_kv"], b + 1)
                if b:
                    v.wait_ge(s["p_num"], 2 * b)
                kv = ps[:, 3, :].rearrange("p (m n) -> p m n", m=KC)
                v.tensor_tensor(bd[:, :, 0:P], kv[:, :, 0:P], bcast(blocks[:, 0:P], 1, [P, KC, P]), ALU.mult)
                v.tensor_tensor(bd[:, :, P:NUM], kv[:, :, P:P + 1].broadcast_to([P, KC, NUM - P]),
                                bcast(blocks[:, P:NUM], 1, [P, KC, NUM - P]), ALU.mult).then_inc(s["v_bd"], 1)

            def normalise(b, half):
                v.wait_ge(s["p_num"], 2 * b + half + 1)
                if b + half:
                    v.wait_ge(s["v_att"], 2 * b + half)
                o = ps[:, 3:5, 0:KC * NUM].rearrange("p t (m n) -> p t m n", m=KC)
                v.tensor_scalar(z[:, :, :, :], o[:, :, :, P:NUM], 1e-6, None, ALU.add).then_inc(s["v_z"], 1)
                v.wait_ge(s["v_z"], 2 * (2 * b + half) + 1)
                v.reciprocal(z[:, :, :, :], z[:, :, :, :]).then_inc(s["v_z"], 1)
                v.wait_ge(s["v_z"], 2 * (2 * b + half) + 2)
                if b:
                    v.wait_ge(s["p_attT"], KC * b)
                for i in range(2):
                    ins = v.tensor_tensor(
                        att[:, 2 * half + i, :].rearrange("p (m h d) -> p m h d", m=KC, d=DH),
                        o[:, i, :, 0:P].rearrange("p m (h d) -> p m h d", d=DH),
                        bcast(z[:, i, :, :], 3, [P, KC, P // DH, DH]), ALU.mult)
                ins.then_inc(s["v_att"], 1)

            def normalise_next(b):
                v.wait_ge(s["v_sum"], b + 1)
                if b >= 2:
                    v.wait_ge(s["p_T"], KC * (b - 1))
                    v.wait_ge(s[f"x3_out{b % 2}"], 16 * (b // 2))
                    v.wait_ge(s["g_xa"], b - 1)
                yield from layernorm_steps(v, chain, g.lnw, g.rsum, hs[:, b % 2, :, :], s["v_norm"])

            norm = iter(())
            for step in range(B + 2):
                if 0 <= step - 2:
                    b = step - 2
                    for c in range(KC):
                        v.wait_ge(s["a_th"], KC * b + c + 1)
                        v.tensor_tensor(att_l[:, c, :], ps[:, 5 + c, :], att_h[:, c, :].bitcast(F32),
                                        ALU.subtract).then_inc(s["v_tl"], 1)
                if step < B:
                    for j in range(UNITS):
                        unit(step, j)
                        next(norm, None)
                        next(norm, None)
                        next(norm, None)
                for _ in norm:
                    pass
                if 0 <= step - 1 < B:
                    block_diagonal(step - 1)
                if 0 <= step - 2:
                    b = step - 2
                    v.wait_ge(s["p_proj"], b + 1)
                    if b:
                        v.wait_ge(s["v_norm"], b)
                    v.tensor_tensor(g.rsum[:, :, :], ps[:, 5:7, :].rearrange("p a (b c) -> p (a b) c", c=D),
                                    g.x_b[:, b * RT:(b + 1) * RT, :], ALU.add).then_inc(s["v_sum"], 1)
                for half in range(2):
                    if 0 <= step - 1 < B:
                        normalise(step - 1, half)
                    if 0 <= step - 3:
                        if step == B + 1:
                            v.wait_ge(s["a_w"], half + 1)
                            v.tensor_tensor(g.w1_l[:, half, :], g.w1_raw[:, half, :],
                                            g.w1_h[:, half, :].bitcast(F32), ALU.subtract)
                        v.wait_ge(s["a_xh"], KC * (step - 3) + half + 1)
                        v.tensor_tensor(g.xT_l[:, step - 3, half, :], ps[:, 7, :],
                                        g.xT_h[:, step - 3, half, :].bitcast(F32),
                                        ALU.subtract).then_inc(s["v_xl"], 1)
                if 0 <= step - 2 < B - 1:
                    norm = normalise_next(step - 2)


def weight_piece(w, w1, w2):
    if w < 4:
        return w2[:, 2 * w:2 * w + 2, :].rearrange("p a b -> p (a b)")
    c, half = divmod(w - 4, 2)
    return w1[:, c, half * S:(half + 1) * S]


def ffn1(nc, A, g, out):
    ps, ident, xn, hs = g.ps, g.ident, g.xn, g.hs
    TU = WP = 8
    PLACES = (3, 0, 1, 2)
    stack = ExitStack()
    with stack:
        s = sems(stack, nc, "p_T a_T v_T a_w v_w p_hid a_g v_gl p_out v_sum v_chain v_norm g_chain g_hs g_res "
                 "x3_in0 x3_in1 y_out0 y_out1 v_x3 x3_out")
        w1_in, w2_in = g.pre["w1_in"], g.pre["w2_in"]
        w1_h, w1_l = g.w1_h, g.w1_l
        w2_h = sb(stack, nc, "w2_h", [P, FC, D], F32R)
        w2_l = sb(stack, nc, "w2_l", [P, FC, D], F32R)
        G_h = sb(stack, nc, "G_h", [P, 2, FC, S], F32R)
        G_l = sb(stack, nc, "G_l", [P, 2, FC, S], F32R)
        G32 = sb(stack, nc, "G32", [P, 4, S])
        y_dram = out.rearrange("b (t p) d -> p b t d", p=P)
        x3 = g.x3_dram.rearrange("b (t p) d -> p b t d", p=P)
        block = stack.enter_context(nc.Block())
        LAST = BLOCKS - 1

        @block.sync
        def _(sp):
            def load_w1(k):
                sp.dma_start(g.w1_raw[:, :, :], A["L1_ffn_W1_T"][k].rearrange("(c p) n -> p c n", p=P)
                             ).then_inc(w1_in, 16)

            def load_w2(k):
                sp.dma_start(g.w2_raw[:, :, :], A["L1_ffn_W2_T"][k].rearrange("(c p) n -> p c n", p=P)
                             ).then_inc(w2_in, 16)

            sp.wait_ge(s["v_x3"], 1)
            sp.dma_start(x3[:, B - 1, :, :], hs[:, (B - 1) % 2, :, :]).then_inc(s["x3_out"], 16)
            load_w1(1)
            with sp.Fori(0, BLOCKS - 2) as i:
                sp.wait_ge(s["v_w"], i * WP + 8)
                load_w2(i + 1)
                sp.wait_ge(s["v_w"], i * WP + 12)
                load_w1(i + 2)
            sp.wait_ge(s["v_w"], (LAST - 1) * WP + 8)
            load_w2(LAST)
            sp.wait_ge(s["v_w"], (LAST - 1) * WP + 12)
            sp.dma_start(g.w1_raw[:, :, :].rearrange("p a (b d) -> p a b d", d=D), x3[:, 0:2, :, :]
                         ).then_inc(s["x3_in0"], 16)
            sp.wait_ge(s["v_w"], LAST * WP + 8)
            sp.wait_ge(s["x3_out"], 16)
            sp.dma_start(g.w2_raw[:, :, :].rearrange("p (b t) d -> p b t d", b=2), x3[:, 2:4, :, :]
                         ).then_inc(s["x3_in1"], 16)
            for b in range(B):
                sp.wait_ge(s["v_norm"], LAST * B + b + 2)
                sp.dma_start(y_dram[:, b, :, :], xn[:, b % 2, :, :]).then_inc(s[f"y_out{b % 2}"], 16)
            for b in range(2):
                sp.wait_ge(s[f"y_out{b}"], 16 * B // 2)

        @block.gpsimd
        def _(pool):
            chain = Chain(pool, s["g_chain"])
            pool.sem_inc(s["g_hs"], 1)
            pool.sem_inc(s["g_res"], B - 1)
            pool.wait_ge(s["v_x3"], 1)
            pool.tensor_tensor(g.x_a[:, (B - 1) * RT:B * RT, :], hs[:, (B - 1) % 2, :, :],
                               bcast(g.mlp_b2[:, 0, :], 1, [P, RT, D]), ALU.add).then_inc(s["g_hs"], 1)
            pool.wait_ge(s["g_hs"], 2)
            pool.sem_inc(s["g_res"], 1)
            pool.wait_ge(s["x3_out"], 16)
            with pool.Fori(0, LAST) as i:
                chain.enter(i, B)
                for b in range(B):
                    pool.wait_ge(s["v_norm"], i * B + b + 2)
                    pool.sem_inc(g.carrier["g_carrier"], 1)
                    chain.step(pool.tensor_tensor(xn[:, b % 2, :, :], xn[:, b % 2, :, :],
                                                  bcast(g.mlp_g[:, i, :], 1, [P, RT, D]), ALU.mult))
                    chain.settle()
                    pool.wait_ge(s["p_T"], i * TU + (2, 4, 6, 8)[b])
                    pool.sem_inc(g.carrier["g_carrier"], 1)
                    pool.tensor_tensor(hs[:, b % 2, :, :], xn[:, b % 2, :, :],
                                       bcast(g.mlp_b[:, i, :], 1, [P, RT, D]), ALU.add).then_inc(s["g_hs"], 1)
                    pool.wait_ge(s["g_hs"], i * B + b + 3)
                    pool.sem_inc(g.carrier["g_carrier"], 1)
                    pool.tensor_tensor(g.x_a[:, b * RT:(b + 1) * RT, :], hs[:, b % 2, :, :],
                                       bcast(g.mlp_b2[:, i + 1, :], 1, [P, RT, D]), ALU.add
                                       ).then_inc(s["g_res"], 1)

        @block.tensor
        def _(pe):
            def transposes(i, place):
                b = PLACES[place]
                pe.wait_ge(s["g_hs"], i * B + place + 2)
                for c in range(KC):
                    pe.wait_ge(s["v_T"], i * TU + 2 * place + c + 7)
                    for t in range(RT):
                        mm = pe.transpose(ps[:, 6 + c, t * P:(t + 1) * P], hs[:, b % 2, t, c * P:(c + 1) * P],
                                          ident[:, :])
                    mm.then_inc(s["p_T"], 1)

            def hidden(i, b, f):
                n = b * FC + f
                pe.wait_ge(s["a_g"], i * B * FC + n + 1)
                k = 0
                for c in range(KC):
                    for w, x in ((w1_h, g.xT_h), (w1_h, g.xT_l), (w1_l, g.xT_h)):
                        mm = pe.matmul(ps[:, n % 4, :], w[:, c, f * P:(f + 1) * P], x[:, b, c, :],
                                       start=(k == 0), stop=(k == 5))
                        k += 1
                mm.then_inc(s["p_hid"], 1)

            def output(i, b):
                pe.wait_ge(s["v_gl"], i * B * FC + b * FC + 12)
                pe.wait_ge(s["v_sum"], i * B + b + 1)
                for t in range(RT):
                    k = 0
                    for f in range(FC):
                        for x, w in ((G_h, w2_h), (G_h, w2_l), (G_l, w2_h)):
                            mm = pe.matmul(ps[:, 4 + t // 2, (t % 2) * D:(t % 2 + 1) * D],
                                           x[:, b % 2, f, t * P:(t + 1) * P], w[:, f, :],
                                           start=(k == 0), stop=(k == 3 * FC - 1))
                            k += 1
                mm.then_inc(s["p_out"], 1)

            def turn(i, last):
                pe.wait_ge(s["v_w"], i * WP + 4)
                pe.wait_ge(s["v_T"], i * TU + 4)
                for f in range(FC):
                    hidden(i, 0, f)
                transposes(i, 0)
                pe.wait_ge(s["v_T"], i * TU + 6)
                for f in range(FC):
                    hidden(i, 1, f)
                pe.wait_ge(s["v_w"], i * WP + 8)
                output(i, 0)
                pe.wait_ge(s["v_T"], i * TU + 8)
                for f in range(FC):
                    hidden(i, 2, f)
                output(i, 1)
                if not last:
                    transposes(i, 1)
                pe.wait_ge(s["v_T"], i * TU + 10)
                for f in range(FC):
                    hidden(i, 3, f)
                output(i, 2)
                if not last:
                    transposes(i, 2)
                output(i, 3)
                if not last:
                    transposes(i, 3)

            with pe.Fori(0, LAST) as i:
                turn(i, False)
            turn(LAST, True)

        @block.scalar
        def _(act):
            def weight_high(i, w):
                if w == 0:
                    act.wait_ge(w2_in, (i + 2) * 16)
                    act.wait_ge(s["p_out"], i * B + 2)
                elif w == 4:
                    act.wait_ge(w1_in, (i + 3) * 16)
                    act.wait_ge(s["p_hid"], (i + 1) * B * FC)
                act.activation(weight_piece(w, w1_h, w2_h), weight_piece(w, g.w1_raw, g.w2_raw), ACT.Copy).then_inc(s["a_w"], 1)

            def high(i, place):
                b = PLACES[place]
                for c in range(KC):
                    act.wait_ge(s["p_T"], i * TU + 2 * place + c + 3)
                    act.activation(g.xT_h[:, b, c, :], ps[:, 6 + c, :], ACT.Copy).then_inc(s["a_T"], 1)

            def gelu(i, b, f):
                n = b * FC + f
                bias = g.bias_col[:, bass.ds(4 + 2 * MC0 + i * FC + f, 1)]
                act.wait_ge(s["p_hid"], i * B * FC + n + 1)
                act.wait_ge(s["v_gl"], i * B * FC + n + 1)
                if f == 0:
                    act.wait_ge(s["p_out"], i * B + b + 1)
                act.sem_inc(g.carrier["a_carrier"], 1)
                act.activation(G32[:, n % 4, :], ps[:, n % 4, :], ACT.Gelu, bias=bias)
                act.activation(G_h[:, b % 2, f, :], ps[:, n % 4, :], ACT.Gelu, bias=bias).then_inc(s["a_g"], 1)

            def turn(i, last):
                for f in range(FC):
                    gelu(i, 0, f)
                    if f % 2:
                        weight_high(i, f // 2)
                high(i, 0)
                for b in (1, 2):
                    for f in range(FC):
                        gelu(i, b, f)
                if not last:
                    high(i, 1)
                for f in range(FC):
                    gelu(i, 3, f)
                if not last:
                    for w in range(4, 8):
                        weight_high(i, w)
                    high(i, 2)
                    high(i, 3)

            with act.Fori(0, LAST) as i:
                turn(i, False)
            turn(LAST, True)

        @block.vector
        def _(v):
            chain = Chain(v, s["v_chain"])
            v.sem_inc(s["v_T"], 8)
            v.sem_inc(s["v_w"], 4)
            v.sem_inc(s["p_T"], 2)
            v.sem_inc(s["a_g"], 4)
            v.sem_inc(s["v_gl"], 4)
            v.sem_inc(s["p_out"], 2)
            v.sem_inc(s["v_sum"], 1)
            v.sem_inc(s["v_norm"], 1)

            def weight_low(i, w):
                v.wait_ge(s["a_w"], i * WP + w + 1)
                v.tensor_tensor(weight_piece(w, w1_l, w2_l), weight_piece(w, g.w1_raw, g.w2_raw),
                                weight_piece(w, w1_h, w2_h).bitcast(F32), ALU.subtract).then_inc(s["v_w"], 1)

            def low(i, place):
                b = PLACES[place]
                for c in range(KC):
                    v.wait_ge(s["a_T"], i * TU + 2 * place + c + 1)
                    v.tensor_tensor(g.xT_l[:, b, c, :], ps[:, 6 + c, :], g.xT_h[:, b, c, :].bitcast(F32),
                                    ALU.subtract).then_inc(s["v_T"], 1)

            def gelu_low(i, b, f):
                n = b * FC + f
                v.wait_ge(s["a_g"], i * B * FC + n + 5)
                v.tensor_tensor(G_l[:, b % 2, f, :], G32[:, n % 4, :], G_h[:, b % 2, f, :].bitcast(F32),
                                ALU.subtract).then_inc(s["v_gl"], 1)

            def residual(i, b):
                v.wait_ge(s["p_out"], i * B + b + 3)
                v.wait_ge(s["g_res"], i * B + b + 1)
                v.wait_ge(s["v_norm"], i * B + b + 1)
                v.tensor_tensor(g.rsum[:, :, :], ps[:, 4:6, :].rearrange("p a (b c) -> p (a b) c", c=D),
                                g.x_a[:, b * RT:(b + 1) * RT, :], ALU.add).then_inc(s["v_sum"], 1)

            def norm(i, b, last):
                v.wait_ge(s["v_sum"], i * B + b + 2)
                if last:
                    v.wait_ge(s[f"x3_in{b // 2}"], 16)
                    kept = (g.w1_raw[:, :, :].rearrange("p a (b d) -> p (a b) d", d=D) if b < 2 else
                            g.w2_raw[:, :, :])
                    chain.step(v.tensor_tensor(g.rsum[:, :, :], g.rsum[:, :, :],
                                               kept[:, b % 2 * RT:(b % 2 + 1) * RT, :], ALU.add))
                    chain.settle()
                if last and b >= 2:
                    v.wait_ge(s[f"y_out{b % 2}"], 16)
                else:
                    v.wait_ge(s["g_hs"], i * B + b + 1)
                layernorm(v, chain, g.lnw, g.rsum, xn[:, b % 2, :, :], s["v_norm"])

            def turn(i, last):
                for f in range(FC):
                    gelu_low(i, 0, f)
                    if f % 2:
                        weight_low(i, f // 2)
                low(i, 0)
                for f in range(FC):
                    gelu_low(i, 1, f)
                residual(i, 0)
                norm(i, 0, last)
                for f in range(FC):
                    gelu_low(i, 2, f)
                residual(i, 1)
                if not last:
                    low(i, 1)
                norm(i, 1, last)
                for f in range(FC):
                    gelu_low(i, 3, f)
                if not last:
                    for w in range(4, 8):
                        weight_low(i, w)
                residual(i, 2)
                if not last:
                    low(i, 2)
                norm(i, 2, last)
                residual(i, 3)
                if not last:
                    low(i, 3)
                norm(i, 3, last)

            layernorm(v, chain, g.lnw, g.rsum, hs[:, (B - 1) % 2, :, :], s["v_x3"])
            v.wait_ge(s["v_x3"], 1)
            with v.Fori(0, LAST) as i:
                chain.enter(i, 14 * B)
                turn(i, False)
            chain.leave(LAST)
            turn(LAST, True)


TRANSPOSED = ("L0_ffn_ent_w", "L1_attn_Wq", "L1_attn_Wk", "L1_attn_Wv", "L1_attn_Wo", "L1_ffn_W1", "L1_ffn_W2")
UNUSED = ("L1_attn_cos", "L1_attn_sin")


def laid_out(inputs):
    arrays = {}
    for name, value in inputs.items():
        if name in TRANSPOSED:
            arrays[name + "_T"] = np.ascontiguousarray(np.swapaxes(np.asarray(value), -1, -2))
        elif name not in UNUSED:
            arrays[name] = np.ascontiguousarray(value)
    return {**arrays, **shape_constants()}


def shape_constants():
    q = np.arange(P)
    kmask = np.where(q[:, None] > q[None, :], np.float32(MASKED), np.float32(0))
    qmask = np.zeros((P, S), np.float32)
    qmask[:, S - P:] = kmask.T
    inv_freq = (np.float32(1.0) / np.float32(10000.0) ** (np.arange(0, 4, 2, dtype=np.float32) / np.float32(4)))
    angle = np.arange(S, dtype=np.float32)[:, None] * inv_freq[None, :].astype(np.float32)
    angle = np.concatenate([angle, angle], axis=1)
    sign = np.array([-1, -1, 1, 1], np.float32)
    rope = np.stack([np.cos(angle), np.sin(angle) * sign]).astype(np.float32)
    rope = rope.reshape(2, RT, P, 4).transpose(2, 0, 1, 3)
    heads = (q[:, None] // DH == q[None, :] // DH).astype(np.float32)
    column = (q[:, None] // DH == np.arange(P // DH)[None, :]).astype(np.float32)
    return {"c_ident": np.eye(P, dtype=np.float32), "c_kmask": kmask, "c_qmask": qmask,
            "c_rope": np.ascontiguousarray(rope), "c_blocks": np.concatenate([heads, column], axis=1)}


def kernel(**inputs):
    import concourse.bacc as bacc
    from concourse.bass_utils import run_bass_kernel_spmd

    nc = bacc.Bacc("TRN2", target_bir_lowering=False, num_devices=1)
    arrays = laid_out(inputs)
    A = {name: nc.dram_tensor(name, a.shape, mybir.dt.from_np(a.dtype), kind="ExternalInput").ap()
         for name, a in arrays.items()}
    out = nc.dram_tensor("out", (B, S, D), F32, kind="ExternalOutput").ap()
    build(nc, A, out)
    result = run_bass_kernel_spmd(nc, [arrays], core_ids=[0])
    return result.results[0]["out"]
```
